# Optimizing a Trainium2 kernel written in Bass

```python
import numpy as np
import jax
import jax.numpy as jnp

def _softmax(x, axis=-1):
    return jax.nn.softmax(x, axis=axis)

def _gelu(x):
    return jax.nn.gelu(x, approximate=True)

def _silu(x):
    return jax.nn.silu(x)

def _sigmoid(x):
    return jax.nn.sigmoid(x)

def _layernorm(x, axis=-1, eps=1e-05):
    m = jnp.mean(x, axis=axis, keepdims=True)
    v = jnp.var(x, axis=axis, keepdims=True)
    return (x - m) / jnp.sqrt(v + eps)

def _scatter_add(tgt, idx, src, axis=0):
    return tgt.at[idx].add(src)

def _segment_sum(src, seg, n):
    return jax.ops.segment_sum(src, seg, n)
kernel_name = 'mk_gnn_resnorm_d4_gnn_r32_be802b'

def setup_inputs(seed: int=0):
    np.random.seed(seed)
    _w = jnp.asarray

    def _rec_inputs():
        import jax
        import jax.numpy as jnp
        _gk = jax.random.key(seed)
        x = -0.0003713 + 1 * jax.random.normal(jax.random.fold_in(_gk, 1), (50000, 256), jnp.float32)
        src = jax.random.randint(jax.random.fold_in(_gk, 2), (50000,), 0, 50000, jnp.int32)
        dst = jnp.minimum((50000 * jax.random.uniform(jax.random.fold_in(_gk, 3), (50000,)) ** 2.0).astype(jnp.int32), 49999)
        _o = jnp.argsort(dst, stable=True)
        src = src[_o]
        dst = dst[_o]
        edge_weight = jax.random.uniform(jax.random.fold_in(_gk, 13), (50000,), jnp.float32, 0.0, 0.999998)
        return (x, src, dst, edge_weight)
    x, src, dst, edge_weight = _rec_inputs()

    def _L0_gnn_setup():
        import jax, jax.numpy as jnp
        import numpy as np
        N = 50000
        D = 256
        E = 25000
        key = jax.random.key(seed)
        ks = jax.random.split(key, 9)
        X = jax.random.normal(ks[0], (N, D), dtype=jnp.float32)
        edge_index = jax.random.randint(ks[1], (2, E), 0, N, dtype=jnp.int32)
        edge_weight = jax.random.uniform(ks[2], (E,), dtype=jnp.float32)
        p = jax.random.normal(ks[3], (D,), dtype=jnp.float32)
        s = 1.0 / np.sqrt(D)
        W_ih = jax.random.normal(ks[4], (3 * D, D), dtype=jnp.float32) * s
        W_hh = jax.random.normal(ks[5], (3 * D, D), dtype=jnp.float32) * s
        b_ih = jax.random.normal(ks[6], (3 * D,), dtype=jnp.float32) * s
        b_hh = jax.random.normal(ks[7], (3 * D,), dtype=jnp.float32) * s
        W0 = jax.random.normal(ks[8], (D, D), dtype=jnp.float32) * s
        return {'X': X, 'edge_index': edge_index, 'edge_weight': edge_weight, 'p': p, 'W_ih': W_ih, 'W_hh': W_hh, 'b_ih': b_ih, 'b_hh': b_hh, 'W0': W0}
    _L0_gnn_all = _L0_gnn_setup()
    _L0_gnn_in = {k: v for k, v in _L0_gnn_all.items() if k in ('p', 'W_ih', 'W_hh', 'b_ih', 'b_hh', 'W0')}
    del _L0_gnn_all

    def _L1_gnn_setup():
        import jax, jax.numpy as jnp
        import numpy as np
        N_NODES = 50000
        N_EDGES = 25000
        D = 256
        L = 3
        key = jax.random.key(seed)
        k1, k2, k3, k4, k5 = jax.random.split(key, 5)
        features = jax.random.normal(k1, (N_NODES, D), dtype=jnp.float32)
        scale = 1.0 / np.sqrt(D)
        W_self = jax.random.normal(k2, (L, D, D), dtype=jnp.float32) * scale
        W_neigh = jax.random.normal(k3, (L, D, D), dtype=jnp.float32) * scale
        bias = jnp.zeros((L, D), dtype=jnp.float32)
        src = jax.random.randint(k4, (N_EDGES,), 0, N_NODES, dtype=jnp.int32)
        dst = jax.random.randint(k5, (N_EDGES,), 0, N_NODES, dtype=jnp.int32)
        return {'features': features, 'W_self': W_self, 'W_neigh': W_neigh, 'bias': bias, 'src': src, 'dst': dst}
    _L1_gnn_all = _L1_gnn_setup()
    _L1_gnn_in = {k: v for k, v in _L1_gnn_all.items() if k in ('W_self', 'W_neigh', 'bias')}
    del _L1_gnn_all

    def _L2_gnn_setup():
        import jax, jax.numpy as jnp
        import numpy as np
        N_NODES = 25000
        N_EDGES = 12500
        D = 256
        key = jax.random.key(seed)
        k1, k2, k3, k4, k5 = jax.random.split(key, 5)
        feat = jax.random.normal(k1, (N_NODES, D), dtype=jnp.float32)
        src = jax.random.randint(k2, (N_EDGES,), 0, N_NODES, dtype=jnp.int32)
        dst = jax.random.randint(k3, (N_EDGES,), 0, N_NODES, dtype=jnp.int32)
        a = float(np.sqrt(6.0 / (D + D)))
        W1 = jax.random.uniform(k4, (D, D), minval=-a, maxval=a, dtype=jnp.float32)
        W2 = jax.random.uniform(k5, (D, D), minval=-a, maxval=a, dtype=jnp.float32)
        b = jnp.zeros((D,), dtype=jnp.float32)
        return {'feat': feat, 'W1': W1, 'W2': W2, 'b': b, 'src': src, 'dst': dst}
    _L2_gnn_all = _L2_gnn_setup()
    _L2_gnn_in = {k: v for k, v in _L2_gnn_all.items() if k in ('W1', 'W2', 'b')}
    del _L2_gnn_all

    def _L3_gnn_setup():
        import jax, jax.numpy as jnp
        import numpy as np
        N_NODES = 50000
        N_EDGES = 25000
        F_IN = 256
        F_OUT = 256
        key = jax.random.key(seed)
        k_x, k_w, k_r, k_c, k_v = jax.random.split(key, 5)
        limit = np.sqrt(6.0 / (F_IN + F_OUT)).astype(np.float32)
        x = jax.random.normal(k_x, (N_NODES, F_IN), dtype=jnp.float32)
        weight = jax.random.uniform(k_w, (F_IN, F_OUT), dtype=jnp.float32, minval=-limit, maxval=limit)
        bias = jnp.zeros((F_OUT,), dtype=jnp.float32)
        rows = jax.random.randint(k_r, (N_EDGES,), 0, N_NODES, dtype=jnp.int64 if jax.config.jax_enable_x64 else jnp.int32)
        cols = jax.random.randint(k_c, (N_EDGES,), 0, N_NODES, dtype=jnp.int64 if jax.config.jax_enable_x64 else jnp.int32)
        vals = jax.random.uniform(k_v, (N_EDGES,), dtype=jnp.float32)
        return {'x': x, 'weight': weight, 'bias': bias, 'rows': rows, 'cols': cols, 'vals': vals}
    _L3_gnn_all = _L3_gnn_setup()
    _L3_gnn_in = {k: v for k, v in _L3_gnn_all.items() if k in ('weight', 'bias')}
    del _L3_gnn_all
    return {'x': x, 'src': src, 'dst': dst, 'edge_weight': edge_weight, 'L0_gnn_p': _L0_gnn_in['p'], 'L0_gnn_W_ih': _L0_gnn_in['W_ih'], 'L0_gnn_W_hh': _L0_gnn_in['W_hh'], 'L0_gnn_b_ih': _L0_gnn_in['b_ih'], 'L0_gnn_b_hh': _L0_gnn_in['b_hh'], 'L0_gnn_W0': _L0_gnn_in['W0'], 'L1_gnn_W_self': _L1_gnn_in['W_self'], 'L1_gnn_W_neigh': _L1_gnn_in['W_neigh'], 'L1_gnn_bias': _L1_gnn_in['bias'], 'L2_gnn_W1': _L2_gnn_in['W1'], 'L2_gnn_W2': _L2_gnn_in['W2'], 'L2_gnn_b': _L2_gnn_in['b'], 'L3_gnn_weight': _L3_gnn_in['weight'], 'L3_gnn_bias': _L3_gnn_in['bias']}

def reference(x, src, dst, edge_weight, L0_gnn_p, L0_gnn_W_ih, L0_gnn_W_hh, L0_gnn_b_ih, L0_gnn_b_hh, L0_gnn_W0, L1_gnn_W_self, L1_gnn_W_neigh, L1_gnn_bias, L2_gnn_W1, L2_gnn_W2, L2_gnn_b, L3_gnn_weight, L3_gnn_bias):
    import jax
    import jax.numpy as jnp

    def _L0_gnn_ref(X, edge_index, edge_weight, p, W_ih, W_hh, b_ih, b_hh, W0):
        import jax, jax.numpy as jnp
        import numpy as np
        N = 50000
        D = 256
        E = 25000
        n, d = X.shape
        k = d
        score = X @ p / jnp.linalg.norm(p)
        top_score, idx = jax.lax.top_k(score, k)
        x_tilde = X[idx] * jnp.tanh(top_score)[:, None]
        h = W0
        gi = x_tilde @ W_ih.T + b_ih
        gh = h @ W_hh.T + b_hh
        i_r, i_z, i_n = jnp.split(gi, 3, axis=1)
        h_r, h_z, h_n = jnp.split(gh, 3, axis=1)
        r = jax.nn.sigmoid(i_r + h_r)
        z = jax.nn.sigmoid(i_z + h_z)
        nn_ = jnp.tanh(i_n + r * h_n)
        W_new = (1.0 - z) * nn_ + z * h
        xw = X @ W_new
        src, dst = (edge_index[0], edge_index[1])
        loop = jnp.arange(n, dtype=src.dtype)
        src_f = jnp.concatenate([src, loop])
        dst_f = jnp.concatenate([dst, loop])
        ew_f = jnp.concatenate([edge_weight, jnp.ones((n,), dtype=X.dtype)])
        deg = jax.ops.segment_sum(ew_f, dst_f, num_segments=n)
        dinv = jnp.where(deg > 0, jax.lax.rsqrt(deg), 0.0)
        norm = dinv[src_f] * ew_f * dinv[dst_f]
        msgs = norm[:, None] * xw[src_f]
        out = jax.ops.segment_sum(msgs, dst_f, num_segments=n)
        return out

    def _L1_gnn_ref(features, W_self, W_neigh, bias, src, dst):
        import jax, jax.numpy as jnp
        import numpy as np
        N_NODES = 50000
        N_EDGES = 25000
        D = 256
        L = 3
        "3-layer GraphSAGE encoder (DGL SAGEConv, mean aggregator), eval mode.\n\n            Per layer: h_neigh = mean over in-neighbors of h (messages src -> dst);\n                       out = h @ W_self + h_neigh @ W_neigh + bias; relu except last.\n            feat_drop / wrapper dropout are identity in eval mode. The wrapper's relu\n            after layers 0,1 is idempotent with SAGEConv's internal relu.\n            "
        n = features.shape[0]
        ones = jnp.ones(src.shape[0], dtype=features.dtype)
        deg = jax.ops.segment_sum(ones, dst, num_segments=n)
        inv_deg = jnp.where(deg > 0, 1.0 / jnp.maximum(deg, 1.0), 0.0)[:, None]
        h = features
        for l in range(L):
            agg = jax.ops.segment_sum(h[src], dst, num_segments=n) * inv_deg
            h = h @ W_self[l] + agg @ W_neigh[l] + bias[l]
            if l < L - 1:
                h = jax.nn.relu(h)
        return h

    def _L2_gnn_ref(feat, W1, W2, b, src, dst):
        import jax, jax.numpy as jnp
        import numpy as np
        N_NODES = 25000
        N_EDGES = 12500
        D = 256
        n = feat.shape[0]
        ones = jnp.ones(src.shape[0], dtype=feat.dtype)
        out_deg = jnp.maximum(jax.ops.segment_sum(ones, src, num_segments=n), 1.0)
        in_cnt = jax.ops.segment_sum(ones, dst, num_segments=n)
        t1 = feat @ W1
        msg = t1[src] + feat[src] * feat[dst] @ W2
        scale = jnp.sqrt(out_deg[src]) * jnp.sqrt(out_deg[dst])
        msg = msg / scale[:, None]
        agg = jax.ops.segment_sum(msg, dst, num_segments=n)
        embed = jnp.where(in_cnt[:, None] > 0, t1 + agg, jnp.zeros_like(t1))
        embed = embed + b
        embed = jax.nn.leaky_relu(embed, negative_slope=0.01)
        norm = jnp.linalg.norm(embed, axis=1, keepdims=True)
        embed = embed / jnp.maximum(norm, 1e-12)
        return embed

    def _L3_gnn_ref(x, weight, bias, rows, cols, vals):
        import jax, jax.numpy as jnp
        import numpy as np
        N_NODES = 50000
        N_EDGES = 25000
        F_IN = 256
        F_OUT = 256
        support = jnp.matmul(x, weight)
        msgs = vals[:, None] * support[cols]
        out = jax.ops.segment_sum(msgs, rows, num_segments=x.shape[0])
        return out + bias
    edge_index = jnp.stack([src, dst])
    x = _layernorm(x + _L0_gnn_ref(x, edge_index, edge_weight, L0_gnn_p, L0_gnn_W_ih, L0_gnn_W_hh, L0_gnn_b_ih, L0_gnn_b_hh, L0_gnn_W0), axis=-1)
    x = _layernorm(x + _L1_gnn_ref(x, L1_gnn_W_self, L1_gnn_W_neigh, L1_gnn_bias, src, dst), axis=-1)
    x = _layernorm(x + _L2_gnn_ref(x, L2_gnn_W1, L2_gnn_W2, L2_gnn_b, src, dst), axis=-1)
    x = _layernorm(x + _L3_gnn_ref(x, L3_gnn_weight, L3_gnn_bias, src, dst, edge_weight), axis=-1)
    return x

_drawn_inputs = setup_inputs


def setup_inputs(seed=0):
    import zlib

    import numpy as np

    out = dict(_drawn_inputs(seed))
    spreads = {'L1_gnn_bias': (0.0, 0.1), 'L2_gnn_b': (0.0, 0.1), 'L3_gnn_bias': (0.0, 0.1)}
    factors = {}
    for name, (base, spread) in spreads.items():
        noise = np.random.default_rng([zlib.crc32(name.encode()), seed]).standard_normal(out[name].shape)
        drawn = base * np.exp(spread * noise) if base else spread * noise
        out[name] = jnp.asarray(drawn.astype(out[name].dtype))
    for name, factor in factors.items():
        out[name] = (out[name] * factor).astype(out[name].dtype)
    return out
```

```python
from contextlib import ExitStack, contextmanager

import concourse.bass as bass
from concourse import mybir

F32 = mybir.dt.float32
BF16 = mybir.dt.bfloat16
FP16 = mybir.dt.float16
I32 = mybir.dt.int32
ALU = mybir.AluOpType
ACT = mybir.ActivationFunctionType
AX = mybir.AxisListType

P = 128
D = 256
DB = D // P
K = D
U = 8
XU = 8
EPS = 1e-5


class Plan:

    def __init__(self, sb, dram, sem, name, T, TW, rows):
        self.name = name
        self.overflow = sb(f"{name}_overflow", [P, TW])
        self.upto = sb(f"{name}_upto", [P, TW])
        self.first = sb(f"{name}_first", [P, TW])
        self.base = sb(f"{name}_base", [P, TW])
        self.sums_at = sb(f"{name}_sums_at", [P, T], I32)
        self.x_last = sb(f"{name}_x_last", [P, 1], I32)
        self.carry = sb(f"{name}_carry", [P, TW])
        self.main, self.extra = [(sb(f"{name}_{h}_from", [P, TW], I32),
                                  sb(f"{name}_{h}_to", [P, TW]),
                                  sb(f"{name}_{h}_weight", [P, TW]))
                                 for h in ("main", "extra")]
        self.tables = [dram(f"{name}_table{k}", [rows, 4]) for k in range(U)]
        self.gathered = [sem(f"{name}_gathered{k}") for k in range(U)]
        self.sweeps = 0


@contextmanager
def phase(nc, *names):
    with ExitStack() as held:
        sems = [held.enter_context(nc.semaphore(n)) for n in names]
        with nc.Block() as block:
            yield block, sems
        nums = [s.num for s in sems]
        assert set(range(min(nums), max(nums) + 1)) <= set(nums) | set(nc.free_semaphores)
        nc.all_engine_barrier(sems_to_clear=range(min(nums), max(nums) + 1))


def need(eng, sem, value):
    if not isinstance(value, int) or value > 0:
        eng.wait_ge(sem, value)


def slot_freed(eng, sem, i, base):
    if not (isinstance(i, int) and i == 0):
        eng.wait_ge(sem, 16 * (i + base))


def tile_at(i, k):
    return i + k // U, k % U


def sweep(eng, tiles, lead, step, lag, peeled=1):
    n = tiles // U
    for k in range(-lead, U * peeled):
        step(*((0, k) if k < 0 else divmod(k, U)))
    if n > peeled + 1:
        with eng.Fori(peeled, n - 1) as i:
            for k in range(U):
                step(i, k)
    for k in range(U + lag):
        step(n - 1, k)


def graph_stack(nc, x, src, dst, edge_weight, p, W_ih, W_hh, b_ih, b_hh, W0, W_self, W_neigh, b_sage,
                W_one, W_two, b_pair, W_conv, b_conv, out):
    N, E = x.shape[0], src.shape[0]
    assert x.shape[1] == D
    T = -(-max(N, E) // (P * U)) * U
    C = T
    REAL = N // P
    REST = N - REAL * P
    assert T // U >= 2 and T == REAL + 2 and REAL % 2 == 0 and REST
    XB = -(-(E // P + 1) // XU) * XU + 2 * XU
    TB = -(-max(T, XB, K) // P)
    TW = TB * P
    SLOTS = 2 * TW + 2
    TRASH = SLOTS * P
    ROW = D + 1

    ctx = ExitStack()
    with ctx:
        def sb(name, shape, dt=F32):
            return ctx.enter_context(nc.sbuf_tensor(name, shape, dt))

        def dram(name, shape, dt=F32):
            return nc.dram_tensor(name, shape, dt, kind="Internal").ap()

        table0 = dram("table0", [T * P, ROW])
        table1 = dram("table1", [T * P, D])
        table1a = dram("table1a", [T * P, D])
        table1b = dram("table1b", [T * P, D])
        table2 = dram("table2", [T * P, ROW])
        table3 = dram("table3", [T * P, D])
        overflow_sums = dram("overflow_sums", [XB + 1, P, D])

        gathered_m = [ctx.enter_context(nc.semaphore(f"gathered{k}")) for k in range(U)]
        before_now = [0] * U

        psA = ctx.enter_context(nc.psum_tensor("psA", [P, 2, 512], F32))
        psT = ctx.enter_context(nc.psum_tensor("psT", [P, 2, 512], F32))
        psO = ctx.enter_context(nc.psum_tensor("psO", [P, 2, 512], F32))
        psM = ctx.enter_context(nc.psum_tensor("psM", [P, 2, 512], F32))

        iota_i = sb("iota_i", [P, TW], I32)
        pcol_i = sb("pcol_i", [P, 1], I32)
        iota_f = sb("iota_f", [P, TW])
        iota_h = sb("iota_h", [P, TW], FP16)
        pcol = sb("pcol", [P, 1])
        ident = sb("ident", [P, P])
        ones_f = sb("ones_f", [P, P])
        ones_row = sb("ones_row", [P, TW])
        eps_col = sb("eps_col", [P, 1])
        tiny_col = sb("tiny_col", [P, 1])
        ones_b = sb("ones_b", [P, P], BF16)
        before = sb("before", [P, P], BF16)
        not_before = sb("not_before", [P, P], BF16)
        zeros = sb("zeros", [P, D])
        p_row = sb("p_row", [P, D])
        bsage_row = sb("bsage_row", [P, 3, D])
        bpair_row = sb("bpair_row", [P, D])
        bconv_row = sb("bconv_row", [P, D])
        dinv = sb("dinv", [P, T])
        inv_deg = sb("inv_deg", [P, T])
        has_in = sb("has_in", [P, T])
        root_out = sb("root_out", [P, T])
        score = sb("score", [P, T])
        def sem(name):
            return ctx.enter_context(nc.semaphore(name))

        by_dst, by_src = [Plan(sb, dram, sem, name, T, TW, TRASH + P) for name in ("by_dst", "by_src")]
        w_gcn = sb("w_gcn", [P, 2, D])

        pool_waits = sb("pool_waits", [P, 5])

        def take_waits(pool, at=0):
            pool.tensor_tensor(pool_waits[0:1, at:at + 1], pool_waits[0:1, 1:2], pool_waits[0:1, 2:3], ALU.add)

        early = ExitStack()

        def tmp(name, shape, dt=F32):
            return early.enter_context(nc.sbuf_tensor(name, shape, dt))

        src_i = tmp("src_i", [P, C], I32)
        dst_i = tmp("dst_i", [P, C], I32)
        w_f = tmp("w_f", [P, C])
        fields = {plan: tmp(f"{plan.name}_fields", [P, C, 4]) for plan in (by_dst, by_src)}
        dst_hi = tmp("dst_hi", [P, C])
        dst_lo = tmp("dst_lo", [P, C])
        src_hi = tmp("src_hi", [P, C])
        src_lo = tmp("src_lo", [P, C])
        w_part = tmp("w_part", [P, 3, C])
        w_half = tmp("w_half", [P, C], BF16)
        w_rest = tmp("w_rest", [P, C])
        pad_at = tmp("pad_at", [P, C])
        cut_i = tmp("cut_i", [P, C], I32)
        table_fill = tmp("table_fill", [P, 2 * P, 4])

        full, rest = E // C, E % C
        with phase(nc, "pads_set", "iotas_made", "edges_in", "rows_in", "fill_set", "fill_out", "dve_done") as (
                block, (pads_set, iotas_made, edges_in, rows_in, fill_set, fill_out, dve_done)):
            @block.gpsimd
            def _(pool):
                pool.iota(iota_i[:], [[1, TW]], base=0, channel_multiplier=0)
                pool.iota(pcol_i[:], [[0, 1]], base=0, channel_multiplier=1).then_inc(iotas_made, 1)

            @block.sync
            def _(sp):
                sp.wait_ge(pads_set, 1)
                for to, what in ((src_i, src), (dst_i, dst), (w_f, edge_weight)):
                    sp.dma_start(to[0:full, :], what[0:full * C].rearrange("(a c) -> a c", c=C)).then_inc(edges_in, 16)
                    if rest:
                        sp.dma_start(to[full:full + 1, 0:rest],
                                     what[full * C:E].rearrange("(a c) -> a c", a=1)).then_inc(edges_in, 16)
                for to, what in ((p_row[:], p), (bpair_row[:], b_pair), (bconv_row[:], b_conv),
                                 (bsage_row[:, 0], b_sage[0]), (bsage_row[:, 1], b_sage[1]),
                                 (bsage_row[:, 2], b_sage[2])):
                    sp.dma_start(to, what.rearrange("(a d) -> a d", a=1).to_broadcast([P, D])).then_inc(rows_in, 16)
                sp.wait_ge(fill_set, 1)
                rows = (TRASH + P) // P
                n = 0
                for edge_table in by_dst.tables + by_src.tables:
                    fills = edge_table.rearrange("(a r) f -> a r f", a=P)
                    for r in range(0, rows, 2 * P):
                        m = min(2 * P, rows - r)
                        sp.dma_start(fills[:, r:r + m, :], table_fill[:, 0:m, :]).then_inc(fill_out, 16)
                        n += 16
                sp.dma_start(overflow_sums[XB], zeros[:]).then_inc(fill_out, 16)
                sp.wait_ge(fill_out, n + 16)
                sp.wait_ge(rows_in, 16 * 6)

            @block.vector
            def _(dve):
                steps = [0]

                def link(ins):
                    steps[0] += 1
                    ins.then_inc(dve_done, 1)
                    dve.wait_ge(dve_done, steps[0])

                dve.memset(pool_waits[:], 0.0)
                dve.memset(src_i[:], -1)
                dve.memset(dst_i[:], -1)
                dve.memset(w_f[:], 0.0).then_inc(pads_set, 1)
                dve.memset(zeros[:], 0.0)
                dve.memset(table_fill[:], 0.0).then_inc(fill_set, 1)
                dve.memset(ones_f[:], 1.0)
                dve.memset(ones_row[:], 1.0)
                dve.memset(eps_col[:], EPS)
                dve.memset(tiny_col[:], 1e-34)
                dve.memset(ones_b[:], 1.0)
                for f in fields.values():
                    dve.memset(f[:], 0.0)
                dve.wait_ge(iotas_made, 1)
                dve.tensor_copy(iota_f[:], iota_i[:])
                dve.tensor_copy(iota_h[:], iota_i[:])
                link(dve.tensor_copy(pcol[:], pcol_i[:]))
                dve.tensor_scalar(ident[:], iota_f[:, 0:P], pcol[:, 0:1], None, ALU.is_equal)
                dve.tensor_scalar(before[:], iota_f[:, 0:P], pcol[:, 0:1], None, ALU.is_gt)
                dve.tensor_scalar(not_before[:], iota_f[:, 0:P], pcol[:, 0:1], None, ALU.is_le)
                dve.wait_ge(edges_in, 16 * 3 * (1 + (rest > 0)))
                for to_hi, to_lo, what in ((dst_hi, dst_lo, dst_i), (src_hi, src_lo, src_i)):
                    link(dve.tensor_scalar(cut_i[:], what[:], 7, None, ALU.arith_shift_right))
                    link(dve.tensor_copy(to_hi[:], cut_i[:]))
                    link(dve.tensor_scalar(cut_i[:], what[:], P - 1, None, ALU.bitwise_and))
                    link(dve.tensor_copy(to_lo[:], cut_i[:]))
                for plan, taken, lo in ((by_dst, src_i, dst_lo), (by_src, dst_i, src_lo)):
                    dve.tensor_copy(fields[plan][:, :, 0], taken[:])
                    dve.tensor_scalar(fields[plan][:, :, 1], lo[:], 1.0, None, ALU.add)
                    dve.tensor_copy(fields[plan][:, :, 2], w_f[:])
                link(dve.tensor_copy(w_half[:], w_f[:]))
                link(dve.tensor_copy(w_part[:, 0], w_half[:]))
                link(dve.tensor_tensor(w_rest[:], w_f[:], w_part[:, 0], ALU.subtract))
                link(dve.tensor_copy(w_half[:], w_rest[:]))
                link(dve.tensor_copy(w_part[:, 1], w_half[:]))
                link(dve.tensor_tensor(w_part[:, 2], w_rest[:], w_part[:, 1], ALU.subtract))
                link(dve.tensor_scalar(w_rest[:], dst_hi[:], 0.0, None, ALU.is_lt))
                link(dve.tensor_scalar(pad_at[:], w_rest[:], pcol[:, 0:1], None, ALU.mult))
                dve.scalar_tensor_tensor(pad_at[:], w_rest[:], float(TRASH), pad_at[:], ALU.mult, ALU.add)

        RING = 4
        oh_dst = tmp("oh_dst", [P, RING, T], BF16)
        oh_src = tmp("oh_src", [P, RING, T], BF16)
        lo_dst = tmp("lo_dst", [P, RING, P], BF16)
        lo_src = tmp("lo_src", [P, RING, P], BF16)
        lo_w = tmp("lo_w", [P, RING, 3, P], BF16)
        in_count, in_weight, out_count = psA[:, 0, 0:T], psA[:, 1, 0:T], psT[:, 0, 0:T]
        with phase(nc, "onehots", "weighted", "counted") as (block, (onehots, weighted, counted)):
            @block.vector
            def _(dve):
                def step(i, k):
                    c, r = U * i + k, k % RING
                    need(dve, counted, c - RING + 1)
                    dve.tensor_scalar(lo_dst[:, r], iota_h[:, 0:P], dst_lo[:, bass.ds(c, 1)], None,
                                      ALU.is_equal).then_inc(onehots, 1)
                    dve.tensor_scalar(oh_dst[:, r], iota_h[:, 0:T], dst_hi[:, bass.ds(c, 1)], None, ALU.is_equal)
                    dve.tensor_scalar(oh_src[:, r], iota_h[:, 0:T], src_hi[:, bass.ds(c, 1)], None, ALU.is_equal)
                    dve.tensor_scalar(lo_src[:, r], iota_h[:, 0:P], src_lo[:, bass.ds(c, 1)], None,
                                      ALU.is_equal).then_inc(onehots, 1)
                sweep(dve, C, 0, step, 0)

            @block.scalar
            def _(act):
                def step(i, k):
                    c, r = U * i + k, k % RING
                    act.wait_ge(onehots, 2 * c + 1)
                    need(act, counted, c - RING + 1)
                    for j in range(3):
                        last = act.activation(lo_w[:, r, j], lo_dst[:, r], ACT.Copy,
                                              scale=w_part[:, j, bass.ds(c, 1)])
                    last.then_inc(weighted, 1)
                sweep(act, C, 0, step, 0)

            @block.tensor
            def _(pe):
                def step(i, k):
                    c, r = U * i + k, k % RING
                    at_start = isinstance(i, int) and i == 0 and k == 0
                    at_end = isinstance(i, int) and i == C // U - 1 and k == U - 1
                    pe.wait_ge(onehots, 2 * c + 2)
                    pe.matmul(in_count, lo_dst[:, r], oh_dst[:, r], start=at_start, stop=at_end)
                    pe.matmul(out_count, lo_src[:, r], oh_src[:, r], start=at_start, stop=at_end)
                    pe.wait_ge(weighted, c + 1)
                    for j in range(3):
                        last = pe.matmul(in_weight, lo_w[:, r, j], oh_dst[:, r], start=at_start and j == 0,
                                         stop=at_end and j == 2)
                    last.then_inc(counted, 1)
                sweep(pe, C, 0, step, 0)

        in_sb = tmp("in_sb", [P, T])
        out_sb = tmp("out_sb", [P, T])
        deg = tmp("deg", [P, T])
        row_i = tmp("row_i", [P, T], I32)
        seed = tmp("seed", [P, T])
        ranks = [psO[:, 0, 0:T], psO[:, 1, 0:T]]
        with phase(nc, "degrees", "rooted", "dve_done") as (block, (degrees, rooted, dve_done)):
            @block.scalar
            def _(act):
                act.wait_ge(degrees, 1)
                act.activation(dinv[:], dinv[:], ACT.Sqrt)
                act.activation(root_out[:], root_out[:], ACT.Sqrt).then_inc(rooted, 1)

            @block.vector
            def _(dve):
                steps = [0]

                def link(ins):
                    steps[0] += 1
                    ins.then_inc(dve_done, 1)
                    dve.wait_ge(dve_done, steps[0])

                dve.tensor_copy(in_sb[:], in_count)
                link(dve.tensor_copy(out_sb[:], out_count))
                for plan in (by_dst, by_src):
                    for a in (plan.overflow, plan.upto, plan.first, plan.base):
                        dve.memset(a[:], 0.0)
                link(dve.tensor_scalar(deg[:], in_weight, 1.0, None, ALU.add))
                dve.tensor_scalar(dinv[:], deg[:], 1e-30, None, ALU.max)
                dve.tensor_scalar(root_out[:], out_sb[:], 1.0, None, ALU.max).then_inc(degrees, 1)
                dve.wait_ge(rooted, 1)
                link(dve.tensor_scalar(deg[:], deg[:], 0.0, None, ALU.is_gt))
                link(dve.reciprocal(dinv[:], dinv[:]))
                dve.reciprocal(root_out[:], root_out[:])
                link(dve.tensor_tensor(dinv[:], dinv[:], deg[:], ALU.mult))
                dve.tensor_scalar(has_in[:], in_sb[:], 0.0, None, ALU.is_gt)
                link(dve.tensor_scalar(inv_deg[:], in_sb[:], 1.0, None, ALU.max))
                link(dve.reciprocal(inv_deg[:], inv_deg[:]))
                dve.tensor_tensor(inv_deg[:], inv_deg[:], has_in[:], ALU.mult)

        def place_tiles(plan, counts):
            with phase(nc, "totals", "seed_made", "dve_done") as (block, (totals, seed_made, dve_done)):
                @block.tensor
                def _(pe):
                    pe.matmul(psM[:, 0, 0:T], ones_f[:], counts[:], start=True, stop=True).then_inc(totals, 1)
                    pe.wait_ge(seed_made, 1)
                    for rank in ranks:
                        pe.matmul(rank, ones_f[0:1, :], seed[0:1, :], start=True, stop=True)

                @block.vector
                def _(dve):
                    steps = [0]

                    def link(ins):
                        steps[0] += 1
                        ins.then_inc(dve_done, 1)
                        dve.wait_ge(dve_done, steps[0])

                    overflow, upto, first, base = [a[:, 0:T] for a in (plan.overflow, plan.upto, plan.first, plan.base)]
                    dve.wait_ge(totals, 1)
                    link(dve.tensor_scalar(row_i[:], psM[:, 0, 0:T], 1.0, -1.0, ALU.max, ALU.add))
                    link(dve.tensor_scalar(row_i[:], row_i[:], 7, None, ALU.arith_shift_right))
                    link(dve.tensor_copy(overflow, row_i[:]))
                    link(dve.tensor_tensor_scan(upto, ones_row[:, 0:T], overflow, 0.0, ALU.mult, ALU.add))
                    link(dve.tensor_tensor(first, upto, overflow, ALU.subtract))
                    link(dve.tensor_tensor(base, first, iota_f[:, 0:T], ALU.add))
                    dve.tensor_scalar(seed[:], base, float(P), None, ALU.mult).then_inc(seed_made, 1)
                    link(dve.tensor_scalar(deg[:], overflow, 0.0, None, ALU.is_gt))
                    link(dve.scalar_tensor_tensor(deg[:], upto, -1.0 - XB, deg[:], ALU.add, ALU.mult))
                    dve.tensor_scalar(plan.sums_at[:], deg[:], float(XB), None, ALU.add)
                    link(dve.tensor_scalar(row_i[:, 0:1], plan.upto[:, T - 1:T], -1.0, 2.0 * XU, ALU.add, ALU.max))
                    assert XU == 8
                    dve.tensor_scalar(plan.x_last[:], row_i[:, 0:1], 3, None, ALU.arith_shift_right)

        rank8 = tmp("rank8", [P, U])
        junk_t = tmp("junk_t", [P, T])
        row_at = tmp("row_at", [P, U], I32)
        staged = tmp("staged", [P, U, 4])
        xin = tmp("xin", [P, 4, 2, ROW])
        junk_d = tmp("junk_d", [P, D])
        score8 = tmp("score8", [P, 2, 4])
        x_pairs = x[0:(N // (2 * P)) * 2 * P, :].rearrange("(g k p) d -> g p k d", k=2, p=P)
        t0_pairs = table0.rearrange("(g k p) d -> g p k d", k=2, p=P)
        WHOLE_PAIRS = N // (2 * P)

        def place_edges(plan, key_hi, with_scores, uses):
            with phase(nc, f"{plan.name}_onehot", "rank_ready", "rank_read", "places", "fields_staged", "dots", "dots_kept", "pad_zero",
                       *[f"x_in{k}" for k in range(4)],
                       *[f"t0_out{k}" for k in range(4)], "coef_set", "ones_used") as (
                    block, (onehot, rank_ready, rank_read, places, fields_staged, dots, dots_kept, pad_zero, *dmas)):
                x_in, t0_out, coef_set, ones_used = dmas[0:4], dmas[4:8], dmas[8], dmas[9]

                @block.tensor
                def _(pe):
                    def step(i, k):
                        c, r, mine, other = U * i + k, k % RING, ranks[k % 2], ranks[(k + 1) % 2]
                        pe.wait_ge(onehot, c + 1)
                        pe.matmul(mine, before[:], oh_dst[:, r], start=False, stop=True,
                                  skip_group_check=True).then_inc(rank_ready, 1)
                        need(pe, rank_read, c)
                        if not (isinstance(c, int) and c == 0):
                            pe.matmul(other, not_before[:], oh_dst[:, (k - 1) % RING], start=False, stop=True,
                                      skip_group_check=True)
                        pe.matmul(other, ones_b[:], oh_dst[:, r], start=False, stop=True,
                                  skip_group_check=True).then_inc(ones_used, 1)
                    sweep(pe, C, 0, step, 0)

                @block.vector
                def _(dve):
                    def step(i, k):
                        c, r = U * i + k, k % RING
                        need(dve, ones_used, c - RING + 2)
                        dve.tensor_scalar(oh_dst[:, r], iota_h[:, 0:T], key_hi[:, bass.ds(c, 1)], None,
                                          ALU.is_equal).then_inc(onehot, 1)
                        h, q = k // 4, k % 4
                        if with_scores:
                            if isinstance(c, int) and c == T - U:
                                dve.wait_ge(t0_out[3], 16 * (T // U - 1))
                                dve.memset(xin[:, 3], 0.0).then_inc(pad_zero, 1)
                            dve.wait_ge(x_in[k // 2], 16 * (i + 1))
                            need(dve, dots, c)
                            dve.tensor_tensor_reduce(junk_d[:], xin[:, k // 2, k % 2, 0:D], p_row[:], 1.0, 0.0, ALU.mult,
                                                     ALU.add, score8[:, h, q:q + 1]).then_inc(dots, 1)
                            if q == 3:
                                dve.wait_ge(dots, U * i + k + 1)
                                dve.tensor_copy(score[:, bass.ds(U * i + 4 * h, 4)], score8[:, h]).then_inc(dots_kept, 1)
                        dve.wait_ge(rank_ready, c + 1)
                        dve.wait_ge(onehot, c + 1)
                        need(dve, rank_read, c)
                        dve.tensor_tensor_reduce(junk_t[:], ranks[k % 2], oh_dst[:, r], 1.0, 0.0, ALU.mult, ALU.add,
                                                 rank8[:, k:k + 1]).then_inc(rank_read, 1)
                        if q == 3:
                            for j in range(4 * h, 4 * h + 4):
                                slot_freed(dve, gathered_m[j], i, uses)
                            dve.wait_ge(rank_read, c + 1)
                            dve.tensor_tensor(row_at[:, 4 * h:4 * h + 4], rank8[:, 4 * h:4 * h + 4],
                                              pad_at[:, bass.ds(U * i + 4 * h, 4)], ALU.add).then_inc(places, 1)
                    sweep(dve, C, 0, step, 0)

                @block.gpsimd
                def _(pool):
                    def step(i, k):
                        if k % 4 == 0:
                            for j in range(k, k + 4):
                                slot_freed(pool, gathered_m[j], i, uses)
                            pool.tensor_copy(staged[:, k:k + 4, :], fields[plan][:, bass.ds(U * i + k, 4), :]).then_inc(
                                fields_staged, 1)
                            pool.wait_ge(fields_staged, 2 * i + k // 4 + 1)
                            pool.wait_ge(places, 2 * i + k // 4 + 1)
                            take_waits(pool)
                        pool.indirect_dma_start(plan.tables[k], bass.IndirectOffsetOnAxis(ap=row_at[:, k:k + 1], axis=0),
                                                staged[:, k, :], None).then_inc(gathered_m[k], 16)
                    sweep(pool, C, 0, step, 0)
                    for j in range(U):
                        pool.wait_ge(gathered_m[j], 16 * (uses + C // U))

                @block.sync
                def _(sp):
                    if not with_scores:
                        return

                    def step(i, k):
                        if k % 2:
                            return
                        g, r = 4 * i + k // 2, k // 2
                        need(sp, t0_out[r], 16 * i)
                        if isinstance(g, int) and g >= WHOLE_PAIRS:
                            if g == WHOLE_PAIRS:
                                sp.wait_ge(pad_zero, 1)
                                sp.dma_start(xin[0:REST, r, 0, 0:D], x[N - REST:N, :]).then_inc(x_in[r], 16)
                            return
                        sp.dma_start(xin[:, r, :, 0:D], x_pairs[g]).then_inc(x_in[r], 16)
                    sweep(sp, T, 0, step, 0)

                @block.scalar
                def _(act):
                    if not with_scores:
                        return

                    def step(i, k):
                        if k % 2 == 0:
                            return
                        g, r, t = 4 * i + k // 2, k // 2, U * i + k - 1
                        need(act, t0_out[r], 16 * i)
                        act.copy(xin[:, r, :, D], dinv[:, bass.ds(t, 2)]).then_inc(coef_set, 1)
                        act.wait_ge(coef_set, g + 1)
                        act.wait_ge(dots, U * i + k + 1)
                        act.dma_start(t0_pairs[g], xin[:, r]).then_inc(t0_out[r], 16)
                    sweep(act, T, 0, step, 0)
                    for r in range(4):
                        act.wait_ge(t0_out[r], 16 * (T // U))

        place_tiles(by_dst, in_sb)
        place_edges(by_dst, dst_hi, True, 0)
        place_tiles(by_src, out_sb)
        place_edges(by_src, src_hi, False, C // U)
        early.close()
        before_now = [2 * (C // U)] * U

        mid = ExitStack()

        def tmp(name, shape, dt=F32):
            return mid.enter_context(nc.sbuf_tensor(name, shape, dt))

        main_at = tmp("main_at", [P, TB], I32)
        extra_at = tmp("extra_at", [P, TB], I32)
        first_col = tmp("first_col", [P, TB])
        has_over = tmp("has_over", [P, TB, P])
        starts = tmp("starts", [P, TB, TW])
        x_num = tmp("x_num", [P, TB])
        before_x = tmp("before_x", [P, T])
        tile_of = tmp("tile_of", [P, TB])
        table_rows = tmp("table_rows", [P, 2, U, 4 * P])
        chunk_rows = tmp("chunk_rows", [P, 2, 4 * P])

        def list_chunks(plan, uses):
            edge_chunks = [e[0:SLOTS * P, :].rearrange("(v e) f -> v (e f)", e=P) for e in plan.tables]
            with phase(nc, "cols_made", "cols_read", "lists_made", "fields_made", "fields_read", "starts_made",
                       "carried", "rows_summed", "dve_done") as (
                    block, (cols_made, cols_read, lists_made, fields_made, fields_read, starts_made, carried,
                            rows_summed, dve_done)):
                jobs = [(b, half) for half in range(2) for b in range(TB)]

                @block.tensor
                def _(pe):
                    for b in range(TB):
                        at = slice(b * P, b * P + P)
                        need(pe, cols_read, b)
                        for j, row in enumerate((plan.base, plan.first, plan.overflow)):
                            last = pe.transpose(psM[:, 0, j * P:j * P + P], row[:, at], ident[:])
                        last.then_inc(cols_made, 1)
                    for b in range(TB):
                        pe.wait_ge(starts_made, b + 1)
                        last = pe.matmul(psT[:, 0, 0:TW], has_over[:, b], starts[:, b], start=b == 0, stop=b == TB - 1)
                    last.then_inc(carried, 1)
                    for n, (b, half) in enumerate(jobs):
                        pe.wait_ge(rows_summed, n + 1)
                        rows = chunk_rows[:, n % 2].rearrange("v (e f) -> v f e", f=4)
                        need(pe, fields_read, n - 1)
                        for f in range(3):
                            last = pe.transpose(psO[:, n % 2, f * P:f * P + P], rows[:, f], ident[:])
                        last.then_inc(fields_made, 1)

                @block.vector
                def _(dve):
                    steps = [0]

                    def link(ins):
                        steps[0] += 1
                        ins.then_inc(dve_done, 1)
                        dve.wait_ge(dve_done, steps[0])

                    for b in range(TB):
                        dve.wait_ge(cols_made, b + 1)
                        dve.tensor_copy(main_at[:, b:b + 1], psM[:, 0, 0:1])
                        dve.tensor_copy(first_col[:, b:b + 1], psM[:, 0, P:P + 1])
                        dve.tensor_scalar(has_over[:, b], psM[:, 0, 2 * P:3 * P], 0.0, None, ALU.is_gt).then_inc(cols_read, 1)
                    dve.wait_ge(cols_read, TB)
                    for b in range(TB):
                        link(dve.tensor_scalar(x_num[:, b:b + 1], pcol[:], float(b * P), None, ALU.add))
                        link(dve.tensor_scalar(before_x[:], plan.upto[:, 0:T], x_num[:, b:b + 1], None, ALU.is_le))
                        link(dve.tensor_reduce(tile_of[:, b:b + 1], before_x[:], AX.X, ALU.add))
                        link(dve.scalar_tensor_tensor(extra_at[:, b:b + 1], tile_of[:, b:b + 1], 1.0, x_num[:, b:b + 1],
                                                      ALU.add, ALU.add))
                    dve.tensor_scalar(x_num[:, 0:1], pcol[:], 0.0, None, ALU.add).then_inc(lists_made, 1)
                    for b in range(TB):
                        dve.tensor_scalar(starts[:, b], iota_f[:], first_col[:, b:b + 1], None, ALU.is_equal).then_inc(
                            starts_made, 1)
                    dve.wait_ge(carried, 1)
                    dve.tensor_scalar(plan.carry[:], psT[:, 0, 0:TW], -1.0, 1.0, ALU.mult, ALU.add)
                    def copy_fields(n):
                        b, half = jobs[n]
                        at = slice(b * P, b * P + P)
                        to_src, to_lo, to_w = (plan.main, plan.extra)[half]
                        dve.wait_ge(fields_made, n + 1)
                        dve.tensor_copy(to_src[:, at], psO[:, n % 2, 0:P])
                        dve.tensor_scalar(to_lo[:, at], psO[:, n % 2, P:2 * P], -1.0, None, ALU.add)
                        dve.tensor_copy(to_w[:, at], psO[:, n % 2, 2 * P:3 * P]).then_inc(fields_read, 1)

                    for n in range(len(jobs)):
                        if n >= 2:
                            copy_fields(n - 2)
                        dve.wait_ge(gathered_m[n % 2], 16 * (uses[n % 2] + U * (n // 2 + 1)))
                        dve.tensor_reduce(chunk_rows[:, n % 2], table_rows[:, n % 2].rearrange("v k x -> v x k"), AX.X,
                                          ALU.add).then_inc(rows_summed, 1)
                    for n in range(len(jobs) - 2, len(jobs)):
                        copy_fields(n)

                @block.gpsimd
                def _(pool):
                    pool.wait_ge(lists_made, 1)
                    for n, (b, half) in enumerate(jobs):
                        at = (main_at, extra_at)[half]
                        need(pool, rows_summed, n - 1)
                        for k in range(U):
                            pool.indirect_dma_start(table_rows[:, n % 2, k], None, edge_chunks[k],
                                                    bass.IndirectOffsetOnAxis(ap=at[:, b:b + 1], axis=0)).then_inc(
                                gathered_m[n % 2], 16)

        for plan in (by_dst, by_src):
            list_chunks(plan, before_now)
            before_now = [n + U * TB * (k < 2) for k, n in enumerate(before_now)]
        mid.close()
        mid = ExitStack()

        bits = score[:].bitcast(I32)
        key_i = tmp("key_i", [P, T], I32)
        half_i = tmp("half_i", [P, T], I32)
        key_hi = tmp("key_hi", [P, T])
        key_lo = tmp("key_lo", [P, T])
        real = tmp("real", [P, T])
        hits = tmp("hits", [P, T])
        count = tmp("count", [P, 1])
        wanted = tmp("wanted", [P, 1])
        best_hi = tmp("best_hi", [P, 1])
        best_lo = tmp("best_lo", [P, 1])
        unit = tmp("unit", [P, 1])
        trial = tmp("trial", [P, 1])
        taken = tmp("taken", [P, 1])
        above = tmp("above", [P, T], BF16)
        equal = tmp("equal", [P, T], BF16)
        tmp_t = tmp("tmp_t", [P, T])
        col_sum = tmp("col_sum", [P, T])
        place = tmp("place", [P, T])
        place_eq = tmp("place_eq", [P, T])
        pair_of = tmp("pair_of", [P, T, 2], FP16)

        HALF = 16
        with phase(nc, "counts", "total", "dve_done", "loop_done") as (block, (counts, total, dve_done, loop_done)):
            @block.tensor
            def _(pe):
                for half in range(2):
                    with pe.Fori(0, HALF) as j:
                        n = (HALF + 1) * half + j
                        pe.wait_ge(counts, n + 1)
                        pe.matmul(psM[:, 0, 0:1], ones_f[:], count[:], start=True, stop=True).then_inc(total, 1)
                    n = (HALF + 1) * half + HALF
                    pe.wait_ge(counts, n + 1)
                    pe.matmul(psM[:, 0, 0:1], ones_f[:], count[:], start=True, stop=True).then_inc(total, 1)

            @block.vector
            def _(dve):
                steps = [0]

                def link(ins):
                    steps[0] += 1
                    ins.then_inc(dve_done, 1)
                    dve.wait_ge(dve_done, steps[0])

                def bisect(keys, best, half):
                    link(dve.memset(best[:], 0.0))
                    link(dve.memset(unit[:], float(1 << (HALF - 1))))
                    with dve.Fori(0, HALF) as j:
                        n, m = (HALF + 1) * half + j, 5 * (HALF * half + j)
                        dve.tensor_scalar(trial[:], best[:], unit[:, 0:1], None, ALU.add).then_inc(loop_done, 1)
                        dve.wait_ge(loop_done, m + 1)
                        dve.tensor_scalar(hits[:], keys[:], trial[:, 0:1], None, ALU.is_ge).then_inc(loop_done, 1)
                        dve.wait_ge(loop_done, m + 2)
                        dve.tensor_reduce(count[:], hits[:], AX.X, ALU.add).then_inc(counts, 1)
                        dve.wait_ge(total, n + 1)
                        dve.scalar_tensor_tensor(taken[:], psM[:, 0, 0:1], wanted[:, 0:1], unit[:], ALU.is_ge,
                                                 ALU.mult).then_inc(loop_done, 1)
                        dve.wait_ge(loop_done, m + 3)
                        dve.tensor_tensor(best[:], best[:], taken[:], ALU.add).then_inc(loop_done, 1)
                        dve.tensor_scalar(unit[:], unit[:], 0.5, None, ALU.mult).then_inc(loop_done, 1)
                        dve.wait_ge(loop_done, m + 5)
                    link(dve.tensor_scalar(hits[:], keys[:], best[:, 0:1], None, ALU.is_gt))
                    dve.tensor_reduce(count[:], hits[:], AX.X, ALU.add).then_inc(counts, 1)
                    dve.wait_ge(total, (HALF + 1) * half + HALF + 1)
                    link(dve.scalar_tensor_tensor(wanted[:], psM[:, 0, 0:1], -1.0, wanted[:], ALU.mult, ALU.add))

                link(dve.tensor_scalar(key_i[:], bits, 31, None, ALU.arith_shift_right))
                link(dve.tensor_scalar(key_i[:], key_i[:], -2147483648, None, ALU.bitwise_or))
                link(dve.tensor_tensor(key_i[:], key_i[:], bits, ALU.bitwise_xor))
                link(dve.tensor_scalar(half_i[:], key_i[:], HALF, 0xFFFF, ALU.logical_shift_right, ALU.bitwise_and))
                link(dve.tensor_copy(key_hi[:], half_i[:]))
                link(dve.tensor_scalar(half_i[:], key_i[:], 0xFFFF, None, ALU.bitwise_and))
                link(dve.tensor_copy(key_lo[:], half_i[:]))
                link(dve.tensor_scalar(tmp_t[:], iota_f[:, 0:T], float(P), pcol[:, 0:1], ALU.mult, ALU.add))
                link(dve.tensor_scalar(real[:], tmp_t[:], float(N), None, ALU.is_lt))
                link(dve.scalar_tensor_tensor(key_hi[:], key_hi[:], 1.0, real[:], ALU.add, ALU.mult))
                link(dve.tensor_scalar(key_hi[:], key_hi[:], -1.0, None, ALU.add))
                link(dve.memset(wanted[:], float(K)))
                bisect(key_hi, best_hi, 0)
                link(dve.tensor_scalar(above[:], key_hi[:], best_hi[:, 0:1], None, ALU.is_gt))
                link(dve.tensor_scalar(hits[:], key_hi[:], best_hi[:, 0:1], None, ALU.is_equal))
                link(dve.scalar_tensor_tensor(key_lo[:], key_lo[:], 1.0, hits[:], ALU.add, ALU.mult))
                link(dve.tensor_scalar(key_lo[:], key_lo[:], -1.0, None, ALU.add))
                bisect(key_lo, best_lo, 1)
                link(dve.tensor_scalar(hits[:], key_lo[:], best_lo[:, 0:1], None, ALU.is_gt))
                dve.tensor_tensor(above[:], above[:], hits[:], ALU.add)
                dve.tensor_scalar(equal[:], key_lo[:], best_lo[:, 0:1], None, ALU.is_equal)
                dve.tensor_copy(pair_of[:, :, 0], iota_f[:, 0:T])
                dve.tensor_copy(pair_of[:, :, 1], pcol[:, 0:1].to_broadcast([P, T]))

        with phase(nc, "prefixed", "dve_done") as (block, (prefixed, dve_done)):
            @block.tensor
            def _(pe):
                for j, mask in enumerate((above, equal)):
                    pe.matmul((psM, psO)[j][:, 0, 0:T], before[:], mask[:], start=True, stop=True)
                    last = pe.matmul((psM, psO)[j][:, 1, 0:T], ones_b[:], mask[:], start=True, stop=True)
                last.then_inc(prefixed, 1)

            @block.vector
            def _(dve):
                steps = [0]

                def link(ins):
                    steps[0] += 1
                    ins.then_inc(dve_done, 1)
                    dve.wait_ge(dve_done, steps[0])

                dve.wait_ge(prefixed, 1)
                for ps, to in ((psM, place), (psO, place_eq)):
                    link(dve.tensor_copy(tmp_t[:], ps[:, 1, 0:T]))
                    link(dve.tensor_tensor_scan(col_sum[:], ones_row[:, 0:T], tmp_t[:], 0.0, ALU.mult, ALU.add))
                    if ps is psM:
                        link(dve.tensor_copy(count[:], col_sum[:, T - 1:T]))
                    link(dve.tensor_tensor(col_sum[:], col_sum[:], tmp_t[:], ALU.subtract))
                    link(dve.tensor_tensor(to[:], ps[:, 0, 0:T], col_sum[:], ALU.add))
                link(dve.scalar_tensor_tensor(place[:], place[:], 1.0, above[:], ALU.add, ALU.mult))
                link(dve.tensor_scalar(hits[:], place_eq[:], wanted[:, 0:1], None, ALU.is_lt))
                link(dve.tensor_tensor(hits[:], hits[:], equal[:], ALU.mult))
                link(dve.tensor_scalar(count[:], count[:], 1.0, None, ALU.add))
                link(dve.scalar_tensor_tensor(place_eq[:], place_eq[:], count[:, 0:1], hits[:], ALU.add, ALU.mult))
                link(dve.tensor_tensor(place[:], place[:], place_eq[:], ALU.add))
                dve.tensor_scalar(place[:], place[:], -1.0, None, ALU.add)

        picks = tmp("picks", [P, RING, K], FP16)
        picked = [psM[:, 0, 0:2], psM[:, 1, 0:2]]
        with phase(nc, "picks_made", "picks_used") as (block, (picks_made, picks_used)):
            @block.vector
            def _(dve):
                def step(i, k):
                    c = U * i + k
                    need(dve, picks_used, c - RING + 1)
                    dve.tensor_scalar(picks[:, k % RING], iota_h[:, 0:K], place[:, bass.ds(c, 1)], None,
                                      ALU.is_equal).then_inc(picks_made, 1)
                sweep(dve, T, 0, step, 0)

            @block.tensor
            def _(pe):
                def step(i, k):
                    c = U * i + k
                    at_start = isinstance(c, int) and c == 0
                    at_end = isinstance(c, int) and c == T - 1
                    pe.wait_ge(picks_made, c + 1)
                    for b in range(K // P):
                        last = pe.matmul(picked[b], picks[:, k % RING, b * P:b * P + P],
                                         pair_of[:, bass.ds(c, 1), :].rearrange("p a b -> p (a b)"),
                                         start=at_start, stop=at_end)
                    last.then_inc(picks_used, 1)
                sweep(pe, T, 0, step, 0)

        KB = K // P
        node = tmp("node", [P, KB])
        node_i = tmp("node_i", [P, KB], I32)
        pick_rows = tmp("pick_rows", [P, KB, ROW])
        pick_dot = tmp("pick_dot", [P, KB])
        norm = tmp("norm", [P, 1])
        tanh_s = tmp("tanh_s", [P, KB])
        shared = tmp("shared", [P, 2, KB, P])
        rows_sn = tmp("rows_sn", [P, 2, K])
        greater = tmp("greater", [P, K])
        same = tmp("same", [P, K])
        rank = tmp("rank", [P, KB])
        order = tmp("order", [P, KB, K])
        w_ih = tmp("w_ih", [P, 6, D])
        w_hh = tmp("w_hh", [P, 6, D])
        w_ih_t = tmp("w_ih_t", [P, DB, 3 * D])
        w_hh_t = tmp("w_hh_t", [P, DB, 3 * D])
        w0 = tmp("w0", [P, DB, D])
        w0_t = tmp("w0_t", [P, DB, D])
        x_t = tmp("x_t", [P, DB, K])
        bih_row = tmp("bih_row", [P, 3 * D])
        bhh_row = tmp("bhh_row", [P, 3 * D])
        gate = tmp("gate", [P, KB, 2 * D])
        cand = tmp("cand", [P, KB, D])
        hid = tmp("hid", [P, KB, D])

        with phase(nc, "nodes_made", "w_in", "dots_made", "tanhs", "shared_made", "turned", "dve_done",
                   "w_turned", "w_copied", "ordered", "norm_made") as (
                block, (nodes_made, w_in, dots_made, tanhs, shared_made, turned, dve_done, w_turned, w_copied,
                        ordered, norm_made)):
            @block.sync
            def _(sp):
                sp.dma_start(w_ih[:], W_ih.rearrange("(b p) d -> p b d", p=P)).then_inc(w_in, 16)
                sp.dma_start(w_hh[:], W_hh.rearrange("(b p) d -> p b d", p=P)).then_inc(w_in, 16)
                sp.dma_start(w0[:], W0.rearrange("(b p) d -> p b d", p=P)).then_inc(w_in, 16)
                for to, what in ((bih_row, b_ih), (bhh_row, b_hh)):
                    sp.dma_start(to[:], what.rearrange("(a d) -> a d", a=1).to_broadcast([P, 3 * D])).then_inc(w_in, 16)
                sp.wait_ge(w_in, 16 * 5)

            @block.gpsimd
            def _(pool):
                pool.wait_ge(nodes_made, 1)
                for b in range(KB):
                    pool.indirect_dma_start(pick_rows[:, b], None, table0,
                                            bass.IndirectOffsetOnAxis(ap=node_i[:, b:b + 1], axis=0)).then_inc(
                        gathered_m[0], 16)

            turns = [(w_ih, w_ih_t, o) for o in range(6)] + [(w_hh, w_hh_t, o) for o in range(6)] + \
                    [(w0, w0_t, o) for o in range(DB)]

            @block.vector
            def _(dve):
                steps = [0]

                def link(ins):
                    steps[0] += 1
                    ins.then_inc(dve_done, 1)
                    dve.wait_ge(dve_done, steps[0])

                for b in range(KB):
                    link(dve.tensor_copy(tmp_t[:, 0:2], picked[b]))
                    link(dve.scalar_tensor_tensor(node[:, b:b + 1], tmp_t[:, 0:1], float(P), tmp_t[:, 1:2], ALU.mult,
                                                  ALU.add))
                dve.tensor_copy(node_i[:], node[:]).then_inc(nodes_made, 1)
                link(dve.tensor_tensor_reduce(greater[:], p_row[:], p_row[:], 1.0, 0.0, ALU.mult, ALU.add, norm[:]))
                dve.tensor_copy(norm[:], norm[:]).then_inc(norm_made, 1)
                dve.wait_ge(norm_made, 2)
                link(dve.reciprocal(norm[:], norm[:]))
                dve.wait_ge(gathered_m[0], 16 * (before_now[0] + KB))
                for b in range(KB):
                    link(dve.tensor_tensor_reduce(greater[:], pick_rows[:, b, 0:D], p_row[:], 1.0, 0.0, ALU.mult, ALU.add,
                                                  pick_dot[:, b:b + 1]))
                dve.tensor_copy(rank[:], pick_dot[:]).then_inc(dots_made, 1)
                for b in range(KB):
                    dve.tensor_scalar(shared[:, 0, b], ones_f[:], pick_dot[:, b:b + 1], None, ALU.mult)
                    last = dve.tensor_scalar(shared[:, 1, b], ones_f[:], node[:, b:b + 1], None, ALU.mult)
                last.then_inc(shared_made, 1)
                dve.wait_ge(turned, 1)
                link(dve.tensor_copy(rows_sn[:].rearrange("p a k -> p (a k)"), psA[:, 0, :]))
                for b in range(KB):
                    link(dve.tensor_scalar(greater[:], rows_sn[:, 0], pick_dot[:, b:b + 1], None, ALU.is_gt))
                    link(dve.tensor_scalar(same[:], rows_sn[:, 0], pick_dot[:, b:b + 1], None, ALU.is_equal))
                    link(dve.scalar_tensor_tensor(same[:], rows_sn[:, 1], node[:, b:b + 1], same[:], ALU.is_lt, ALU.mult))
                    link(dve.tensor_tensor(same[:], same[:], greater[:], ALU.add))
                    link(dve.tensor_reduce(rank[:, b:b + 1], same[:], AX.X, ALU.add))
                    link(dve.tensor_scalar(order[:, b], iota_f[:, 0:K], rank[:, b:b + 1], None, ALU.is_equal))
                dve.wait_ge(tanhs, 1)
                for b in range(KB):
                    link(dve.tensor_scalar(pick_rows[:, b, 0:D], pick_rows[:, b, 0:D], tanh_s[:, b:b + 1], None, ALU.mult))
                dve.tensor_copy(count[:], norm[:]).then_inc(ordered, 1)
                for n, (_, to, o) in enumerate(turns):
                    dve.wait_ge(w_turned, n + 1)
                    for b in range(DB):
                        last = dve.tensor_copy(to[:, b, o * P:o * P + P], psT[:, n % 2, b * P:b * P + P])
                    last.then_inc(w_copied, 1)
                dve.wait_ge(ordered, 2)
                for b in range(DB):
                    dve.tensor_copy(x_t[:, b], psO[:, b, 0:K])

            @block.scalar
            def _(act):
                act.wait_ge(norm_made, 1)
                act.activation(norm[:], norm[:], ACT.Sqrt).then_inc(norm_made, 1)
                act.wait_ge(dots_made, 1)
                act.activation(tanh_s[:], pick_dot[:], ACT.Tanh, scale=norm[:, 0:1]).then_inc(tanhs, 1)

            @block.tensor
            def _(pe):
                pe.wait_ge(shared_made, 1)
                for a in range(2):
                    for b in range(KB):
                        last = pe.transpose(psA[:, 0, (a * KB + b) * P:(a * KB + b + 1) * P], shared[:, a, b], ident[:])
                last.then_inc(turned, 1)
                pe.wait_ge(ordered, 1)
                for d in range(DB):
                    for b in range(KB):
                        last = pe.matmul(psO[:, d, 0:K], pick_rows[:, b, d * P:d * P + P], order[:, b], start=b == 0,
                                         stop=b == KB - 1)
                last.then_inc(ordered, 1)
                pe.wait_ge(w_in, 16 * 5)
                for n, (what, _, o) in enumerate(turns):
                    need(pe, w_copied, n - 1)
                    for b in range(DB):
                        last = pe.transpose(psT[:, n % 2, b * P:b * P + P], what[:, o, b * P:b * P + P], ident[:])
                    last.then_inc(w_turned, 1)

        with phase(nc, "products", "dve_done", "gates", "gated", "cands") as (
                block, (products, dve_done, gates, gated, cands)):
            @block.tensor
            def _(pe):
                for b in range(KB):
                    at = slice(b * P, b * P + P)
                    for n, (left, right) in enumerate([(x_t, w_ih_t), (w0_t, w_hh_t)]):
                        for d in range(DB):
                            pe.matmul(psA[:, b, 0:2 * D], left[:, d, at], right[:, d, 0:2 * D], start=n + d == 0,
                                      stop=n + d == DB)
                        for d in range(DB):
                            last = pe.matmul((psT, psO)[n][:, b, 0:D], left[:, d, at], right[:, d, 2 * D:3 * D],
                                             start=d == 0, stop=d == DB - 1)
                    last.then_inc(products, 1)

            @block.vector
            def _(dve):
                steps = [0]

                def link(ins):
                    steps[0] += 1
                    ins.then_inc(dve_done, 1)
                    dve.wait_ge(dve_done, steps[0])

                for b in range(KB):
                    dve.wait_ge(products, b + 1)
                    link(dve.tensor_tensor(gate[:, b], psA[:, b, 0:2 * D], bih_row[:, 0:2 * D], ALU.add))
                    dve.tensor_tensor(gate[:, b], gate[:, b], bhh_row[:, 0:2 * D], ALU.add).then_inc(gates, 1)
                    link(dve.tensor_tensor(cand[:, b], psT[:, b, 0:D], bih_row[:, 2 * D:], ALU.add))
                    link(dve.tensor_tensor(hid[:, b], psO[:, b, 0:D], bhh_row[:, 2 * D:], ALU.add))
                    dve.wait_ge(gated, b + 1)
                    link(dve.tensor_tensor(hid[:, b], hid[:, b], gate[:, b, 0:D], ALU.mult))
                    dve.tensor_tensor(cand[:, b], cand[:, b], hid[:, b], ALU.add).then_inc(gates, 1)
                    dve.wait_ge(cands, b + 1)
                    link(dve.tensor_tensor(hid[:, b], w0[:, b], cand[:, b], ALU.subtract))
                    link(dve.tensor_tensor(hid[:, b], hid[:, b], gate[:, b, D:2 * D], ALU.mult))
                    link(dve.tensor_tensor(w_gcn[:, b], hid[:, b], cand[:, b], ALU.add))

            @block.scalar
            def _(act):
                for b in range(KB):
                    act.wait_ge(gates, 2 * b + 1)
                    act.activation(gate[:, b], gate[:, b], ACT.Sigmoid).then_inc(gated, 1)
                    act.wait_ge(gates, 2 * b + 2)
                    act.activation(cand[:, b], cand[:, b], ACT.Tanh).then_inc(cands, 1)
        mid.close()
        before_now[0] += KB

        rows = sb("rows", [P, U, ROW])
        gather_at = sb("gather_at", [P, U], I32)
        select = sb("select", [P, 4, P])
        edge_coef = sb("edge_coef", [P, U])
        running = sb("running", [P, U, D])
        xb = sb("xb", [P, 4, 2, ROW])
        rb = sb("rb", [P, 4, 2, D])
        extra = sb("extra", [P, U, D])
        total_b = sb("total_b", [P, 4, D])
        mixed = sb("mixed", [P, 4, 2, D])
        turned_b = sb("turned_b", [P, 2, 4, P])
        wb = sb("wb", [P, 2 * DB, D])
        u_b = sb("u_b", [P, 4, D])
        act_b = sb("act_b", [P, 2, D])
        v_b = sb("v_b", [P, 4, D])
        squares = sb("squares", [P, D])
        sq_sum = sb("sq_sum", [P, 2])
        inv_norm = sb("inv_norm", [P, 2])
        stats = sb("stats", [P, 4, 6])
        mean_var = sb("mean_var", [P, 4, 2])
        root = sb("root", [P, 4])
        length = sb("length", [P, 2])
        rstd = sb("rstd", [P, 4])
        shift = sb("shift", [P, 4])
        ob = sb("ob", [P, 4, 2, ROW])

        GCN, SAGE, SAGE_LAST, PAIR, CONV = range(5)

        def edge_sums(kind, width, table, srcs, los, ws, gathered):
            def gather(pool, i, k, base, staged, summed):
                c = U * i + k
                if k % 4 == 0:
                    for j in range(k, k + 4):
                        slot_freed(pool, gathered[j], i, base[j])
                    if isinstance(i, int) and i and not isinstance(base[k], int):
                        take_waits(pool, 3 + k // 4)
                    pool.tensor_copy(gather_at[:, k:k + 4], srcs[:, bass.ds(c, 4)]).then_inc(staged, 1)
                    pool.wait_ge(staged, 2 * i + k // 4 + 1)
                    need(pool, summed, c - U + 4)
                    take_waits(pool)
                pool.indirect_dma_start(rows[:, k, 0:width], None, table,
                                        bass.IndirectOffsetOnAxis(ap=gather_at[:, k:k + 1], axis=0)).then_inc(
                    gathered[k], 16)

            def coefficient(act, i, k, base, coef_made, selected):
                c = U * i + k
                act.wait_ge(gathered[k], 16 * (i + 1 + base[k]))
                need(act, selected, c - U + 1)
                act.activation(edge_coef[:, k:k + 1], ws[:, bass.ds(c, 1)], ACT.Copy,
                               scale=rows[:, k, D:D + 1]).then_inc(coef_made, 1)

            def choose(dve, i, k, base, coef_made, selected, summed):
                c, r = U * i + k, k % 4
                need(dve, summed, c - 3)
                if kind == GCN:
                    dve.wait_ge(coef_made, c + 1)
                    coef = edge_coef[:, k:k + 1]
                elif kind == PAIR:
                    dve.wait_ge(gathered[k], 16 * (i + 1 + base[k]))
                    coef = rows[:, k, D:D + 1]
                elif kind == CONV:
                    coef = ws[:, bass.ds(c, 1)]
                else:
                    coef = None
                lo = los[:, bass.ds(c, 1)]
                if coef is None:
                    dve.tensor_scalar(select[:, r], iota_f[:, 0:P], lo, None, ALU.is_equal).then_inc(selected, 1)
                else:
                    dve.tensor_scalar(select[:, r], iota_f[:, 0:P], lo, coef, ALU.is_equal, ALU.mult).then_inc(
                        selected, 1)

            def multiply(pe, i, k, base, selected, sum_read, summed):
                c = U * i + k
                pe.wait_ge(selected, c + 1)
                pe.wait_ge(gathered[k], 16 * (i + 1 + base[k]))
                need(pe, sum_read, c - 1)
                pe.matmul(psA[:, k % 2, 0:D], select[:, k % 4], rows[:, k, 0:D], start=True, stop=True).then_inc(
                    summed, 1)
            return gather, coefficient, choose, multiply

        def overflow_sweep(name, kind, width, table, weights, plan):
            gather, coefficient, choose, multiply = edge_sums(kind, width, table, *plan.extra, plan.gathered)

            def counted(eng, step):
                final = eng.value_load(plan.x_last[0:1, 0:1], min_val=2, max_val=XB // U - 1)
                base = [(final + 1) * plan.sweeps if plan.sweeps else 0] * U
                for i in range(2):
                    for k in range(U):
                        step(i, k, base)
                with eng.Fori(2, final + 1) as i:
                    for k in range(U):
                        step(i, k, base)
                return final

            with phase(nc, *[f"{name}_{n}" for n in ("staged", "coef_made", "selected", "summed", "sum_done", "w_in",
                                                     "carry_set")],
                       *[f"{name}_sums_out{k}" for k in range(U)]) as (
                    block, (staged, coef_made, selected, summed, sum_done, w_in, carry_set, *sums_out)):

                @block.gpsimd
                def _(pool):
                    counted(pool, lambda i, k, base: gather(pool, i, k, base, staged, summed))

                @block.scalar
                def _(act):
                    if kind == GCN:
                        counted(act, lambda i, k, base: coefficient(act, i, k, base, coef_made, selected))

                @block.tensor
                def _(pe):
                    final = counted(pe, lambda i, k, base: multiply(pe, i, k, base, selected, sum_done, summed))
                    for k in range(U):
                        pe.wait_ge(sums_out[k], 16 * final + 16)

                @block.vector
                def _(dve):
                    dve.memset(running[:, U - 1], 0.0).then_inc(carry_set, 1)
                    dve.wait_ge(carry_set, 1)

                    def add(i, k):
                        if isinstance(i, int) and i < 0:
                            return
                        c = U * i + k
                        dve.wait_ge(summed, c + 1)
                        need(dve, sum_done, c)
                        need(dve, sums_out[k], 16 * i)
                        dve.scalar_tensor_tensor(running[:, k], running[:, (k - 1) % U], plan.carry[:, bass.ds(c, 1)],
                                                 psA[:, k % 2, 0:D], ALU.mult, ALU.add).then_inc(sum_done, 1)

                    def step(i, k, base):
                        choose(dve, i, k, base, coef_made, selected, summed)
                        add(*tile_at(i, k - 1))
                    final = counted(dve, step)
                    add(final, U - 1)

                @block.sync
                def _(sp):
                    for j, w in enumerate(weights):
                        sp.dma_start(wb[:, DB * j:DB * j + DB], w.rearrange("(b p) d -> p b d", p=P)).then_inc(w_in, 16)

                    def step(i, k, base):
                        c = U * i + k
                        sp.wait_ge(sum_done, c + 1)
                        sp.dma_start(overflow_sums[bass.ds(c, 1)].rearrange("a p d -> p (a d)"), running[:, k]).then_inc(
                            sums_out[k], 16)
                    counted(sp, step)
                    need(sp, w_in, 16 * len(weights))
                    sp.wait_ge(sum_done, 1)

        def tile_sweep(name, kind, width, table, weights, bias, residual, target, plan):
            gather, coefficient, choose, multiply = edge_sums(kind, width, table, *plan.main, gathered_m)
            base = list(before_now)
            pairs = table.rearrange("(g k p) d -> g p k d", k=2, p=P)
            final = target is None
            out_width = D if final else target.shape[1]
            out_pairs = (out[0:WHOLE_PAIRS * 2 * P] if final else target).rearrange("(g k p) d -> g p k d", k=2, p=P)
            LAG = {GCN: 5, SAGE: 3, SAGE_LAST: 5, PAIR: 6, CONV: 5}[kind]
            CHAIN = {GCN: 2, SAGE_LAST: 3, PAIR: 4, CONV: 3, SAGE: 0}[kind]
            BLOCKS = DB if kind in (GCN, CONV) else 2 * DB
            normed = kind != SAGE

            def real(i, k):
                return not isinstance(i, int) or 0 <= U * i + k < T

            with phase(nc, *[f"{name}_{n}" for n in ("staged", "coef_made", "selected", "summed", "part_done",
                                                     "total_done", "scaled", "turned", "copied", "product", "product_read",
                                                     "chained", "measured", "rooted", "inverted", "ready", "activated", "leaked",
                                                     "rows_done")],
                       *[f"{name}_x_in{k}" for k in range(4)],
                       *[f"{name}_extra_in{k}" for k in range(U)], *[f"{name}_rows_out{k}" for k in range(4)]) as (
                    block, (staged, coef_made, selected, summed, part_done, total_done, scaled, turned, copied, product,
                            product_read, chained, measured, rooted, inverted, ready, activated, leaked,
                            rows_done, *dmas)):
                x_in, extra_in, rows_out = dmas[0:4], dmas[4:U + 4], dmas[U + 4:]
                sum_read = part_done if kind in (GCN, PAIR) else total_done
                X_LOADS = 2 if residual is not None else 1

                @block.gpsimd
                def _(pool):
                    sweep(pool, T, 0, lambda i, k: gather(pool, i, k, base, staged, summed), 0)

                @block.sync
                def _(sp):
                    def step(i, k):
                        t, g, r = U * i + k, 4 * i + k // 2, k // 2
                        if k % 2 == 0:
                            need(sp, rows_done, t - 6)
                            sp.dma_start(xb[:, r, :, 0:width], pairs[g]).then_inc(x_in[r], 16)
                            if residual is not None:
                                sp.dma_start(rb[:, r], residual.rearrange("(g k p) d -> g p k d", k=2, p=P)[g]).then_inc(
                                    x_in[r], 16)
                        at = sp.value_load(plan.sums_at[0:1, bass.ds(t, 1)], min_val=0, max_val=XB)
                        need(sp, total_done, t - U + 1)
                        sp.dma_start(extra[:, k], overflow_sums[bass.ds(at, 1)].rearrange("a p d -> p (a d)")).then_inc(
                            extra_in[k], 16)
                    sweep(sp, T, 0, step, 0)

                @block.tensor
                def _(pe):
                    def turn(i, k):
                        if not real(i, k):
                            return
                        t, r, q = U * i + k, k % 4, k % 2
                        pe.wait_ge(total_done, t + 1)
                        if kind in (SAGE, SAGE_LAST):
                            pe.wait_ge(x_in[k // 2], 16 * X_LOADS * (i + 1))
                            pe.wait_ge(scaled, t + 1)
                            left = [xb[:, k // 2, k % 2], mixed[:, r, 0]]
                        else:
                            left = {GCN: [mixed[:, r, 0]], PAIR: [mixed[:, r, 0], mixed[:, r, 1]],
                                    CONV: [total_b[:, r]]}[kind]
                        need(pe, copied, t - 1)
                        for j, a in enumerate(left):
                            for b in range(DB):
                                n = DB * j + b
                                last = pe.transpose(psT[:, q, n * P:n * P + P], a[:, b * P:b * P + P], ident[:])
                        last.then_inc(turned, 1)

                    def multiply_w(i, k):
                        if not real(i, k):
                            return
                        t, q = U * i + k, k % 2
                        pe.wait_ge(copied, t + 1)
                        if kind == PAIR:
                            need(pe, product_read, t - 1)
                        elif kind == SAGE:
                            need(pe, ready, t - 1)
                        else:
                            need(pe, chained, CHAIN * (t - 2) + 1)
                        for n in range(BLOCKS):
                            w = w_gcn[:, n] if kind == GCN else wb[:, n]
                            last = pe.matmul(psO[:, q, 0:D], turned_b[:, q, n], w, start=n == 0, stop=n == BLOCKS - 1)
                        last.then_inc(product, 1)

                    def step(i, k):
                        if real(i, k):
                            multiply(pe, i, k, base, selected, sum_read, summed)
                        turn(*tile_at(i, k - 1))
                        multiply_w(*tile_at(i, k - 2))
                    sweep(pe, T, 0, lambda i, k: step(*tile_at(i, k)), 2)

                @block.vector
                def _(dve):
                    def add(i, k):
                        if not real(i, k):
                            return
                        t, r = U * i + k, k % 4
                        x_t = xb[:, k // 2, k % 2, 0:D]
                        dve.wait_ge(summed, t + 1)
                        need(dve, turned, t - 3)
                        if kind == GCN:
                            dve.wait_ge(x_in[k // 2], 16 * X_LOADS * (i + 1))
                            dve.scalar_tensor_tensor(total_b[:, r], x_t, dinv[:, bass.ds(t, 1)], psA[:, k % 2, 0:D],
                                                     ALU.mult, ALU.add).then_inc(part_done, 1)
                            dve.wait_ge(extra_in[k], 16 * (i + 1))
                            dve.wait_ge(part_done, t + 1)
                            dve.tensor_tensor(mixed[:, r, 0], total_b[:, r], extra[:, k], ALU.add).then_inc(total_done, 1)
                            return
                        dve.wait_ge(extra_in[k], 16 * (i + 1))
                        dve.tensor_tensor(total_b[:, r], psA[:, k % 2, 0:D], extra[:, k], ALU.add).then_inc(sum_read, 1)
                        if kind == PAIR:
                            root_t = root_out[:, bass.ds(t, 1)]
                            dve.wait_ge(part_done, t + 1)
                            dve.wait_ge(x_in[k // 2], 16 * X_LOADS * (i + 1))
                            dve.scalar_tensor_tensor(mixed[:, r, 0], total_b[:, r], root_t, x_t, ALU.mult, ALU.add)
                            dve.scalar_tensor_tensor(mixed[:, r, 1], total_b[:, r], root_t, x_t, ALU.mult,
                                                     ALU.mult).then_inc(total_done, 1)

                    def measure(v, i, k, done):
                        t = U * i + k
                        dve.wait_ge(chained, CHAIN * t + done)
                        dve.bn_stats(stats[:, k % 4], v).then_inc(chained, 1)

                    def scale(i, k):
                        if not real(i, k):
                            return
                        t, r = U * i + k, k % 4
                        dve.wait_ge(rooted, t + 1)
                        dve.reciprocal(rstd[:, r:r + 1], root[:, r:r + 1]).then_inc(inverted, 1)
                        dve.wait_ge(inverted, t + 1)
                        dve.scalar_tensor_tensor(shift[:, r:r + 1], mean_var[:, r, 0:1], -1.0, rstd[:, r:r + 1], ALU.mult,
                                                 ALU.mult).then_inc(ready, 1)

                    def finish(i, k):
                        if not real(i, k):
                            return
                        t, q, r = U * i + k, k % 2, k % 4
                        x_t = xb[:, k // 2, k % 2, 0:D]
                        dve.wait_ge(product, t + 1)
                        if kind != PAIR:
                            need(dve, rows_done, t - 3)
                        if kind == GCN:
                            dve.scalar_tensor_tensor(u_b[:, r], psO[:, q, 0:D], dinv[:, bass.ds(t, 1)], x_t, ALU.mult,
                                                     ALU.add).then_inc(chained, 1)
                            measure(u_b[:, r], i, k, 1)
                        elif kind == SAGE:
                            dve.tensor_tensor(u_b[:, r], psO[:, q, 0:D], bias, ALU.add).then_inc(ready, 1)
                        elif kind == PAIR:
                            dve.scalar_tensor_tensor(u_b[:, r], psO[:, q, 0:D], has_in[:, bass.ds(t, 1)], bias, ALU.mult,
                                                     ALU.add).then_inc(product_read, 1)
                            dve.wait_ge(product_read, t + 1)
                            need(dve, activated, t - 1)
                            dve.scalar_tensor_tensor(act_b[:, q], u_b[:, r], 0.01, u_b[:, r], ALU.mult,
                                                     ALU.max).then_inc(leaked, 1)
                        else:
                            dve.tensor_tensor(v_b[:, r], psO[:, q, 0:D], bias, ALU.add).then_inc(chained, 1)
                            dve.wait_ge(chained, CHAIN * t + 1)
                            other = rb[:, k // 2, k % 2] if residual is not None else x_t
                            dve.tensor_tensor(u_b[:, r], v_b[:, r], other, ALU.add).then_inc(chained, 1)
                            measure(u_b[:, r], i, k, 2)

                    def finish_pair(i, k):
                        if not real(i, k) or kind != PAIR:
                            return
                        t, q, r = U * i + k, k % 2, k % 4
                        x_t = xb[:, k // 2, k % 2, 0:D]
                        dve.wait_ge(activated, t + 1)
                        need(dve, rows_done, t - 3)
                        dve.tensor_scalar(inv_norm[:, q:q + 1], length[:, q:q + 1], 1e-12, None,
                                          ALU.max).then_inc(chained, 1)
                        dve.wait_ge(chained, CHAIN * t + 1)
                        dve.reciprocal(inv_norm[:, q:q + 1], inv_norm[:, q:q + 1]).then_inc(chained, 1)
                        dve.wait_ge(chained, CHAIN * t + 2)
                        dve.scalar_tensor_tensor(v_b[:, r], act_b[:, q], inv_norm[:, q:q + 1], x_t, ALU.mult,
                                                 ALU.add).then_inc(chained, 1)
                        measure(v_b[:, r], i, k, 3)

                    def step(i, k):
                        a = tile_at(i, k)
                        if real(*a):
                            add(*a)
                        b = tile_at(i, k + 2)
                        m, mk = tile_at(i, k - LAG + 1)
                        measures = normed and real(m, mk)
                        if measures:
                            dve.wait_ge(chained, CHAIN * (U * m + mk + 1))
                        if real(*b):
                            choose(dve, *b, base, coef_made, selected, summed)
                        if measures:
                            dve.bn_aggr(mean_var[:, mk % 4], stats[:, mk % 4]).then_inc(measured, 1)
                        if normed:
                            scale(*tile_at(i, k - LAG))
                        finish(*tile_at(i, k - 3))
                        finish_pair(*tile_at(i, k - 4))
                    sweep(dve, T, 2, step, LAG)

                @block.scalar
                def _(act):
                    def store(i, k):
                        g, r = 4 * i + k // 2, k // 2
                        act.wait_ge(rows_done, U * i + k + 1)
                        if final and isinstance(g, int) and g == WHOLE_PAIRS:
                            act.dma_start(out[N - REST:N, :], ob[0:REST, r, 0, 0:D]).then_inc(rows_out[r], 16)
                        else:
                            act.dma_start(out_pairs[g], ob[:, r, :, 0:out_width]).then_inc(rows_out[r], 16)

                    def finish(i, k):
                        if not real(i, k):
                            return
                        t, q, r, s = U * i + k, k % 2, k // 2, k % 4
                        need(act, rows_out[r], 16 * i)
                        act.wait_ge(ready, t + 1)
                        if out_width == ROW:
                            act.copy(ob[:, r, q, D:ROW], root_out[:, bass.ds(t, 1)])
                        if normed:
                            act.activation(ob[:, r, q, 0:D], (v_b if kind == PAIR else u_b)[:, s], ACT.Identity,
                                           bias=shift[:, s:s + 1], scale=rstd[:, s:s + 1]).then_inc(rows_done, 1)
                        else:
                            act.activation(ob[:, r, q, 0:D], u_b[:, s], ACT.Relu).then_inc(rows_done, 1)
                        if k % 2:
                            store(i, k)

                    def step(i, k):
                        b = tile_at(i, k + 2)
                        if kind == GCN and real(*b):
                            coefficient(act, *b, base, coef_made, selected)
                        a = tile_at(i, k)
                        if kind in (SAGE, SAGE_LAST) and real(*a):
                            t, r = U * a[0] + a[1], a[1] % 4
                            act.wait_ge(total_done, t + 1)
                            need(act, turned, t - 3)
                            act.activation(mixed[:, r, 0], total_b[:, r], ACT.Copy,
                                           scale=inv_deg[:, bass.ds(t, 1)]).then_inc(scaled, 1)
                        a = tile_at(i, k - 1)
                        if real(*a):
                            t, q = U * a[0] + a[1], a[1] % 2
                            act.wait_ge(turned, t + 1)
                            need(act, product, t - 1)
                            act.copy(turned_b[:, q, 0:BLOCKS].rearrange("p b n -> p (b n)"),
                                     psT[:, q, 0:BLOCKS * P]).then_inc(copied, 1)
                        a = tile_at(i, k - 3)
                        if kind == PAIR and real(*a):
                            t, q = U * a[0] + a[1], a[1] % 2
                            act.wait_ge(leaked, t + 1)
                            act.activation(squares[:], act_b[:, q], ACT.Square,
                                           accum_out=sq_sum[:, q:q + 1]).then_inc(scaled, 1)
                            act.wait_ge(scaled, t + 1)
                            act.activation(length[:, q:q + 1], sq_sum[:, q:q + 1], ACT.Sqrt,
                                           bias=tiny_col[:, 0:1]).then_inc(activated, 1)
                        finish(*tile_at(i, k - LAG))
                        a = tile_at(i, k - LAG + 1)
                        if normed and real(*a):
                            t, s = U * a[0] + a[1], a[1] % 4
                            act.wait_ge(measured, t + 1)
                            act.activation(root[:, s:s + 1], mean_var[:, s, 1:2], ACT.Sqrt,
                                           bias=eps_col[:, 0:1]).then_inc(rooted, 1)
                    sweep(act, T, 2, step, LAG, peeled=2)
                    for r in range(4):
                        act.wait_ge(rows_out[r], 16 * (T // U))

        def layer(name, kind, table, weights, bias, residual, target, plan=by_dst):
            width = table.shape[1]
            overflow_sweep("x_" + name, kind, width, table, weights, plan)
            tile_sweep(name, kind, width, table, weights, bias, residual, target, plan)
            before_now[:] = [n + T // U for n in before_now]
            plan.sweeps += 1

        layer("gcn", GCN, table0, [], None, None, table1)
        layer("sage0", SAGE, table1, [W_self[0], W_neigh[0]], bsage_row[:, 0], None, table1a)
        layer("sage1", SAGE, table1a, [W_self[1], W_neigh[1]], bsage_row[:, 1], None, table1b)
        layer("sage2", SAGE_LAST, table1b, [W_self[2], W_neigh[2]], bsage_row[:, 2], table1, table2)
        layer("pair", PAIR, table2, [W_one, W_two], bpair_row[:], None, table3)
        layer("conv", CONV, table3, [W_conv], bconv_row[:], None, None, by_src)


_INS = ["x", "src", "dst", "edge_weight", "L0_gnn_p", "L0_gnn_W_ih", "L0_gnn_W_hh", "L0_gnn_b_ih", "L0_gnn_b_hh",
        "L0_gnn_W0", "L1_gnn_W_self", "L1_gnn_W_neigh", "L1_gnn_bias", "L2_gnn_W1", "L2_gnn_W2", "L2_gnn_b",
        "L3_gnn_weight", "L3_gnn_bias"]


def kernel(**inputs):
    import numpy as _np
    import concourse.bacc as _bacc
    from concourse import mybir as _mybir
    from concourse.bass_utils import run_bass_kernel_spmd as _run

    nc = _bacc.Bacc("TRN2", target_bir_lowering=False, num_devices=1)
    arrays, args = {}, []
    for name in _INS:
        a = _np.ascontiguousarray(inputs[name])
        arrays[f"in_{name}_dram"] = a
        args.append(nc.dram_tensor(f"in_{name}_dram", a.shape, _mybir.dt.from_np(a.dtype), kind="ExternalInput").ap())
    shape = tuple(inputs["x"].shape)
    result = nc.dram_tensor("out_0_dram", shape, _mybir.dt.float32, kind="ExternalOutput").ap()
    graph_stack(nc, *args, result)
    r = _run(nc, [arrays], core_ids=[0])
    return r.results[0]["out_0_dram"]
```

```python
from contextlib import ExitStack, contextmanager

import concourse.bass as bass
from concourse import mybir

F32 = mybir.dt.float32
BF16 = mybir.dt.bfloat16
FP16 = mybir.dt.float16
I32 = mybir.dt.int32
ALU = mybir.AluOpType
ACT = mybir.ActivationFunctionType
AX = mybir.AxisListType

P = 128
D = 256
DB = D // P
K = D
U = 8
XU = 8
EPS = 1e-5


class Plan:

    def __init__(self, sb, dram, sem, name, T, TW, rows):
        self.name = name
        self.overflow = sb(f"{name}_overflow", [P, TW])
        self.upto = sb(f"{name}_upto", [P, TW])
        self.first = sb(f"{name}_first", [P, TW])
        self.base = sb(f"{name}_base", [P, TW])
        self.sums_at = sb(f"{name}_sums_at", [P, T], I32)
        self.x_last = sb(f"{name}_x_last", [P, 1], I32)
        self.carry = sb(f"{name}_carry", [P, TW])
        self.main, self.extra = [(sb(f"{name}_{h}_from", [P, TW], I32),
                                  sb(f"{name}_{h}_to", [P, TW]),
                                  sb(f"{name}_{h}_weight", [P, TW]))
                                 for h in ("main", "extra")]
        self.tables = [dram(f"{name}_table{k}", [rows, 4]) for k in range(U)]
        self.gathered = [sem(f"{name}_gathered{k}") for k in range(U)]
        self.sweeps = 0


@contextmanager
def phase(nc, *names):
    with ExitStack() as held:
        sems = [held.enter_context(nc.semaphore(n)) for n in names]
        with nc.Block() as block:
            yield block, sems
        nums = [s.num for s in sems]
        assert set(range(min(nums), max(nums) + 1)) <= set(nums) | set(nc.free_semaphores)
        nc.all_engine_barrier(sems_to_clear=range(min(nums), max(nums) + 1))


def need(eng, sem, value):
    if not isinstance(value, int) or value > 0:
        eng.wait_ge(sem, value)


def slot_freed(eng, sem, i, base):
    if not (isinstance(i, int) and i == 0):
        eng.wait_ge(sem, 16 * (i + base))


def tile_at(i, k):
    return i + k // U, k % U


def sweep(eng, tiles, lead, step, lag, peeled=1):
    n = tiles // U
    for k in range(-lead, U * peeled):
        step(*((0, k) if k < 0 else divmod(k, U)))
    if n > peeled + 1:
        with eng.Fori(peeled, n - 1) as i:
            for k in range(U):
                step(i, k)
    for k in range(U + lag):
        step(n - 1, k)


def graph_stack(nc, x, src, dst, edge_weight, p, W_ih, W_hh, b_ih, b_hh, W0, W_self, W_neigh, b_sage,
                W_one, W_two, b_pair, W_conv, b_conv, out):
    N, E = x.shape[0], src.shape[0]
    assert x.shape[1] == D
    T = -(-max(N, E) // (P * U)) * U
    C = T
    REAL = N // P
    REST = N - REAL * P
    assert T // U >= 4 and T == REAL + 2 and REAL % 2 == 0 and REST
    XB = -(-(E // P + 1) // XU) * XU + 2 * XU
    TB = -(-max(T, XB, K) // P)
    TW = TB * P
    SLOTS = 2 * TW + 2
    TRASH = SLOTS * P
    ROW = D + 1

    ctx = ExitStack()
    with ctx:
        def sb(name, shape, dt=F32):
            return ctx.enter_context(nc.sbuf_tensor(name, shape, dt))

        def dram(name, shape, dt=F32):
            return nc.dram_tensor(name, shape, dt, kind="Internal").ap()

        table0 = dram("table0", [T * P, ROW])
        table1 = dram("table1", [T * P, D])
        table1a = dram("table1a", [T * P, D])
        table1b = dram("table1b", [T * P, D])
        table2 = dram("table2", [T * P, ROW])
        table3 = dram("table3", [T * P, D])
        overflow_sums = dram("overflow_sums", [XB + 1, P, D])

        gathered_m = [ctx.enter_context(nc.semaphore(f"gathered{k}")) for k in range(U)]
        before_now = [0] * U

        psA = ctx.enter_context(nc.psum_tensor("psA", [P, 2, 512], F32))
        psT = ctx.enter_context(nc.psum_tensor("psT", [P, 2, 512], F32))
        psO = ctx.enter_context(nc.psum_tensor("psO", [P, 2, 512], F32))
        psM = ctx.enter_context(nc.psum_tensor("psM", [P, 2, 512], F32))

        sum_ps = [psA[:, s, 0:D] for s in range(2)]
        turned_ps = [psT[:, s] for s in range(2)]
        product_ps = [ps[:, s] for ps in (psO, psM) for s in range(2)]

        iota_i = sb("iota_i", [P, TW], I32)
        pcol_i = sb("pcol_i", [P, 1], I32)
        iota_f = sb("iota_f", [P, TW])
        iota_h = sb("iota_h", [P, TW], FP16)
        pcol = sb("pcol", [P, 1])
        ident = sb("ident", [P, P])
        ones_f = sb("ones_f", [P, P])
        ones_row = sb("ones_row", [P, TW])
        eps_col = sb("eps_col", [P, 1])
        tiny_col = sb("tiny_col", [P, 1])
        ones_b = sb("ones_b", [P, P], BF16)
        before = sb("before", [P, P], BF16)
        not_before = sb("not_before", [P, P], BF16)
        zeros = sb("zeros", [P, D])
        p_row = sb("p_row", [P, D])
        bsage_row = sb("bsage_row", [P, 3, D])
        bpair_row = sb("bpair_row", [P, D])
        bconv_row = sb("bconv_row", [P, D])
        dinv = sb("dinv", [P, T])
        inv_deg = sb("inv_deg", [P, T])
        has_in = sb("has_in", [P, T])
        root_out = sb("root_out", [P, T])
        score = sb("score", [P, T])
        def sem(name):
            return ctx.enter_context(nc.semaphore(name))

        by_dst, by_src = [Plan(sb, dram, sem, name, T, TW, TRASH + P) for name in ("by_dst", "by_src")]
        w_gcn = sb("w_gcn", [P, 2, D])

        pool_waits = sb("pool_waits", [P, 5])

        def take_waits(pool, at=0):
            pool.tensor_tensor(pool_waits[0:1, at:at + 1], pool_waits[0:1, 1:2], pool_waits[0:1, 2:3], ALU.add)

        early = ExitStack()

        def tmp(name, shape, dt=F32):
            return early.enter_context(nc.sbuf_tensor(name, shape, dt))

        src_i = tmp("src_i", [P, C], I32)
        dst_i = tmp("dst_i", [P, C], I32)
        w_f = tmp("w_f", [P, C])
        fields = {plan: tmp(f"{plan.name}_fields", [P, C, 4]) for plan in (by_dst, by_src)}
        dst_hi = tmp("dst_hi", [P, C])
        dst_lo = tmp("dst_lo", [P, C])
        src_hi = tmp("src_hi", [P, C])
        src_lo = tmp("src_lo", [P, C])
        w_part = tmp("w_part", [P, 3, C])
        w_half = tmp("w_half", [P, C], BF16)
        w_rest = tmp("w_rest", [P, C])
        pad_at = tmp("pad_at", [P, C])
        cut_i = tmp("cut_i", [P, C], I32)
        table_fill = tmp("table_fill", [P, 2 * P, 4])

        full, rest = E // C, E % C
        with phase(nc, "pads_set", "iotas_made", "edges_in", "rows_in", "fill_set", "dve_done") as (
                block, (pads_set, iotas_made, edges_in, rows_in, fill_set, dve_done)):
            @block.gpsimd
            def _(pool):
                pool.iota(iota_i[:], [[1, TW]], base=0, channel_multiplier=0)
                pool.iota(pcol_i[:], [[0, 1]], base=0, channel_multiplier=1).then_inc(iotas_made, 1)

            @block.sync
            def _(sp):
                sp.wait_ge(pads_set, 1)
                for to, what in ((src_i, src), (dst_i, dst), (w_f, edge_weight)):
                    sp.dma_start(to[0:full, :], what[0:full * C].rearrange("(a c) -> a c", c=C)).then_inc(edges_in, 16)
                    if rest:
                        sp.dma_start(to[full:full + 1, 0:rest],
                                     what[full * C:E].rearrange("(a c) -> a c", a=1)).then_inc(edges_in, 16)
                for to, what in ((p_row[:], p), (bpair_row[:], b_pair), (bconv_row[:], b_conv),
                                 (bsage_row[:, 0], b_sage[0]), (bsage_row[:, 1], b_sage[1]),
                                 (bsage_row[:, 2], b_sage[2])):
                    sp.dma_start(to, what.rearrange("(a d) -> a d", a=1).to_broadcast([P, D])).then_inc(rows_in, 16)
                sp.wait_ge(fill_set, 1)
                sp.wait_ge(rows_in, 16 * 6)

            @block.vector
            def _(dve):
                steps = [0]

                def link(ins):
                    steps[0] += 1
                    ins.then_inc(dve_done, 1)
                    dve.wait_ge(dve_done, steps[0])

                dve.memset(pool_waits[:], 0.0)
                dve.memset(src_i[:], -1)
                dve.memset(dst_i[:], -1)
                dve.memset(w_f[:], 0.0).then_inc(pads_set, 1)
                dve.memset(zeros[:], 0.0)
                dve.memset(table_fill[:], 0.0).then_inc(fill_set, 1)
                dve.memset(ones_f[:], 1.0)
                dve.memset(ones_row[:], 1.0)
                dve.memset(eps_col[:], EPS)
                dve.memset(tiny_col[:], 1e-34)
                dve.memset(ones_b[:], 1.0)
                for f in fields.values():
                    dve.memset(f[:], 0.0)
                dve.wait_ge(iotas_made, 1)
                dve.tensor_copy(iota_f[:], iota_i[:])
                dve.tensor_copy(iota_h[:], iota_i[:])
                link(dve.tensor_copy(pcol[:], pcol_i[:]))
                dve.tensor_scalar(ident[:], iota_f[:, 0:P], pcol[:, 0:1], None, ALU.is_equal)
                dve.tensor_scalar(before[:], iota_f[:, 0:P], pcol[:, 0:1], None, ALU.is_gt)
                dve.tensor_scalar(not_before[:], iota_f[:, 0:P], pcol[:, 0:1], None, ALU.is_le)
                dve.wait_ge(edges_in, 16 * 3 * (1 + (rest > 0)))
                for to_hi, to_lo, what in ((dst_hi, dst_lo, dst_i), (src_hi, src_lo, src_i)):
                    link(dve.tensor_scalar(cut_i[:], what[:], 7, None, ALU.arith_shift_right))
                    link(dve.tensor_copy(to_hi[:], cut_i[:]))
                    link(dve.tensor_scalar(cut_i[:], what[:], P - 1, None, ALU.bitwise_and))
                    link(dve.tensor_copy(to_lo[:], cut_i[:]))
                for plan, taken, lo in ((by_dst, src_i, dst_lo), (by_src, dst_i, src_lo)):
                    dve.tensor_copy(fields[plan][:, :, 0], taken[:])
                    dve.tensor_scalar(fields[plan][:, :, 1], lo[:], 1.0, None, ALU.add)
                    dve.tensor_copy(fields[plan][:, :, 2], w_f[:])
                link(dve.tensor_copy(w_half[:], w_f[:]))
                link(dve.tensor_copy(w_part[:, 0], w_half[:]))
                link(dve.tensor_tensor(w_rest[:], w_f[:], w_part[:, 0], ALU.subtract))
                link(dve.tensor_copy(w_half[:], w_rest[:]))
                link(dve.tensor_copy(w_part[:, 1], w_half[:]))
                link(dve.tensor_tensor(w_part[:, 2], w_rest[:], w_part[:, 1], ALU.subtract))
                link(dve.tensor_scalar(w_rest[:], dst_hi[:], 0.0, None, ALU.is_lt))
                link(dve.tensor_scalar(pad_at[:], w_rest[:], pcol[:, 0:1], None, ALU.mult))
                dve.scalar_tensor_tensor(pad_at[:], w_rest[:], float(TRASH), pad_at[:], ALU.mult, ALU.add)

        RING = 8
        oh_dst = tmp("oh_dst", [P, RING, T], BF16)
        oh_src = tmp("oh_src", [P, RING, T], BF16)
        lo_dst = tmp("lo_dst", [P, RING, P], BF16)
        lo_src = tmp("lo_src", [P, RING, P], BF16)
        lo_w = tmp("lo_w", [P, RING, 3, P], BF16)
        in_count, in_weight, out_count = psA[:, 0, 0:T], psA[:, 1, 0:T], psT[:, 0, 0:T]
        with phase(nc, "onehots", "weighted", "counted", "fill_out") as (block, (onehots, weighted, counted, fill_out)):
            @block.sync
            def _(sp):
                rows = (TRASH + P) // P
                n = 0
                for edge_table in by_dst.tables + by_src.tables:
                    fills = edge_table.rearrange("(a r) f -> a r f", a=P)
                    for r in range(0, rows, 2 * P):
                        m = min(2 * P, rows - r)
                        sp.dma_start(fills[:, r:r + m, :], table_fill[:, 0:m, :]).then_inc(fill_out, 16)
                        n += 16
                sp.dma_start(overflow_sums[XB], zeros[:]).then_inc(fill_out, 16)
                sp.wait_ge(fill_out, n + 16)

            @block.vector
            def _(dve):
                def step(i, k):
                    c, r = U * i + k, k % RING
                    need(dve, counted, c - RING + 1)
                    dve.tensor_scalar(lo_dst[:, r], iota_h[:, 0:P], dst_lo[:, bass.ds(c, 1)], None,
                                      ALU.is_equal).then_inc(onehots, 1)
                    dve.tensor_scalar(oh_dst[:, r], iota_h[:, 0:T], dst_hi[:, bass.ds(c, 1)], None, ALU.is_equal)
                    dve.tensor_scalar(oh_src[:, r], iota_h[:, 0:T], src_hi[:, bass.ds(c, 1)], None, ALU.is_equal)
                    dve.tensor_scalar(lo_src[:, r], iota_h[:, 0:P], src_lo[:, bass.ds(c, 1)], None,
                                      ALU.is_equal).then_inc(onehots, 1)
                sweep(dve, C, 0, step, 0)

            @block.scalar
            def _(act):
                def step(i, k):
                    c, r = U * i + k, k % RING
                    act.wait_ge(onehots, 2 * c + 1)
                    need(act, counted, c - RING + 1)
                    for j in range(3):
                        last = act.activation(lo_w[:, r, j], lo_dst[:, r], ACT.Copy,
                                              scale=w_part[:, j, bass.ds(c, 1)])
                    last.then_inc(weighted, 1)
                sweep(act, C, 0, step, 0)

            @block.tensor
            def _(pe):
                def step(i, k):
                    c, r = U * i + k, k % RING
                    at_start = isinstance(i, int) and i == 0 and k == 0
                    at_end = isinstance(i, int) and i == C // U - 1 and k == U - 1
                    pe.wait_ge(onehots, 2 * c + 2)
                    pe.matmul(in_count, lo_dst[:, r], oh_dst[:, r], start=at_start, stop=at_end)
                    pe.matmul(out_count, lo_src[:, r], oh_src[:, r], start=at_start, stop=at_end)
                    pe.wait_ge(weighted, c + 1)
                    for j in range(3):
                        last = pe.matmul(in_weight, lo_w[:, r, j], oh_dst[:, r], start=at_start and j == 0,
                                         stop=at_end and j == 2)
                    last.then_inc(counted, 1)
                sweep(pe, C, 0, step, 0)

        in_sb = tmp("in_sb", [P, T])
        out_sb = tmp("out_sb", [P, T])
        deg = tmp("deg", [P, T])
        row_i = tmp("row_i", [P, T], I32)
        seed = tmp("seed", [P, T])
        ranks = [psO[:, 0, 0:T], psO[:, 1, 0:T]]
        with phase(nc, "degrees", "rooted", "dve_done") as (block, (degrees, rooted, dve_done)):
            @block.scalar
            def _(act):
                act.wait_ge(degrees, 1)
                act.activation(dinv[:], dinv[:], ACT.Sqrt)
                act.activation(root_out[:], root_out[:], ACT.Sqrt).then_inc(rooted, 1)

            @block.vector
            def _(dve):
                steps = [0]

                def link(ins):
                    steps[0] += 1
                    ins.then_inc(dve_done, 1)
                    dve.wait_ge(dve_done, steps[0])

                dve.tensor_copy(in_sb[:], in_count)
                link(dve.tensor_copy(out_sb[:], out_count))
                for plan in (by_dst, by_src):
                    for a in (plan.overflow, plan.upto, plan.first, plan.base):
                        dve.memset(a[:], 0.0)
                link(dve.tensor_scalar(deg[:], in_weight, 1.0, None, ALU.add))
                dve.tensor_scalar(dinv[:], deg[:], 1e-30, None, ALU.max)
                dve.tensor_scalar(root_out[:], out_sb[:], 1.0, None, ALU.max).then_inc(degrees, 1)
                dve.wait_ge(rooted, 1)
                link(dve.tensor_scalar(deg[:], deg[:], 0.0, None, ALU.is_gt))
                link(dve.reciprocal(dinv[:], dinv[:]))
                dve.reciprocal(root_out[:], root_out[:])
                link(dve.tensor_tensor(dinv[:], dinv[:], deg[:], ALU.mult))
                dve.tensor_scalar(has_in[:], in_sb[:], 0.0, None, ALU.is_gt)
                link(dve.tensor_scalar(inv_deg[:], in_sb[:], 1.0, None, ALU.max))
                link(dve.reciprocal(inv_deg[:], inv_deg[:]))
                dve.tensor_tensor(inv_deg[:], inv_deg[:], has_in[:], ALU.mult)

        def place_tiles(plan, counts):
            with phase(nc, "totals", "seed_made", "dve_done") as (block, (totals, seed_made, dve_done)):
                @block.tensor
                def _(pe):
                    pe.matmul(psM[:, 0, 0:T], ones_f[:], counts[:], start=True, stop=True).then_inc(totals, 1)
                    pe.wait_ge(seed_made, 1)
                    for rank in ranks:
                        pe.matmul(rank, ones_f[0:1, :], seed[0:1, :], start=True, stop=True)

                @block.vector
                def _(dve):
                    steps = [0]

                    def link(ins):
                        steps[0] += 1
                        ins.then_inc(dve_done, 1)
                        dve.wait_ge(dve_done, steps[0])

                    overflow, upto, first, base = [a[:, 0:T] for a in (plan.overflow, plan.upto, plan.first, plan.base)]
                    dve.wait_ge(totals, 1)
                    link(dve.tensor_scalar(row_i[:], psM[:, 0, 0:T], 1.0, -1.0, ALU.max, ALU.add))
                    link(dve.tensor_scalar(row_i[:], row_i[:], 7, None, ALU.arith_shift_right))
                    link(dve.tensor_copy(overflow, row_i[:]))
                    link(dve.tensor_tensor_scan(upto, ones_row[:, 0:T], overflow, 0.0, ALU.mult, ALU.add))
                    link(dve.tensor_tensor(first, upto, overflow, ALU.subtract))
                    link(dve.tensor_tensor(base, first, iota_f[:, 0:T], ALU.add))
                    dve.tensor_scalar(seed[:], base, float(P), None, ALU.mult).then_inc(seed_made, 1)
                    link(dve.tensor_scalar(deg[:], overflow, 0.0, None, ALU.is_gt))
                    link(dve.scalar_tensor_tensor(deg[:], upto, -1.0 - XB, deg[:], ALU.add, ALU.mult))
                    dve.tensor_scalar(plan.sums_at[:], deg[:], float(XB), None, ALU.add)
                    link(dve.tensor_scalar(row_i[:, 0:1], plan.upto[:, T - 1:T], -1.0, 2.0 * XU, ALU.add, ALU.max))
                    assert XU == 8
                    dve.tensor_scalar(plan.x_last[:], row_i[:, 0:1], 3, None, ALU.arith_shift_right)

        rank8 = tmp("rank8", [P, U])
        junk_t = tmp("junk_t", [P, T])
        row_at = tmp("row_at", [P, U], I32)
        staged = tmp("staged", [P, U, 4])
        xin = tmp("xin", [P, 4, 2, ROW])
        junk_d = tmp("junk_d", [P, D])
        score8 = tmp("score8", [P, 2, 4])
        x_pairs = x[0:(N // (2 * P)) * 2 * P, :].rearrange("(g k p) d -> g p k d", k=2, p=P)
        t0_pairs = table0.rearrange("(g k p) d -> g p k d", k=2, p=P)
        WHOLE_PAIRS = N // (2 * P)

        def place_edges(plan, key_hi, with_scores, uses):
            with phase(nc, f"{plan.name}_onehot", "rank_ready", "rank_read", "places", "fields_staged", "dots", "dots_kept", "pad_zero",
                       *[f"x_in{k}" for k in range(4)],
                       *[f"t0_out{k}" for k in range(4)], "coef_set", "ones_used") as (
                    block, (onehot, rank_ready, rank_read, places, fields_staged, dots, dots_kept, pad_zero, *dmas)):
                x_in, t0_out, coef_set, ones_used = dmas[0:4], dmas[4:8], dmas[8], dmas[9]

                @block.tensor
                def _(pe):
                    def step(i, k):
                        c, r, mine, other = U * i + k, k % RING, ranks[k % 2], ranks[(k + 1) % 2]
                        pe.wait_ge(onehot, c + 1)
                        pe.matmul(mine, before[:], oh_dst[:, r], start=False, stop=True,
                                  skip_group_check=True).then_inc(rank_ready, 1)
                        need(pe, rank_read, c)
                        if not (isinstance(c, int) and c == 0):
                            pe.matmul(other, not_before[:], oh_dst[:, (k - 1) % RING], start=False, stop=True,
                                      skip_group_check=True)
                        pe.matmul(other, ones_b[:], oh_dst[:, r], start=False, stop=True,
                                  skip_group_check=True).then_inc(ones_used, 1)
                    sweep(pe, C, 0, step, 0)

                @block.vector
                def _(dve):
                    def set_onehot(i, k):
                        c = U * i + k
                        if isinstance(c, int) and c >= C:
                            return
                        need(dve, ones_used, c - RING + 2)
                        dve.tensor_scalar(oh_dst[:, k % RING], iota_h[:, 0:T], key_hi[:, bass.ds(c, 1)], None,
                                          ALU.is_equal).then_inc(onehot, 1)

                    def step(i, k):
                        set_onehot(*tile_at(i, k + 3))
                        if k < 0:
                            return
                        c, r = U * i + k, k % RING
                        h, q = k // 4, k % 4
                        if with_scores:
                            if isinstance(c, int) and c == T - U:
                                dve.wait_ge(t0_out[3], 16 * (T // U - 1))
                                dve.memset(xin[:, 3], 0.0).then_inc(pad_zero, 1)
                            dve.wait_ge(x_in[k // 2], 16 * (i + 1))
                            need(dve, dots, c)
                            dve.tensor_tensor_reduce(junk_d[:], xin[:, k // 2, k % 2, 0:D], p_row[:], 1.0, 0.0, ALU.mult,
                                                     ALU.add, score8[:, h, q:q + 1]).then_inc(dots, 1)
                            if q == 3:
                                dve.wait_ge(dots, U * i + k + 1)
                                dve.tensor_copy(score[:, bass.ds(U * i + 4 * h, 4)], score8[:, h]).then_inc(dots_kept, 1)
                        dve.wait_ge(rank_ready, c + 1)
                        dve.wait_ge(onehot, c + 1)
                        need(dve, rank_read, c)
                        dve.tensor_tensor_reduce(junk_t[:], ranks[k % 2], oh_dst[:, r], 1.0, 0.0, ALU.mult, ALU.add,
                                                 rank8[:, k:k + 1]).then_inc(rank_read, 1)
                        if q == 3:
                            for j in range(4 * h, 4 * h + 4):
                                slot_freed(dve, gathered_m[j], i, uses)
                            dve.wait_ge(rank_read, c + 1)
                            dve.tensor_tensor(row_at[:, 4 * h:4 * h + 4], rank8[:, 4 * h:4 * h + 4],
                                              pad_at[:, bass.ds(U * i + 4 * h, 4)], ALU.add).then_inc(places, 1)
                    sweep(dve, C, 3, step, 0)

                @block.gpsimd
                def _(pool):
                    def step(i, k):
                        if k % 4 == 0:
                            for j in range(k, k + 4):
                                slot_freed(pool, gathered_m[j], i, uses)
                            pool.tensor_copy(staged[:, k:k + 4, :], fields[plan][:, bass.ds(U * i + k, 4), :]).then_inc(
                                fields_staged, 1)
                            pool.wait_ge(fields_staged, 2 * i + k // 4 + 1)
                            pool.wait_ge(places, 2 * i + k // 4 + 1)
                            take_waits(pool)
                        pool.indirect_dma_start(plan.tables[k], bass.IndirectOffsetOnAxis(ap=row_at[:, k:k + 1], axis=0),
                                                staged[:, k, :], None).then_inc(gathered_m[k], 16)
                    sweep(pool, C, 0, step, 0)
                    for j in range(U):
                        pool.wait_ge(gathered_m[j], 16 * (uses + C // U))

                @block.sync
                def _(sp):
                    if not with_scores:
                        return

                    def step(i, k):
                        if k % 2:
                            return
                        g, r = 4 * i + k // 2, k // 2
                        need(sp, t0_out[r], 16 * i)
                        if isinstance(g, int) and g >= WHOLE_PAIRS:
                            if g == WHOLE_PAIRS:
                                sp.wait_ge(pad_zero, 1)
                                sp.dma_start(xin[0:REST, r, 0, 0:D], x[N - REST:N, :]).then_inc(x_in[r], 16)
                            return
                        sp.dma_start(xin[:, r, :, 0:D], x_pairs[g]).then_inc(x_in[r], 16)
                    sweep(sp, T, 0, step, 0)

                @block.scalar
                def _(act):
                    if not with_scores:
                        return

                    def step(i, k):
                        if k % 2 == 0:
                            return
                        g, r, t = 4 * i + k // 2, k // 2, U * i + k - 1
                        need(act, t0_out[r], 16 * i)
                        act.copy(xin[:, r, :, D], dinv[:, bass.ds(t, 2)]).then_inc(coef_set, 1)
                        act.wait_ge(coef_set, g + 1)
                        act.wait_ge(dots, U * i + k + 1)
                        act.dma_start(t0_pairs[g], xin[:, r]).then_inc(t0_out[r], 16)
                    sweep(act, T, 0, step, 0)
                    for r in range(4):
                        act.wait_ge(t0_out[r], 16 * (T // U))

        place_tiles(by_dst, in_sb)
        place_edges(by_dst, dst_hi, True, 0)
        place_tiles(by_src, out_sb)
        place_edges(by_src, src_hi, False, C // U)
        early.close()
        before_now = [2 * (C // U)] * U

        mid = ExitStack()

        def tmp(name, shape, dt=F32):
            return mid.enter_context(nc.sbuf_tensor(name, shape, dt))

        main_at = tmp("main_at", [P, TB], I32)
        extra_at = tmp("extra_at", [P, TB], I32)
        first_col = tmp("first_col", [P, TB])
        has_over = tmp("has_over", [P, TB, P])
        starts = tmp("starts", [P, TB, TW])
        x_num = tmp("x_num", [P, TB])
        before_x = tmp("before_x", [P, T])
        tile_of = tmp("tile_of", [P, TB])
        table_rows = tmp("table_rows", [P, 2, U, 4 * P])
        chunk_rows = tmp("chunk_rows", [P, 2, 4 * P])

        def list_chunks(plan, uses):
            edge_chunks = [e[0:SLOTS * P, :].rearrange("(v e) f -> v (e f)", e=P) for e in plan.tables]
            with phase(nc, "cols_made", "cols_read", "lists_made", "fields_made", "fields_read", "starts_made",
                       "carried", "rows_summed", "dve_done") as (
                    block, (cols_made, cols_read, lists_made, fields_made, fields_read, starts_made, carried,
                            rows_summed, dve_done)):
                jobs = [(b, half) for half in range(2) for b in range(TB)]

                @block.tensor
                def _(pe):
                    for b in range(TB):
                        at = slice(b * P, b * P + P)
                        need(pe, cols_read, b)
                        for j, row in enumerate((plan.base, plan.first, plan.overflow)):
                            last = pe.transpose(psM[:, 0, j * P:j * P + P], row[:, at], ident[:])
                        last.then_inc(cols_made, 1)
                    for b in range(TB):
                        pe.wait_ge(starts_made, b + 1)
                        last = pe.matmul(psT[:, 0, 0:TW], has_over[:, b], starts[:, b], start=b == 0, stop=b == TB - 1)
                    last.then_inc(carried, 1)
                    for n, (b, half) in enumerate(jobs):
                        pe.wait_ge(rows_summed, n + 1)
                        rows = chunk_rows[:, n % 2].rearrange("v (e f) -> v f e", f=4)
                        need(pe, fields_read, n - 1)
                        for f in range(3):
                            last = pe.transpose(psO[:, n % 2, f * P:f * P + P], rows[:, f], ident[:])
                        last.then_inc(fields_made, 1)

                @block.vector
                def _(dve):
                    steps = [0]

                    def link(ins):
                        steps[0] += 1
                        ins.then_inc(dve_done, 1)
                        dve.wait_ge(dve_done, steps[0])

                    for b in range(TB):
                        dve.wait_ge(cols_made, b + 1)
                        dve.tensor_copy(main_at[:, b:b + 1], psM[:, 0, 0:1])
                        dve.tensor_copy(first_col[:, b:b + 1], psM[:, 0, P:P + 1])
                        dve.tensor_scalar(has_over[:, b], psM[:, 0, 2 * P:3 * P], 0.0, None, ALU.is_gt).then_inc(cols_read, 1)
                    dve.wait_ge(cols_read, TB)
                    for b in range(TB):
                        link(dve.tensor_scalar(x_num[:, b:b + 1], pcol[:], float(b * P), None, ALU.add))
                        link(dve.tensor_scalar(before_x[:], plan.upto[:, 0:T], x_num[:, b:b + 1], None, ALU.is_le))
                        link(dve.tensor_reduce(tile_of[:, b:b + 1], before_x[:], AX.X, ALU.add))
                        link(dve.scalar_tensor_tensor(extra_at[:, b:b + 1], tile_of[:, b:b + 1], 1.0, x_num[:, b:b + 1],
                                                      ALU.add, ALU.add))
                    dve.tensor_scalar(x_num[:, 0:1], pcol[:], 0.0, None, ALU.add).then_inc(lists_made, 1)
                    for b in range(TB):
                        dve.tensor_scalar(starts[:, b], iota_f[:], first_col[:, b:b + 1], None, ALU.is_equal).then_inc(
                            starts_made, 1)
                    dve.wait_ge(carried, 1)
                    dve.tensor_scalar(plan.carry[:], psT[:, 0, 0:TW], -1.0, 1.0, ALU.mult, ALU.add)
                    def copy_fields(n):
                        b, half = jobs[n]
                        at = slice(b * P, b * P + P)
                        to_src, to_lo, to_w = (plan.main, plan.extra)[half]
                        dve.wait_ge(fields_made, n + 1)
                        dve.tensor_copy(to_src[:, at], psO[:, n % 2, 0:P])
                        dve.tensor_scalar(to_lo[:, at], psO[:, n % 2, P:2 * P], -1.0, None, ALU.add)
                        dve.tensor_copy(to_w[:, at], psO[:, n % 2, 2 * P:3 * P]).then_inc(fields_read, 1)

                    for n in range(len(jobs)):
                        if n >= 2:
                            copy_fields(n - 2)
                        dve.wait_ge(gathered_m[n % 2], 16 * (uses[n % 2] + U * (n // 2 + 1)))
                        dve.tensor_reduce(chunk_rows[:, n % 2], table_rows[:, n % 2].rearrange("v k x -> v x k"), AX.X,
                                          ALU.add).then_inc(rows_summed, 1)
                    for n in range(len(jobs) - 2, len(jobs)):
                        copy_fields(n)

                @block.gpsimd
                def _(pool):
                    pool.wait_ge(lists_made, 1)
                    for n, (b, half) in enumerate(jobs):
                        at = (main_at, extra_at)[half]
                        need(pool, rows_summed, n - 1)
                        for k in range(U):
                            pool.indirect_dma_start(table_rows[:, n % 2, k], None, edge_chunks[k],
                                                    bass.IndirectOffsetOnAxis(ap=at[:, b:b + 1], axis=0)).then_inc(
                                gathered_m[n % 2], 16)

        for plan in (by_dst, by_src):
            list_chunks(plan, before_now)
            before_now = [n + U * TB * (k < 2) for k, n in enumerate(before_now)]
        mid.close()
        mid = ExitStack()

        bits = score[:].bitcast(I32)
        key_i = tmp("key_i", [P, T], I32)
        half_i = tmp("half_i", [P, T], I32)
        key_hi = tmp("key_hi", [P, T])
        key_lo = tmp("key_lo", [P, T])
        real = tmp("real", [P, T])
        hits = tmp("hits", [P, T])
        count = tmp("count", [P, 1])
        wanted = tmp("wanted", [P, 1])
        best_hi = tmp("best_hi", [P, 1])
        best_lo = tmp("best_lo", [P, 1])
        unit = tmp("unit", [P, 1])
        trial = tmp("trial", [P, 1])
        taken = tmp("taken", [P, 1])
        above = tmp("above", [P, T], BF16)
        equal = tmp("equal", [P, T], BF16)
        tmp_t = tmp("tmp_t", [P, T])
        col_sum = tmp("col_sum", [P, T])
        place = tmp("place", [P, T])
        place_eq = tmp("place_eq", [P, T])
        pair_of = tmp("pair_of", [P, T, 2], FP16)

        HALF = 16
        with phase(nc, "counts", "total", "dve_done", "loop_done") as (block, (counts, total, dve_done, loop_done)):
            @block.tensor
            def _(pe):
                for half in range(2):
                    with pe.Fori(0, HALF) as j:
                        n = (HALF + 1) * half + j
                        pe.wait_ge(counts, n + 1)
                        pe.matmul(psM[:, 0, 0:1], ones_f[:], count[:], start=True, stop=True).then_inc(total, 1)
                    n = (HALF + 1) * half + HALF
                    pe.wait_ge(counts, n + 1)
                    pe.matmul(psM[:, 0, 0:1], ones_f[:], count[:], start=True, stop=True).then_inc(total, 1)

            @block.vector
            def _(dve):
                steps = [0]

                def link(ins):
                    steps[0] += 1
                    ins.then_inc(dve_done, 1)
                    dve.wait_ge(dve_done, steps[0])

                def bisect(keys, best, half):
                    link(dve.memset(best[:], 0.0))
                    link(dve.memset(unit[:], float(1 << (HALF - 1))))
                    with dve.Fori(0, HALF) as j:
                        n, m = (HALF + 1) * half + j, 5 * (HALF * half + j)
                        dve.tensor_scalar(trial[:], best[:], unit[:, 0:1], None, ALU.add).then_inc(loop_done, 1)
                        dve.wait_ge(loop_done, m + 1)
                        dve.tensor_scalar(hits[:], keys[:], trial[:, 0:1], None, ALU.is_ge).then_inc(loop_done, 1)
                        dve.wait_ge(loop_done, m + 2)
                        dve.tensor_reduce(count[:], hits[:], AX.X, ALU.add).then_inc(counts, 1)
                        dve.wait_ge(total, n + 1)
                        dve.scalar_tensor_tensor(taken[:], psM[:, 0, 0:1], wanted[:, 0:1], unit[:], ALU.is_ge,
                                                 ALU.mult).then_inc(loop_done, 1)
                        dve.wait_ge(loop_done, m + 3)
                        dve.tensor_tensor(best[:], best[:], taken[:], ALU.add).then_inc(loop_done, 1)
                        dve.tensor_scalar(unit[:], unit[:], 0.5, None, ALU.mult).then_inc(loop_done, 1)
                        dve.wait_ge(loop_done, m + 5)
                    link(dve.tensor_scalar(hits[:], keys[:], best[:, 0:1], None, ALU.is_gt))
                    dve.tensor_reduce(count[:], hits[:], AX.X, ALU.add).then_inc(counts, 1)
                    dve.wait_ge(total, (HALF + 1) * half + HALF + 1)
                    link(dve.scalar_tensor_tensor(wanted[:], psM[:, 0, 0:1], -1.0, wanted[:], ALU.mult, ALU.add))

                link(dve.tensor_scalar(key_i[:], bits, 31, None, ALU.arith_shift_right))
                link(dve.tensor_scalar(key_i[:], key_i[:], -2147483648, None, ALU.bitwise_or))
                link(dve.tensor_tensor(key_i[:], key_i[:], bits, ALU.bitwise_xor))
                link(dve.tensor_scalar(half_i[:], key_i[:], HALF, 0xFFFF, ALU.logical_shift_right, ALU.bitwise_and))
                link(dve.tensor_copy(key_hi[:], half_i[:]))
                link(dve.tensor_scalar(half_i[:], key_i[:], 0xFFFF, None, ALU.bitwise_and))
                link(dve.tensor_copy(key_lo[:], half_i[:]))
                link(dve.tensor_scalar(tmp_t[:], iota_f[:, 0:T], float(P), pcol[:, 0:1], ALU.mult, ALU.add))
                link(dve.tensor_scalar(real[:], tmp_t[:], float(N), None, ALU.is_lt))
                link(dve.scalar_tensor_tensor(key_hi[:], key_hi[:], 1.0, real[:], ALU.add, ALU.mult))
                link(dve.tensor_scalar(key_hi[:], key_hi[:], -1.0, None, ALU.add))
                link(dve.memset(wanted[:], float(K)))
                bisect(key_hi, best_hi, 0)
                link(dve.tensor_scalar(above[:], key_hi[:], best_hi[:, 0:1], None, ALU.is_gt))
                link(dve.tensor_scalar(hits[:], key_hi[:], best_hi[:, 0:1], None, ALU.is_equal))
                link(dve.scalar_tensor_tensor(key_lo[:], key_lo[:], 1.0, hits[:], ALU.add, ALU.mult))
                link(dve.tensor_scalar(key_lo[:], key_lo[:], -1.0, None, ALU.add))
                bisect(key_lo, best_lo, 1)
                link(dve.tensor_scalar(hits[:], key_lo[:], best_lo[:, 0:1], None, ALU.is_gt))
                dve.tensor_tensor(above[:], above[:], hits[:], ALU.add)
                dve.tensor_scalar(equal[:], key_lo[:], best_lo[:, 0:1], None, ALU.is_equal)
                dve.tensor_copy(pair_of[:, :, 0], iota_f[:, 0:T])
                dve.tensor_copy(pair_of[:, :, 1], pcol[:, 0:1].to_broadcast([P, T]))

        with phase(nc, "prefixed", "dve_done") as (block, (prefixed, dve_done)):
            @block.tensor
            def _(pe):
                for j, mask in enumerate((above, equal)):
                    pe.matmul((psM, psO)[j][:, 0, 0:T], before[:], mask[:], start=True, stop=True)
                    last = pe.matmul((psM, psO)[j][:, 1, 0:T], ones_b[:], mask[:], start=True, stop=True)
                last.then_inc(prefixed, 1)

            @block.vector
            def _(dve):
                steps = [0]

                def link(ins):
                    steps[0] += 1
                    ins.then_inc(dve_done, 1)
                    dve.wait_ge(dve_done, steps[0])

                dve.wait_ge(prefixed, 1)
                for ps, to in ((psM, place), (psO, place_eq)):
                    link(dve.tensor_copy(tmp_t[:], ps[:, 1, 0:T]))
                    link(dve.tensor_tensor_scan(col_sum[:], ones_row[:, 0:T], tmp_t[:], 0.0, ALU.mult, ALU.add))
                    if ps is psM:
                        link(dve.tensor_copy(count[:], col_sum[:, T - 1:T]))
                    link(dve.tensor_tensor(col_sum[:], col_sum[:], tmp_t[:], ALU.subtract))
                    link(dve.tensor_tensor(to[:], ps[:, 0, 0:T], col_sum[:], ALU.add))
                link(dve.scalar_tensor_tensor(place[:], place[:], 1.0, above[:], ALU.add, ALU.mult))
                link(dve.tensor_scalar(hits[:], place_eq[:], wanted[:, 0:1], None, ALU.is_lt))
                link(dve.tensor_tensor(hits[:], hits[:], equal[:], ALU.mult))
                link(dve.tensor_scalar(count[:], count[:], 1.0, None, ALU.add))
                link(dve.scalar_tensor_tensor(place_eq[:], place_eq[:], count[:, 0:1], hits[:], ALU.add, ALU.mult))
                link(dve.tensor_tensor(place[:], place[:], place_eq[:], ALU.add))
                dve.tensor_scalar(place[:], place[:], -1.0, None, ALU.add)

        picks = tmp("picks", [P, RING, K], FP16)
        picked = [psM[:, 0, 0:2], psM[:, 1, 0:2]]
        with phase(nc, "picks_made", "picks_used") as (block, (picks_made, picks_used)):
            @block.vector
            def _(dve):
                def step(i, k):
                    c = U * i + k
                    need(dve, picks_used, c - RING + 1)
                    dve.tensor_scalar(picks[:, k % RING], iota_h[:, 0:K], place[:, bass.ds(c, 1)], None,
                                      ALU.is_equal).then_inc(picks_made, 1)
                sweep(dve, T, 0, step, 0)

            @block.tensor
            def _(pe):
                def step(i, k):
                    c = U * i + k
                    at_start = isinstance(c, int) and c == 0
                    at_end = isinstance(c, int) and c == T - 1
                    pe.wait_ge(picks_made, c + 1)
                    for b in range(K // P):
                        last = pe.matmul(picked[b], picks[:, k % RING, b * P:b * P + P],
                                         pair_of[:, bass.ds(c, 1), :].rearrange("p a b -> p (a b)"),
                                         start=at_start, stop=at_end)
                    last.then_inc(picks_used, 1)
                sweep(pe, T, 0, step, 0)

        KB = K // P
        node = tmp("node", [P, KB])
        node_i = tmp("node_i", [P, KB], I32)
        pick_rows = tmp("pick_rows", [P, KB, ROW])
        pick_dot = tmp("pick_dot", [P, KB])
        norm = tmp("norm", [P, 1])
        tanh_s = tmp("tanh_s", [P, KB])
        shared = tmp("shared", [P, 2, KB, P])
        rows_sn = tmp("rows_sn", [P, 2, K])
        greater = tmp("greater", [P, K])
        same = tmp("same", [P, K])
        rank = tmp("rank", [P, KB])
        order = tmp("order", [P, KB, K])
        w_ih = tmp("w_ih", [P, 6, D])
        w_hh = tmp("w_hh", [P, 6, D])
        w_ih_t = tmp("w_ih_t", [P, DB, 3 * D])
        w_hh_t = tmp("w_hh_t", [P, DB, 3 * D])
        w0 = tmp("w0", [P, DB, D])
        w0_t = tmp("w0_t", [P, DB, D])
        x_t = tmp("x_t", [P, DB, K])
        bih_row = tmp("bih_row", [P, 3 * D])
        bhh_row = tmp("bhh_row", [P, 3 * D])
        gate = tmp("gate", [P, KB, 2 * D])
        cand = tmp("cand", [P, KB, D])
        hid = tmp("hid", [P, KB, D])

        with phase(nc, "nodes_made", "w_in", "dots_made", "tanhs", "shared_made", "turned", "dve_done",
                   "w_turned", "w_copied", "ordered", "norm_made") as (
                block, (nodes_made, w_in, dots_made, tanhs, shared_made, turned, dve_done, w_turned, w_copied,
                        ordered, norm_made)):
            @block.sync
            def _(sp):
                sp.dma_start(w_ih[:], W_ih.rearrange("(b p) d -> p b d", p=P)).then_inc(w_in, 16)
                sp.dma_start(w_hh[:], W_hh.rearrange("(b p) d -> p b d", p=P)).then_inc(w_in, 16)
                sp.dma_start(w0[:], W0.rearrange("(b p) d -> p b d", p=P)).then_inc(w_in, 16)
                for to, what in ((bih_row, b_ih), (bhh_row, b_hh)):
                    sp.dma_start(to[:], what.rearrange("(a d) -> a d", a=1).to_broadcast([P, 3 * D])).then_inc(w_in, 16)
                sp.wait_ge(w_in, 16 * 5)

            @block.gpsimd
            def _(pool):
                pool.wait_ge(nodes_made, 1)
                for b in range(KB):
                    pool.indirect_dma_start(pick_rows[:, b], None, table0,
                                            bass.IndirectOffsetOnAxis(ap=node_i[:, b:b + 1], axis=0)).then_inc(
                        gathered_m[0], 16)

            turns = [(w_ih, w_ih_t, o) for o in range(6)] + [(w_hh, w_hh_t, o) for o in range(6)] + \
                    [(w0, w0_t, o) for o in range(DB)]

            @block.vector
            def _(dve):
                steps = [0]

                def link(ins):
                    steps[0] += 1
                    ins.then_inc(dve_done, 1)
                    dve.wait_ge(dve_done, steps[0])

                for b in range(KB):
                    link(dve.tensor_copy(tmp_t[:, 0:2], picked[b]))
                    link(dve.scalar_tensor_tensor(node[:, b:b + 1], tmp_t[:, 0:1], float(P), tmp_t[:, 1:2], ALU.mult,
                                                  ALU.add))
                dve.tensor_copy(node_i[:], node[:]).then_inc(nodes_made, 1)
                link(dve.tensor_tensor_reduce(greater[:], p_row[:], p_row[:], 1.0, 0.0, ALU.mult, ALU.add, norm[:]))
                dve.tensor_copy(norm[:], norm[:]).then_inc(norm_made, 1)
                dve.wait_ge(norm_made, 2)
                link(dve.reciprocal(norm[:], norm[:]))
                dve.wait_ge(gathered_m[0], 16 * (before_now[0] + KB))
                for b in range(KB):
                    link(dve.tensor_tensor_reduce(greater[:], pick_rows[:, b, 0:D], p_row[:], 1.0, 0.0, ALU.mult, ALU.add,
                                                  pick_dot[:, b:b + 1]))
                dve.tensor_copy(rank[:], pick_dot[:]).then_inc(dots_made, 1)
                for b in range(KB):
                    dve.tensor_scalar(shared[:, 0, b], ones_f[:], pick_dot[:, b:b + 1], None, ALU.mult)
                    last = dve.tensor_scalar(shared[:, 1, b], ones_f[:], node[:, b:b + 1], None, ALU.mult)
                last.then_inc(shared_made, 1)
                dve.wait_ge(turned, 1)
                link(dve.tensor_copy(rows_sn[:].rearrange("p a k -> p (a k)"), psA[:, 0, :]))
                for b in range(KB):
                    link(dve.tensor_scalar(greater[:], rows_sn[:, 0], pick_dot[:, b:b + 1], None, ALU.is_gt))
                    link(dve.tensor_scalar(same[:], rows_sn[:, 0], pick_dot[:, b:b + 1], None, ALU.is_equal))
                    link(dve.scalar_tensor_tensor(same[:], rows_sn[:, 1], node[:, b:b + 1], same[:], ALU.is_lt, ALU.mult))
                    link(dve.tensor_tensor(same[:], same[:], greater[:], ALU.add))
                    link(dve.tensor_reduce(rank[:, b:b + 1], same[:], AX.X, ALU.add))
                    link(dve.tensor_scalar(order[:, b], iota_f[:, 0:K], rank[:, b:b + 1], None, ALU.is_equal))
                dve.wait_ge(tanhs, 1)
                for b in range(KB):
                    link(dve.tensor_scalar(pick_rows[:, b, 0:D], pick_rows[:, b, 0:D], tanh_s[:, b:b + 1], None, ALU.mult))
                dve.tensor_copy(count[:], norm[:]).then_inc(ordered, 1)
                for n, (_, to, o) in enumerate(turns):
                    dve.wait_ge(w_turned, n + 1)
                    for b in range(DB):
                        last = dve.tensor_copy(to[:, b, o * P:o * P + P], psT[:, n % 2, b * P:b * P + P])
                    last.then_inc(w_copied, 1)
                dve.wait_ge(ordered, 2)
                for b in range(DB):
                    dve.tensor_copy(x_t[:, b], psO[:, b, 0:K])

            @block.scalar
            def _(act):
                act.wait_ge(norm_made, 1)
                act.activation(norm[:], norm[:], ACT.Sqrt).then_inc(norm_made, 1)
                act.wait_ge(dots_made, 1)
                act.activation(tanh_s[:], pick_dot[:], ACT.Tanh, scale=norm[:, 0:1]).then_inc(tanhs, 1)

            @block.tensor
            def _(pe):
                pe.wait_ge(shared_made, 1)
                for a in range(2):
                    for b in range(KB):
                        last = pe.transpose(psA[:, 0, (a * KB + b) * P:(a * KB + b + 1) * P], shared[:, a, b], ident[:])
                last.then_inc(turned, 1)
                pe.wait_ge(ordered, 1)
                for d in range(DB):
                    for b in range(KB):
                        last = pe.matmul(psO[:, d, 0:K], pick_rows[:, b, d * P:d * P + P], order[:, b], start=b == 0,
                                         stop=b == KB - 1)
                last.then_inc(ordered, 1)
                pe.wait_ge(w_in, 16 * 5)
                for n, (what, _, o) in enumerate(turns):
                    need(pe, w_copied, n - 1)
                    for b in range(DB):
                        last = pe.transpose(psT[:, n % 2, b * P:b * P + P], what[:, o, b * P:b * P + P], ident[:])
                    last.then_inc(w_turned, 1)

        with phase(nc, "products", "dve_done", "gates", "gated", "cands") as (
                block, (products, dve_done, gates, gated, cands)):
            @block.tensor
            def _(pe):
                for b in range(KB):
                    at = slice(b * P, b * P + P)
                    for n, (left, right) in enumerate([(x_t, w_ih_t), (w0_t, w_hh_t)]):
                        for d in range(DB):
                            pe.matmul(psA[:, b, 0:2 * D], left[:, d, at], right[:, d, 0:2 * D], start=n + d == 0,
                                      stop=n + d == DB)
                        for d in range(DB):
                            last = pe.matmul((psT, psO)[n][:, b, 0:D], left[:, d, at], right[:, d, 2 * D:3 * D],
                                             start=d == 0, stop=d == DB - 1)
                    last.then_inc(products, 1)

            @block.vector
            def _(dve):
                steps = [0]

                def link(ins):
                    steps[0] += 1
                    ins.then_inc(dve_done, 1)
                    dve.wait_ge(dve_done, steps[0])

                for b in range(KB):
                    dve.wait_ge(products, b + 1)
                    link(dve.tensor_tensor(gate[:, b], psA[:, b, 0:2 * D], bih_row[:, 0:2 * D], ALU.add))
                    dve.tensor_tensor(gate[:, b], gate[:, b], bhh_row[:, 0:2 * D], ALU.add).then_inc(gates, 1)
                    link(dve.tensor_tensor(cand[:, b], psT[:, b, 0:D], bih_row[:, 2 * D:], ALU.add))
                    link(dve.tensor_tensor(hid[:, b], psO[:, b, 0:D], bhh_row[:, 2 * D:], ALU.add))
                    dve.wait_ge(gated, b + 1)
                    link(dve.tensor_tensor(hid[:, b], hid[:, b], gate[:, b, 0:D], ALU.mult))
                    dve.tensor_tensor(cand[:, b], cand[:, b], hid[:, b], ALU.add).then_inc(gates, 1)
                    dve.wait_ge(cands, b + 1)
                    link(dve.tensor_tensor(hid[:, b], w0[:, b], cand[:, b], ALU.subtract))
                    link(dve.tensor_tensor(hid[:, b], hid[:, b], gate[:, b, D:2 * D], ALU.mult))
                    link(dve.tensor_tensor(w_gcn[:, b], hid[:, b], cand[:, b], ALU.add))

            @block.scalar
            def _(act):
                for b in range(KB):
                    act.wait_ge(gates, 2 * b + 1)
                    act.activation(gate[:, b], gate[:, b], ACT.Sigmoid).then_inc(gated, 1)
                    act.wait_ge(gates, 2 * b + 2)
                    act.activation(cand[:, b], cand[:, b], ACT.Tanh).then_inc(cands, 1)
        mid.close()
        before_now[0] += KB

        rows = sb("rows", [P, U, ROW])
        gather_at = sb("gather_at", [P, U], I32)
        select = sb("select", [P, U, P])
        edge_coef = sb("edge_coef", [P, U])
        running = sb("running", [P, U, D])
        xb = sb("xb", [P, 4, 2, ROW])
        diag = sb("diag", [P, 4, P])
        rb = sb("rb", [P, 4, 2, D])
        extra = sb("extra", [P, U, D])
        total_b = sb("total_b", [P, 4, D])
        mixed = sb("mixed", [P, 4, 2, D])
        turned_b = sb("turned_b", [P, 4, 4, P])
        wb = sb("wb", [P, 2 * DB, D])
        u_b = sb("u_b", [P, U, D])
        act_b = sb("act_b", [P, 2, D])
        v_b = sb("v_b", [P, 4, D])
        squares = sb("squares", [P, D])
        sq_sum = sb("sq_sum", [P, 2])
        inv_norm = sb("inv_norm", [P, 2])
        stats = sb("stats", [P, U, 6])
        mean_var = sb("mean_var", [P, U, 2])
        root = sb("root", [P, U])
        length = sb("length", [P, 2])
        rstd = sb("rstd", [P, U])
        shift = sb("shift", [P, U])
        ob = sb("ob", [P, 4, 2, ROW])

        GCN, SAGE, SAGE_LAST, PAIR, CONV = range(5)

        def edge_sums(kind, width, table, srcs, los, ws, gathered):
            def gather(pool, i, k, base, staged, summed):
                c = U * i + k
                if k % 4 == 0:
                    for j in range(k, k + 4):
                        slot_freed(pool, gathered[j], i, base[j])
                    if isinstance(i, int) and i and not isinstance(base[k], int):
                        take_waits(pool, 3 + k // 4)
                    pool.tensor_copy(gather_at[:, k:k + 4], srcs[:, bass.ds(c, 4)]).then_inc(staged, 1)
                    pool.wait_ge(staged, 2 * i + k // 4 + 1)
                    need(pool, summed, c - U + 4)
                    take_waits(pool)
                pool.indirect_dma_start(rows[:, k, 0:width], None, table,
                                        bass.IndirectOffsetOnAxis(ap=gather_at[:, k:k + 1], axis=0)).then_inc(
                    gathered[k], 16)

            def coefficient(act, i, k, base, coef_made, selected):
                c = U * i + k
                act.wait_ge(gathered[k], 16 * (i + 1 + base[k]))
                need(act, selected, c - U + 1)
                act.activation(edge_coef[:, k:k + 1], ws[:, bass.ds(c, 1)], ACT.Copy,
                               scale=rows[:, k, D:D + 1]).then_inc(coef_made, 1)

            def choose(dve, i, k, base, coef_made, selected, summed):
                c, r = U * i + k, k
                need(dve, summed, c - U + 1)
                if kind == GCN:
                    dve.wait_ge(coef_made, c + 1)
                    coef = edge_coef[:, k:k + 1]
                elif kind == PAIR:
                    dve.wait_ge(gathered[k], 16 * (i + 1 + base[k]))
                    coef = rows[:, k, D:D + 1]
                elif kind == CONV:
                    coef = ws[:, bass.ds(c, 1)]
                else:
                    coef = None
                lo = los[:, bass.ds(c, 1)]
                if coef is None:
                    dve.tensor_scalar(select[:, r], iota_f[:, 0:P], lo, None, ALU.is_equal).then_inc(selected, 1)
                else:
                    dve.tensor_scalar(select[:, r], iota_f[:, 0:P], lo, coef, ALU.is_equal, ALU.mult).then_inc(
                        selected, 1)

            def multiply(pe, i, k, base, selected, sum_read, summed, add_own=None):
                c = U * i + k
                pe.wait_ge(selected, c + 1)
                pe.wait_ge(gathered[k], 16 * (i + 1 + base[k]))
                need(pe, sum_read, c - 1)
                if kind == PAIR:
                    last = pe.matmul(sum_ps[k % 2], select[:, k], rows[:, k, 0:D], start=True, stop=True)
                else:
                    for b in range(DB):
                        at = slice(b * P, b * P + P)
                        last = pe.matmul(sum_ps[k % 2][:, at], rows[:, k, at], select[:, k], start=True,
                                         stop=add_own is None)
                        if add_own is not None:
                            last = add_own(sum_ps[k % 2][:, at], at)
                last.then_inc(summed, 1)
            return gather, coefficient, choose, multiply

        def overflow_sweep(name, kind, width, table, weights, plan):
            gather, coefficient, choose, multiply = edge_sums(kind, width, table, *plan.extra, plan.gathered)

            def counted(eng, step):
                final = eng.value_load(plan.x_last[0:1, 0:1], min_val=2, max_val=XB // U - 1)
                base = [(final + 1) * plan.sweeps if plan.sweeps else 0] * U
                for i in range(2):
                    for k in range(U):
                        step(i, k, base)
                with eng.Fori(2, final + 1) as i:
                    for k in range(U):
                        step(i, k, base)
                return final

            with phase(nc, *[f"{name}_{n}" for n in ("staged", "coef_made", "selected", "summed", "sum_done", "w_in",
                                                     "carry_set")],
                       *[f"{name}_sums_out{k}" for k in range(U)]) as (
                    block, (staged, coef_made, selected, summed, sum_done, w_in, carry_set, *sums_out)):

                @block.gpsimd
                def _(pool):
                    counted(pool, lambda i, k, base: gather(pool, i, k, base, staged, summed))

                @block.scalar
                def _(act):
                    if kind == GCN:
                        counted(act, lambda i, k, base: coefficient(act, i, k, base, coef_made, selected))

                @block.tensor
                def _(pe):
                    final = counted(pe, lambda i, k, base: multiply(pe, i, k, base, selected, sum_done, summed))
                    for k in range(U):
                        pe.wait_ge(sums_out[k], 16 * final + 16)

                @block.vector
                def _(dve):
                    dve.memset(running[:, U - 1], 0.0).then_inc(carry_set, 1)
                    dve.wait_ge(carry_set, 1)

                    def add(i, k):
                        if isinstance(i, int) and i < 0:
                            return
                        c = U * i + k
                        dve.wait_ge(summed, c + 1)
                        need(dve, sum_done, c)
                        need(dve, sums_out[k], 16 * i)
                        dve.scalar_tensor_tensor(running[:, k], running[:, (k - 1) % U], plan.carry[:, bass.ds(c, 1)],
                                                 sum_ps[k % 2], ALU.mult, ALU.add).then_inc(sum_done, 1)

                    def step(i, k, base):
                        choose(dve, i, k, base, coef_made, selected, summed)
                        add(*tile_at(i, k - 1))
                    final = counted(dve, step)
                    add(final, U - 1)

                @block.sync
                def _(sp):
                    for j, w in enumerate(weights):
                        sp.dma_start(wb[:, DB * j:DB * j + DB], w.rearrange("(b p) d -> p b d", p=P)).then_inc(w_in, 16)

                    def step(i, k, base):
                        c = U * i + k
                        sp.wait_ge(sum_done, c + 1)
                        sp.dma_start(overflow_sums[bass.ds(c, 1)].rearrange("a p d -> p (a d)"), running[:, k]).then_inc(
                            sums_out[k], 16)
                    counted(sp, step)
                    need(sp, w_in, 16 * len(weights))
                    sp.wait_ge(sum_done, 1)

        def tile_sweep(name, kind, width, table, weights, bias, residual, target, plan):
            gather, coefficient, choose, multiply = edge_sums(kind, width, table, *plan.main, gathered_m)
            base = list(before_now)
            pairs = table.rearrange("(g k p) d -> g p k d", k=2, p=P)
            final = target is None
            out_width = D if final else target.shape[1]
            out_pairs = (out[0:WHOLE_PAIRS * 2 * P] if final else target).rearrange("(g k p) d -> g p k d", k=2, p=P)
            TURN = {GCN: None, SAGE: 1, SAGE_LAST: 1, PAIR: 2, CONV: None}[kind]
            COPY = TURN and TURN + 1
            PRODUCT = TURN + 2 if TURN else 2
            CHOOSE = 1 if kind in (GCN, PAIR) else 3
            FINISH = PRODUCT + 1
            MEASURE = FINISH + (2 if kind == PAIR else 1)
            ROOT, SCALE = MEASURE + 1, MEASURE + 2
            LAG = FINISH + 1 if kind == SAGE else SCALE + 1
            CHAIN = {GCN: 2, SAGE_LAST: 3, PAIR: 4, CONV: 3, SAGE: 0}[kind]
            BLOCKS = 2 * DB if kind == PAIR else DB
            normed = kind != SAGE

            def real(i, k):
                return not isinstance(i, int) or 0 <= U * i + k < T

            with phase(nc, *[f"{name}_{n}" for n in ("staged", "coef_made", "selected", "summed", "part_done",
                                                     "total_done", "scaled", "turned", "copied", "product", "product_read",
                                                     "chained", "measured", "rooted", "inverted", "ready", "activated", "leaked",
                                                     "rows_done")],
                       *[f"{name}_x_in{k}" for k in range(4)],
                       *[f"{name}_extra_in{k}" for k in range(U)], *[f"{name}_rows_out{k}" for k in range(4)]) as (
                    block, (staged, coef_made, selected, summed, part_done, total_done, scaled, turned, copied, product,
                            product_read, chained, measured, rooted, inverted, ready, activated, leaked,
                            rows_done, *dmas)):
                x_in, extra_in, rows_out = dmas[0:4], dmas[4:U + 4], dmas[U + 4:]
                sum_read = part_done if kind == PAIR else total_done
                X_LOADS = 2 if residual is not None else 1

                @block.gpsimd
                def _(pool):
                    sweep(pool, T, 0, lambda i, k: gather(pool, i, k, base, staged, summed), 0)

                @block.sync
                def _(sp):
                    def step(i, k):
                        t, g, r = U * i + k, 4 * i + k // 2, k // 2
                        if k % 2 == 0:
                            if kind == SAGE:
                                need(sp, turned, t - 6)
                            else:
                                need(sp, chained, CHAIN * (t - 7) + {GCN: 1, SAGE_LAST: 2, PAIR: 3, CONV: 2}[kind])
                            sp.dma_start(xb[:, r, :, 0:width], pairs[g]).then_inc(x_in[r], 16)
                            if residual is not None:
                                sp.dma_start(rb[:, r], residual.rearrange("(g k p) d -> g p k d", k=2, p=P)[g]).then_inc(
                                    x_in[r], 16)
                        at = sp.value_load(plan.sums_at[0:1, bass.ds(t, 1)], min_val=0, max_val=XB)
                        need(sp, total_done, t - U + 1)
                        sp.dma_start(extra[:, k], overflow_sums[bass.ds(at, 1)].rearrange("a p d -> p (a d)")).then_inc(
                            extra_in[k], 16)
                    sweep(sp, T, 0, step, 0)

                @block.tensor
                def _(pe):
                    def turn(i, k):
                        if not real(i, k):
                            return
                        t, r = U * i + k, k % 4
                        if kind == PAIR:
                            pe.wait_ge(total_done, t + 1)
                            left = [mixed[:, r, 0], mixed[:, r, 1]]
                        else:
                            pe.wait_ge(x_in[k // 2], 16 * X_LOADS * (i + 1))
                            left = [xb[:, k // 2, k % 2]]
                        need(pe, copied, t - 1)
                        for j, a in enumerate(left):
                            for b in range(DB):
                                n = DB * j + b
                                last = pe.transpose(turned_ps[k % 2][:, n * P:n * P + P], a[:, b * P:b * P + P], ident[:])
                        last.then_inc(turned, 1)

                    def multiply_w(i, k):
                        if not real(i, k):
                            return
                        t, r = U * i + k, k % 4
                        if TURN:
                            pe.wait_ge(copied, t + 1)
                        pe.wait_ge(total_done, t + 1)
                        if kind == PAIR:
                            need(pe, product_read, t - 3)
                        elif kind == SAGE:
                            need(pe, ready, t - 3)
                        else:
                            need(pe, chained, CHAIN * (t - 4) + 1)
                        sums = [mixed[:, r, 0, b * P:b * P + P] for b in range(DB)]
                        if kind == GCN:
                            parts = [list(zip(sums, [w_gcn[:, b] for b in range(DB)]))]
                        elif kind == CONV:
                            parts = [list(zip(sums, [wb[:, b] for b in range(DB)]))]
                        elif kind == PAIR:
                            parts = [[(turned_b[:, r, n], wb[:, n]) for n in range(2 * DB)]]
                        else:
                            parts = [[(turned_b[:, r, b], wb[:, b]) for b in range(DB)],
                                     [(sums[b], wb[:, DB + b]) for b in range(DB)]]
                        for j, part in enumerate(parts):
                            for n, (left, w) in enumerate(part):
                                last = pe.matmul(product_ps[r][:, j * D:j * D + D], left, w, start=n == 0,
                                                 stop=n == len(part) - 1)
                        last.then_inc(product, 1)

                    def step(i, k):
                        if real(i, k):
                            own = None
                            if kind == GCN:
                                pe.wait_ge(x_in[k // 2], 16 * X_LOADS * (i + 1))
                                pe.wait_ge(scaled, U * i + k + 1)

                                def own(to, at):
                                    return pe.matmul(to, xb[:, k // 2, k % 2, at], diag[:, k % 4], start=False, stop=True)
                            multiply(pe, i, k, base, selected, sum_read, summed, own)
                        if TURN:
                            turn(*tile_at(i, k - TURN))
                        multiply_w(*tile_at(i, k - PRODUCT))
                    sweep(pe, T, 0, lambda i, k: step(*tile_at(i, k)), PRODUCT, peeled=2)

                @block.vector
                def _(dve):
                    def add(i, k):
                        if not real(i, k):
                            return
                        t, r = U * i + k, k % 4
                        dve.wait_ge(summed, t + 1)
                        dve.wait_ge(extra_in[k], 16 * (i + 1))
                        if kind == PAIR:
                            need(dve, turned, t - 3)
                            dve.tensor_tensor(total_b[:, r], sum_ps[k % 2], extra[:, k], ALU.add).then_inc(part_done, 1)
                        else:
                            need(dve, product, t - 3)
                            dve.tensor_tensor(mixed[:, r, 0], sum_ps[k % 2], extra[:, k], ALU.add).then_inc(total_done, 1)

                    def make_factors(i, k):
                        if not real(i, k) or kind != PAIR:
                            return
                        t, r = U * i + k, k % 4
                        x_t, root_t = xb[:, k // 2, k % 2, 0:D], root_out[:, bass.ds(t, 1)]
                        dve.wait_ge(part_done, t + 1)
                        dve.wait_ge(x_in[k // 2], 16 * X_LOADS * (i + 1))
                        dve.scalar_tensor_tensor(mixed[:, r, 0], total_b[:, r], root_t, x_t, ALU.mult, ALU.add)
                        dve.scalar_tensor_tensor(mixed[:, r, 1], total_b[:, r], root_t, x_t, ALU.mult,
                                                 ALU.mult).then_inc(total_done, 1)

                    def take_product(i, k):
                        if not real(i, k):
                            return
                        t, r = U * i + k, k % 4
                        dve.wait_ge(product, t + 1)
                        if kind == GCN:
                            need(dve, rows_done, t - U + 1)
                            dve.scalar_tensor_tensor(u_b[:, k], product_ps[r][:, 0:D], dinv[:, bass.ds(t, 1)],
                                                     xb[:, k // 2, k % 2, 0:D], ALU.mult, ALU.add).then_inc(chained, 1)
                        elif kind in (SAGE, SAGE_LAST):
                            if kind == SAGE:
                                need(dve, ready, t - 3)
                            dve.scalar_tensor_tensor(v_b[:, r], product_ps[r][:, D:2 * D], inv_deg[:, bass.ds(t, 1)], bias,
                                                     ALU.mult, ALU.add).then_inc(part_done, 1)
                        elif kind == PAIR:
                            dve.scalar_tensor_tensor(v_b[:, r], product_ps[r][:, 0:D], has_in[:, bass.ds(t, 1)], bias, ALU.mult,
                                                     ALU.add).then_inc(product_read, 1)
                        else:
                            dve.tensor_tensor(v_b[:, r], product_ps[r][:, 0:D], bias, ALU.add).then_inc(chained, 1)

                    def add_rows_product(i, k):
                        if not real(i, k) or kind not in (SAGE, SAGE_LAST):
                            return
                        t = U * i + k
                        dve.wait_ge(part_done, t + 1)
                        if kind == SAGE:
                            need(dve, rows_done, t - U + 1)
                            dve.tensor_tensor(u_b[:, k], product_ps[k % 4][:, 0:D], v_b[:, k % 4], ALU.add).then_inc(ready, 1)
                        else:
                            dve.tensor_tensor(act_b[:, k % 2], product_ps[k % 4][:, 0:D], v_b[:, k % 4], ALU.add).then_inc(chained, 1)

                    def add_residual(i, k):
                        if not real(i, k) or kind not in (SAGE_LAST, CONV):
                            return
                        t = U * i + k
                        row = act_b[:, k % 2] if kind == SAGE_LAST else v_b[:, k % 4]
                        other = rb[:, k // 2, k % 2] if residual is not None else xb[:, k // 2, k % 2, 0:D]
                        dve.wait_ge(chained, CHAIN * t + 1)
                        need(dve, rows_done, t - U + 1)
                        dve.tensor_tensor(u_b[:, k], row, other, ALU.add).then_inc(chained, 1)

                    def leak(i, k):
                        if not real(i, k) or kind != PAIR:
                            return
                        t, q, r = U * i + k, k % 2, k % 4
                        dve.wait_ge(product_read, t + 1)
                        need(dve, activated, t - 1)
                        dve.scalar_tensor_tensor(act_b[:, q], v_b[:, r], 0.01, v_b[:, r], ALU.mult,
                                                 ALU.max).then_inc(leaked, 1)

                    def bound_norm(i, k):
                        if not real(i, k) or kind != PAIR:
                            return
                        q = k % 2
                        dve.wait_ge(activated, U * i + k + 1)
                        dve.tensor_scalar(inv_norm[:, q:q + 1], length[:, q:q + 1], 1e-12, None,
                                          ALU.max).then_inc(chained, 1)

                    def invert_norm(i, k):
                        if not real(i, k) or kind != PAIR:
                            return
                        q = k % 2
                        dve.wait_ge(chained, CHAIN * (U * i + k) + 1)
                        dve.reciprocal(inv_norm[:, q:q + 1], inv_norm[:, q:q + 1]).then_inc(chained, 1)

                    def unit_rows(i, k):
                        if not real(i, k) or kind != PAIR:
                            return
                        t, q = U * i + k, k % 2
                        dve.wait_ge(chained, CHAIN * t + 2)
                        need(dve, rows_done, t - U + 1)
                        dve.scalar_tensor_tensor(u_b[:, k], act_b[:, q], inv_norm[:, q:q + 1],
                                                 xb[:, k // 2, k % 2, 0:D], ALU.mult, ALU.add).then_inc(chained, 1)

                    def measure(i, k):
                        if not real(i, k) or not normed:
                            return
                        dve.wait_ge(chained, CHAIN * (U * i + k + 1) - 1)
                        dve.bn_stats(stats[:, k], u_b[:, k]).then_inc(chained, 1)

                    def invert_root(i, k):
                        if not real(i, k) or not normed:
                            return
                        dve.wait_ge(rooted, U * i + k + 1)
                        dve.reciprocal(rstd[:, k:k + 1], root[:, k:k + 1]).then_inc(inverted, 1)

                    def make_shift(i, k):
                        if not real(i, k) or not normed:
                            return
                        dve.wait_ge(inverted, U * i + k + 1)
                        dve.scalar_tensor_tensor(shift[:, k:k + 1], mean_var[:, k, 0:1], -1.0, rstd[:, k:k + 1], ALU.mult,
                                                 ALU.mult).then_inc(ready, 1)

                    def step(i, k):
                        take_product(*tile_at(i, k - FINISH))
                        bound_norm(*tile_at(i, k - FINISH - 1))
                        add(*tile_at(i, k - 1))
                        invert_root(*tile_at(i, k - SCALE))
                        invert_norm(*tile_at(i, k - FINISH - 1))
                        leak(*tile_at(i, k - FINISH))
                        add_rows_product(*tile_at(i, k - FINISH))
                        if kind == CONV:
                            add_residual(*tile_at(i, k - FINISH))
                        make_shift(*tile_at(i, k - SCALE))
                        unit_rows(*tile_at(i, k - FINISH - 1))
                        make_factors(*tile_at(i, k - 1))
                        m, mk = tile_at(i, k - MEASURE)
                        measures = normed and real(m, mk)
                        if measures:
                            dve.wait_ge(chained, CHAIN * (U * m + mk + 1))
                        b = tile_at(i, k + CHOOSE)
                        if real(*b):
                            choose(dve, *b, base, coef_made, selected, summed)
                        if measures:
                            dve.bn_aggr(mean_var[:, mk], stats[:, mk]).then_inc(measured, 1)
                        if kind == SAGE_LAST:
                            add_residual(*tile_at(i, k - FINISH))
                        measure(*tile_at(i, k - MEASURE + 1))
                    sweep(dve, T, 3, step, LAG, peeled=2)

                @block.scalar
                def _(act):
                    def store(i, k):
                        g, r = 4 * i + k // 2, k // 2
                        act.wait_ge(rows_done, U * i + k + 1)
                        if final and isinstance(g, int) and g == WHOLE_PAIRS:
                            act.dma_start(out[N - REST:N, :], ob[0:REST, r, 0, 0:D]).then_inc(rows_out[r], 16)
                        else:
                            act.dma_start(out_pairs[g], ob[:, r, :, 0:out_width]).then_inc(rows_out[r], 16)

                    def finish(i, k):
                        if not real(i, k):
                            return
                        t, q, r, s = U * i + k, k % 2, k // 2, k
                        need(act, rows_out[r], 16 * i)
                        act.wait_ge(ready, t + 1)
                        if out_width == ROW:
                            act.copy(ob[:, r, q, D:ROW], root_out[:, bass.ds(t, 1)])
                        if normed:
                            act.activation(ob[:, r, q, 0:D], u_b[:, s], ACT.Identity,
                                           bias=shift[:, s:s + 1], scale=rstd[:, s:s + 1]).then_inc(rows_done, 1)
                        else:
                            act.activation(ob[:, r, q, 0:D], u_b[:, s], ACT.Relu).then_inc(rows_done, 1)
                        if k % 2:
                            store(i, k)

                    def step(i, k):
                        finish(*tile_at(i, k - LAG))
                        a = tile_at(i, k - ROOT)
                        if normed and real(*a):
                            t, s = U * a[0] + a[1], a[1]
                            act.wait_ge(measured, t + 1)
                            act.activation(root[:, s:s + 1], mean_var[:, s, 1:2], ACT.Sqrt,
                                           bias=eps_col[:, 0:1]).then_inc(rooted, 1)
                        a = tile_at(i, k - (COPY or 0))
                        if TURN and real(*a):
                            t, r = U * a[0] + a[1], a[1] % 4
                            act.wait_ge(turned, t + 1)
                            need(act, product, t - 3)
                            act.copy(turned_b[:, r, 0:BLOCKS].rearrange("p b n -> p (b n)"),
                                     turned_ps[a[1] % 2][:, 0:BLOCKS * P]).then_inc(copied, 1)
                        a = tile_at(i, k + 1)
                        if kind == GCN and real(*a):
                            t, r = U * a[0] + a[1], a[1] % 4
                            need(act, summed, t - 3)
                            act.activation(diag[:, r], ident[:], ACT.Copy,
                                           scale=dinv[:, bass.ds(t, 1)]).then_inc(scaled, 1)
                        b = tile_at(i, k + 2)
                        if kind == GCN and real(*b):
                            coefficient(act, *b, base, coef_made, selected)
                        a = tile_at(i, k - FINISH)
                        if kind == PAIR and real(*a):
                            t, q = U * a[0] + a[1], a[1] % 2
                            act.wait_ge(leaked, t + 1)
                            act.activation(squares[:], act_b[:, q], ACT.Square,
                                           accum_out=sq_sum[:, q:q + 1]).then_inc(scaled, 1)
                            act.wait_ge(scaled, t + 1)
                            act.activation(length[:, q:q + 1], sq_sum[:, q:q + 1], ACT.Sqrt,
                                           bias=tiny_col[:, 0:1]).then_inc(activated, 1)
                    sweep(act, T, 4, step, LAG, peeled=3)
                    for r in range(4):
                        act.wait_ge(rows_out[r], 16 * (T // U))

        def layer(name, kind, table, weights, bias, residual, target, plan=by_dst):
            width = table.shape[1]
            overflow_sweep("x_" + name, kind, width, table, weights, plan)
            tile_sweep(name, kind, width, table, weights, bias, residual, target, plan)
            before_now[:] = [n + T // U for n in before_now]
            plan.sweeps += 1

        layer("gcn", GCN, table0, [], None, None, table1)
        layer("sage0", SAGE, table1, [W_self[0], W_neigh[0]], bsage_row[:, 0], None, table1a)
        layer("sage1", SAGE, table1a, [W_self[1], W_neigh[1]], bsage_row[:, 1], None, table1b)
        layer("sage2", SAGE_LAST, table1b, [W_self[2], W_neigh[2]], bsage_row[:, 2], table1, table2)
        layer("pair", PAIR, table2, [W_one, W_two], bpair_row[:], None, table3)
        layer("conv", CONV, table3, [W_conv], bconv_row[:], None, None, by_src)


_INS = ["x", "src", "dst", "edge_weight", "L0_gnn_p", "L0_gnn_W_ih", "L0_gnn_W_hh", "L0_gnn_b_ih", "L0_gnn_b_hh",
        "L0_gnn_W0", "L1_gnn_W_self", "L1_gnn_W_neigh", "L1_gnn_bias", "L2_gnn_W1", "L2_gnn_W2", "L2_gnn_b",
        "L3_gnn_weight", "L3_gnn_bias"]


def kernel(**inputs):
    import numpy as _np
    import concourse.bacc as _bacc
    from concourse import mybir as _mybir
    from concourse.bass_utils import run_bass_kernel_spmd as _run

    nc = _bacc.Bacc("TRN2", target_bir_lowering=False, num_devices=1)
    arrays, args = {}, []
    for name in _INS:
        a = _np.ascontiguousarray(inputs[name])
        arrays[f"in_{name}_dram"] = a
        args.append(nc.dram_tensor(f"in_{name}_dram", a.shape, _mybir.dt.from_np(a.dtype), kind="ExternalInput").ap())
    shape = tuple(inputs["x"].shape)
    result = nc.dram_tensor("out_0_dram", shape, _mybir.dt.float32, kind="ExternalOutput").ap()
    graph_stack(nc, *args, result)
    r = _run(nc, [arrays], core_ids=[0])
    return r.results[0]["out_0_dram"]
```

```python
from contextlib import ExitStack, contextmanager

import concourse.bass as bass
from concourse import mybir

F32 = mybir.dt.float32
BF16 = mybir.dt.bfloat16
FP16 = mybir.dt.float16
I32 = mybir.dt.int32
ALU = mybir.AluOpType
ACT = mybir.ActivationFunctionType
AX = mybir.AxisListType

P = 128
D = 256
DB = D // P
K = D
U = 8
XU = 8
EPS = 1e-5


class Plan:

    def __init__(self, sb, dram, sem, name, T, TW, rows):
        self.name = name
        self.overflow = sb(f"{name}_overflow", [P, TW])
        self.upto = sb(f"{name}_upto", [P, TW])
        self.first = sb(f"{name}_first", [P, TW])
        self.base = sb(f"{name}_base", [P, TW])
        self.sums_at = sb(f"{name}_sums_at", [P, T], I32)
        self.x_last = sb(f"{name}_x_last", [P, 1], I32)
        self.carry = sb(f"{name}_carry", [P, TW])
        self.main, self.extra = [(sb(f"{name}_{h}_from", [P, TW], I32),
                                  sb(f"{name}_{h}_to", [P, TW]),
                                  sb(f"{name}_{h}_weight", [P, TW]))
                                 for h in ("main", "extra")]
        self.tables = [dram(f"{name}_table{k}", [rows, 4]) for k in range(U)]
        self.gathered = [sem(f"{name}_gathered{k}") for k in range(U)]
        self.sweeps = 0


@contextmanager
def phase(nc, *names):
    with ExitStack() as held:
        sems = [held.enter_context(nc.semaphore(n)) for n in names]
        with nc.Block() as block:
            yield block, sems
        nums = [s.num for s in sems]
        assert set(range(min(nums), max(nums) + 1)) <= set(nums) | set(nc.free_semaphores)
        nc.all_engine_barrier(sems_to_clear=range(min(nums), max(nums) + 1))


def need(eng, sem, value):
    if not isinstance(value, int) or value > 0:
        eng.wait_ge(sem, value)


def slot_freed(eng, sem, i, base):
    if not (isinstance(i, int) and i == 0):
        eng.wait_ge(sem, 16 * (i + base))


def tile_at(i, k):
    return i + k // U, k % U


def sweep(eng, tiles, lead, step, lag, peeled=1):
    n = tiles // U
    for k in range(-lead, U * peeled):
        step(*((0, k) if k < 0 else divmod(k, U)))
    if n > peeled + 1:
        with eng.Fori(peeled, n - 1) as i:
            for k in range(U):
                step(i, k)
    for k in range(U + lag):
        step(n - 1, k)


def graph_stack(nc, x, src, dst, edge_weight, p, W_ih, W_hh, b_ih, b_hh, W0, W_self, W_neigh, b_sage,
                W_one, W_two, b_pair, W_conv, b_conv, out):
    N, E = x.shape[0], src.shape[0]
    assert x.shape[1] == D
    T = -(-max(N, E) // (P * U)) * U
    C = T
    REAL = N // P
    REST = N - REAL * P
    assert T // U >= 4 and T == REAL + 2 and REAL % 2 == 0 and REST
    XB = -(-(E // P + 1) // XU) * XU + 2 * XU
    TB = -(-max(T, XB, K) // P)
    TW = TB * P
    SLOTS = 2 * TW + 2
    TRASH = SLOTS * P
    ROW = D + 1

    ctx = ExitStack()
    with ctx:
        def sb(name, shape, dt=F32):
            return ctx.enter_context(nc.sbuf_tensor(name, shape, dt))

        def dram(name, shape, dt=F32):
            return nc.dram_tensor(name, shape, dt, kind="Internal").ap()

        table0 = dram("table0", [T * P, ROW])
        table1 = dram("table1", [T * P, D])
        table1a = dram("table1a", [T * P, D])
        table1b = dram("table1b", [T * P, D])
        table2 = dram("table2", [T * P, ROW])
        table3 = dram("table3", [T * P, D])
        overflow_sums = dram("overflow_sums", [XB + 1, P, D])

        gathered_m = [ctx.enter_context(nc.semaphore(f"gathered{k}")) for k in range(U)]
        before_now = [0] * U
        scattered = [ctx.enter_context(nc.semaphore(f"scattered{k}")) for k in range(U)]

        psA = ctx.enter_context(nc.psum_tensor("psA", [P, 2, 512], F32))
        psT = ctx.enter_context(nc.psum_tensor("psT", [P, 2, 512], F32))
        psO = ctx.enter_context(nc.psum_tensor("psO", [P, 2, 512], F32))
        psM = ctx.enter_context(nc.psum_tensor("psM", [P, 2, 512], F32))

        sum_ps = [psA[:, s, 0:D] for s in range(2)]
        turned_ps = [psT[:, s] for s in range(2)]
        product_ps = [ps[:, s] for ps in (psO, psM) for s in range(2)]

        iota_i = sb("iota_i", [P, TW], I32)
        pcol_i = sb("pcol_i", [P, 1], I32)
        iota_f = sb("iota_f", [P, TW])
        iota_h = sb("iota_h", [P, TW], FP16)
        pcol = sb("pcol", [P, 1])
        ident = sb("ident", [P, P])
        ones_f = sb("ones_f", [P, P])
        ones_row = sb("ones_row", [P, TW])
        eps_col = sb("eps_col", [P, 1])
        tiny_col = sb("tiny_col", [P, 1])
        ones_b = sb("ones_b", [P, P], BF16)
        before = sb("before", [P, P], BF16)
        not_before = sb("not_before", [P, P], BF16)
        zeros = sb("zeros", [P, D])
        p_row = sb("p_row", [P, D])
        bsage_row = sb("bsage_row", [P, 3, D])
        bpair_row = sb("bpair_row", [P, D])
        bconv_row = sb("bconv_row", [P, D])
        dinv = sb("dinv", [P, T])
        inv_deg = sb("inv_deg", [P, T])
        has_in = sb("has_in", [P, T])
        root_out = sb("root_out", [P, T])
        root_deg = sb("root_deg", [P, T])
        score = sb("score", [P, T])
        def sem(name):
            return ctx.enter_context(nc.semaphore(name))

        by_dst, by_src = [Plan(sb, dram, sem, name, T, TW, TRASH + P) for name in ("by_dst", "by_src")]
        w_gcn = sb("w_gcn", [P, 2, D])

        pool_waits = sb("pool_waits", [P, 5])

        def take_waits(pool, at=0):
            pool.tensor_tensor(pool_waits[0:1, at:at + 1], pool_waits[0:1, 1:2], pool_waits[0:1, 2:3], ALU.add)

        late = ExitStack()
        kept_fields, src_hi, pad_at, out_sb = [late.enter_context(nc.sbuf_tensor(name, shape, F32)) for name, shape in (
            ("by_src_fields", [P, C, 4]), ("src_hi", [P, C]), ("pad_at", [P, C]), ("out_sb", [P, T]))]
        early = ExitStack()

        def tmp(name, shape, dt=F32):
            return early.enter_context(nc.sbuf_tensor(name, shape, dt))

        src_i = tmp("src_i", [P, C], I32)
        dst_i = tmp("dst_i", [P, C], I32)
        w_f = tmp("w_f", [P, C])
        fields = {by_dst: tmp("by_dst_fields", [P, C, 4]), by_src: kept_fields}
        dst_hi = tmp("dst_hi", [P, C])
        dst_lo = tmp("dst_lo", [P, C])
        src_lo = tmp("src_lo", [P, C])
        w_part = tmp("w_part", [P, 3, C])
        w_half = tmp("w_half", [P, C], BF16)
        w_rest = tmp("w_rest", [P, C])
        cut_i = tmp("cut_i", [P, C], I32)
        table_fill = tmp("table_fill", [P, 2 * P, 4])

        full, rest = E // C, E % C
        with phase(nc, "pads_set", "iotas_made", "edges_in", "rows_in", "fill_set", "dve_done") as (
                block, (pads_set, iotas_made, edges_in, rows_in, fill_set, dve_done)):
            @block.gpsimd
            def _(pool):
                pool.iota(iota_i[:], [[1, TW]], base=0, channel_multiplier=0)
                pool.iota(pcol_i[:], [[0, 1]], base=0, channel_multiplier=1).then_inc(iotas_made, 1)

            @block.sync
            def _(sp):
                sp.wait_ge(pads_set, 1)
                for to, what in ((src_i, src), (dst_i, dst), (w_f, edge_weight)):
                    sp.dma_start(to[0:full, :], what[0:full * C].rearrange("(a c) -> a c", c=C)).then_inc(edges_in, 16)
                    if rest:
                        sp.dma_start(to[full:full + 1, 0:rest],
                                     what[full * C:E].rearrange("(a c) -> a c", a=1)).then_inc(edges_in, 16)
                for to, what in ((p_row[:], p), (bpair_row[:], b_pair), (bconv_row[:], b_conv),
                                 (bsage_row[:, 0], b_sage[0]), (bsage_row[:, 1], b_sage[1]),
                                 (bsage_row[:, 2], b_sage[2])):
                    sp.dma_start(to, what.rearrange("(a d) -> a d", a=1).to_broadcast([P, D])).then_inc(rows_in, 16)
                sp.wait_ge(fill_set, 1)
                sp.wait_ge(rows_in, 16 * 6)

            @block.vector
            def _(dve):
                steps = [0]

                def link(ins):
                    steps[0] += 1
                    ins.then_inc(dve_done, 1)
                    dve.wait_ge(dve_done, steps[0])

                dve.memset(pool_waits[:], 0.0)
                dve.memset(src_i[:], -1)
                dve.memset(dst_i[:], -1)
                dve.memset(w_f[:], 0.0).then_inc(pads_set, 1)
                dve.memset(zeros[:], 0.0)
                dve.memset(table_fill[:], 0.0).then_inc(fill_set, 1)
                dve.memset(ones_f[:], 1.0)
                dve.memset(ones_row[:], 1.0)
                dve.memset(eps_col[:], EPS)
                dve.memset(tiny_col[:], 1e-34)
                dve.memset(ones_b[:], 1.0)
                for f in fields.values():
                    dve.memset(f[:], 0.0)
                dve.wait_ge(iotas_made, 1)
                dve.tensor_copy(iota_f[:], iota_i[:])
                dve.tensor_copy(iota_h[:], iota_i[:])
                link(dve.tensor_copy(pcol[:], pcol_i[:]))
                dve.tensor_scalar(ident[:], iota_f[:, 0:P], pcol[:, 0:1], None, ALU.is_equal)
                dve.tensor_scalar(before[:], iota_f[:, 0:P], pcol[:, 0:1], None, ALU.is_gt)
                dve.tensor_scalar(not_before[:], iota_f[:, 0:P], pcol[:, 0:1], None, ALU.is_le)
                dve.wait_ge(edges_in, 16 * 3 * (1 + (rest > 0)))
                for to_hi, to_lo, what in ((dst_hi, dst_lo, dst_i), (src_hi, src_lo, src_i)):
                    link(dve.tensor_scalar(cut_i[:], what[:], 7, None, ALU.arith_shift_right))
                    link(dve.tensor_copy(to_hi[:], cut_i[:]))
                    link(dve.tensor_scalar(cut_i[:], what[:], P - 1, None, ALU.bitwise_and))
                    link(dve.tensor_copy(to_lo[:], cut_i[:]))
                for plan, taken, lo in ((by_dst, src_i, dst_lo), (by_src, dst_i, src_lo)):
                    dve.tensor_copy(fields[plan][:, :, 0], taken[:])
                    dve.tensor_scalar(fields[plan][:, :, 1], lo[:], 1.0, None, ALU.add)
                    dve.tensor_copy(fields[plan][:, :, 2], w_f[:])
                link(dve.tensor_copy(w_half[:], w_f[:]))
                link(dve.tensor_copy(w_part[:, 0], w_half[:]))
                link(dve.tensor_tensor(w_rest[:], w_f[:], w_part[:, 0], ALU.subtract))
                link(dve.tensor_copy(w_half[:], w_rest[:]))
                link(dve.tensor_copy(w_part[:, 1], w_half[:]))
                link(dve.tensor_tensor(w_part[:, 2], w_rest[:], w_part[:, 1], ALU.subtract))
                link(dve.tensor_scalar(w_rest[:], dst_hi[:], 0.0, None, ALU.is_lt))
                link(dve.tensor_scalar(pad_at[:], w_rest[:], pcol[:, 0:1], None, ALU.mult))
                dve.scalar_tensor_tensor(pad_at[:], w_rest[:], float(TRASH), pad_at[:], ALU.mult, ALU.add)

        RING = 8
        oh_dst = tmp("oh_dst", [P, RING, T], BF16)
        oh_src = tmp("oh_src", [P, RING, T], BF16)
        lo_dst = tmp("lo_dst", [P, RING, P], BF16)
        lo_src = tmp("lo_src", [P, RING, P], BF16)
        lo_w = tmp("lo_w", [P, RING, 3, P], BF16)
        in_count, in_weight, out_count = psA[:, 0, 0:T], psA[:, 1, 0:T], psT[:, 0, 0:T]
        with phase(nc, "onehots", "weighted", "counted", "fill_out") as (block, (onehots, weighted, counted, fill_out)):
            @block.sync
            def _(sp):
                rows = (TRASH + P) // P
                n = 0
                for edge_table in by_dst.tables + by_src.tables:
                    fills = edge_table.rearrange("(a r) f -> a r f", a=P)
                    for r in range(0, rows, 2 * P):
                        m = min(2 * P, rows - r)
                        sp.dma_start(fills[:, r:r + m, :], table_fill[:, 0:m, :]).then_inc(fill_out, 16)
                        n += 16
                sp.dma_start(overflow_sums[XB], zeros[:]).then_inc(fill_out, 16)
                sp.wait_ge(fill_out, n + 16)

            @block.vector
            def _(dve):
                def step(i, k):
                    c, r = U * i + k, k % RING
                    need(dve, counted, c - RING + 1)
                    dve.tensor_scalar(lo_dst[:, r], iota_h[:, 0:P], dst_lo[:, bass.ds(c, 1)], None,
                                      ALU.is_equal).then_inc(onehots, 1)
                    dve.tensor_scalar(oh_dst[:, r], iota_h[:, 0:T], dst_hi[:, bass.ds(c, 1)], None, ALU.is_equal)
                    dve.tensor_scalar(oh_src[:, r], iota_h[:, 0:T], src_hi[:, bass.ds(c, 1)], None, ALU.is_equal)
                    dve.tensor_scalar(lo_src[:, r], iota_h[:, 0:P], src_lo[:, bass.ds(c, 1)], None,
                                      ALU.is_equal).then_inc(onehots, 1)
                sweep(dve, C, 0, step, 0)

            @block.scalar
            def _(act):
                def step(i, k):
                    c, r = U * i + k, k % RING
                    act.wait_ge(onehots, 2 * c + 1)
                    need(act, counted, c - RING + 1)
                    for j in range(3):
                        last = act.activation(lo_w[:, r, j], lo_dst[:, r], ACT.Copy,
                                              scale=w_part[:, j, bass.ds(c, 1)])
                    last.then_inc(weighted, 1)
                sweep(act, C, 0, step, 0)

            @block.tensor
            def _(pe):
                def step(i, k):
                    c, r = U * i + k, k % RING
                    at_start = isinstance(i, int) and i == 0 and k == 0
                    at_end = isinstance(i, int) and i == C // U - 1 and k == U - 1
                    pe.wait_ge(onehots, 2 * c + 2)
                    pe.matmul(in_count, lo_dst[:, r], oh_dst[:, r], start=at_start, stop=at_end)
                    pe.matmul(out_count, lo_src[:, r], oh_src[:, r], start=at_start, stop=at_end)
                    pe.wait_ge(weighted, c + 1)
                    for j in range(3):
                        last = pe.matmul(in_weight, lo_w[:, r, j], oh_dst[:, r], start=at_start and j == 0,
                                         stop=at_end and j == 2)
                    last.then_inc(counted, 1)
                sweep(pe, C, 0, step, 0)

        in_sb = tmp("in_sb", [P, T])
        deg = tmp("deg", [P, T])
        row_i = tmp("row_i", [P, T], I32)
        seed = tmp("seed", [P, T])
        ranks = [psO[:, 0, 0:T], psO[:, 1, 0:T]]
        with phase(nc, "degrees", "rooted", "dve_done") as (block, (degrees, rooted, dve_done)):
            @block.scalar
            def _(act):
                act.wait_ge(degrees, 1)
                act.activation(dinv[:], dinv[:], ACT.Sqrt)
                act.activation(root_out[:], root_out[:], ACT.Sqrt).then_inc(rooted, 1)

            @block.vector
            def _(dve):
                steps = [0]

                def link(ins):
                    steps[0] += 1
                    ins.then_inc(dve_done, 1)
                    dve.wait_ge(dve_done, steps[0])

                dve.tensor_copy(in_sb[:], in_count)
                link(dve.tensor_copy(out_sb[:], out_count))
                for plan in (by_dst, by_src):
                    for a in (plan.overflow, plan.upto, plan.first, plan.base):
                        dve.memset(a[:], 0.0)
                link(dve.tensor_scalar(deg[:], in_weight, 1.0, None, ALU.add))
                dve.tensor_scalar(dinv[:], deg[:], 1e-30, None, ALU.max)
                dve.tensor_scalar(root_out[:], out_sb[:], 1.0, None, ALU.max).then_inc(degrees, 1)
                dve.wait_ge(rooted, 1)
                link(dve.tensor_scalar(deg[:], deg[:], 0.0, None, ALU.is_gt))
                dve.tensor_copy(root_deg[:], root_out[:])
                link(dve.reciprocal(dinv[:], dinv[:]))
                dve.reciprocal(root_out[:], root_out[:])
                link(dve.tensor_tensor(dinv[:], dinv[:], deg[:], ALU.mult))
                dve.tensor_scalar(has_in[:], in_sb[:], 0.0, None, ALU.is_gt)
                link(dve.tensor_scalar(inv_deg[:], in_sb[:], 1.0, None, ALU.max))
                link(dve.reciprocal(inv_deg[:], inv_deg[:]))
                link(dve.tensor_tensor(inv_deg[:], inv_deg[:], has_in[:], ALU.mult))
                dve.tensor_tensor(has_in[:], has_in[:], root_out[:], ALU.mult)

        def place_tiles(plan, counts, seed, row_i, deg):
            with phase(nc, "totals", "seed_made", "dve_done") as (block, (totals, seed_made, dve_done)):
                @block.tensor
                def _(pe):
                    pe.matmul(psM[:, 0, 0:T], ones_f[:], counts[:], start=True, stop=True).then_inc(totals, 1)
                    pe.wait_ge(seed_made, 1)
                    for rank in ranks:
                        pe.matmul(rank, ones_f[0:1, :], seed[0:1, :], start=True, stop=True)

                @block.vector
                def _(dve):
                    steps = [0]

                    def link(ins):
                        steps[0] += 1
                        ins.then_inc(dve_done, 1)
                        dve.wait_ge(dve_done, steps[0])

                    overflow, upto, first, base = [a[:, 0:T] for a in (plan.overflow, plan.upto, plan.first, plan.base)]
                    dve.wait_ge(totals, 1)
                    link(dve.tensor_scalar(row_i[:], psM[:, 0, 0:T], 1.0, -1.0, ALU.max, ALU.add))
                    link(dve.tensor_scalar(row_i[:], row_i[:], 7, None, ALU.arith_shift_right))
                    link(dve.tensor_copy(overflow, row_i[:]))
                    link(dve.tensor_tensor_scan(upto, ones_row[:, 0:T], overflow, 0.0, ALU.mult, ALU.add))
                    link(dve.tensor_tensor(first, upto, overflow, ALU.subtract))
                    link(dve.tensor_tensor(base, first, iota_f[:, 0:T], ALU.add))
                    dve.tensor_scalar(seed[:], base, float(P), None, ALU.mult).then_inc(seed_made, 1)
                    link(dve.tensor_scalar(deg[:], overflow, 0.0, None, ALU.is_gt))
                    link(dve.scalar_tensor_tensor(deg[:], upto, -1.0 - XB, deg[:], ALU.add, ALU.mult))
                    dve.tensor_scalar(plan.sums_at[:], deg[:], float(XB), None, ALU.add)
                    link(dve.tensor_scalar(row_i[:, 0:1], plan.upto[:, T - 1:T], -1.0, 2.0 * XU, ALU.add, ALU.max))
                    assert XU == 8
                    dve.tensor_scalar(plan.x_last[:], row_i[:, 0:1], 3, None, ALU.arith_shift_right)

        class Placer:

            def __init__(self, plan, key_hi, bufs, sems, scattered):
                self.plan, self.key_hi = plan, key_hi
                self.onehots, self.junk, self.rank8, self.row_at, self.staged = bufs
                self.onehot, self.rank_ready, self.rank_read, self.places, self.fields_staged, self.ones_used = sems
                self.scattered = scattered
                self.ring = self.onehots.shape[1]

            def count(self, pe, i, k):
                c, mine, other = U * i + k, ranks[k % 2], ranks[(k + 1) % 2]
                slot, last_slot = self.onehots[:, k % self.ring], self.onehots[:, (k - 1) % self.ring]
                pe.wait_ge(self.onehot, c + 1)
                pe.matmul(mine, before[:], slot, start=False, stop=True, skip_group_check=True).then_inc(
                    self.rank_ready, 1)
                need(pe, self.rank_read, c)
                if not (isinstance(c, int) and c == 0):
                    pe.matmul(other, not_before[:], last_slot, start=False, stop=True, skip_group_check=True)
                pe.matmul(other, ones_b[:], slot, start=False, stop=True, skip_group_check=True).then_inc(
                    self.ones_used, 1)

            def set_onehot(self, dve, i, k):
                c = U * i + k
                if isinstance(c, int) and not 0 <= c < C:
                    return
                need(dve, self.ones_used, c - self.ring + 2)
                dve.tensor_scalar(self.onehots[:, k % self.ring], iota_h[:, 0:T], self.key_hi[:, bass.ds(c, 1)], None,
                                  ALU.is_equal).then_inc(self.onehot, 1)

            def read_rank(self, dve, i, k):
                c, h = U * i + k, k // 4
                dve.wait_ge(self.rank_ready, c + 1)
                dve.wait_ge(self.onehot, c + 1)
                need(dve, self.rank_read, c)
                dve.tensor_tensor_reduce(self.junk[:], ranks[k % 2], self.onehots[:, k % self.ring], 1.0, 0.0, ALU.mult,
                                         ALU.add, self.rank8[:, k:k + 1]).then_inc(self.rank_read, 1)
                if k % 4 == 3:
                    for j in range(4 * h, 4 * h + 4):
                        slot_freed(dve, self.scattered[j], i, 0)
                    dve.wait_ge(self.rank_read, c + 1)
                    dve.tensor_tensor(self.row_at[:, 4 * h:4 * h + 4], self.rank8[:, 4 * h:4 * h + 4],
                                      pad_at[:, bass.ds(U * i + 4 * h, 4)], ALU.add).then_inc(self.places, 1)

            def scatter(self, pool, i, k):
                if k % 4 == 0:
                    for j in range(k, k + 4):
                        slot_freed(pool, self.scattered[j], i, 0)
                    pool.tensor_copy(self.staged[:, k:k + 4, :], fields[self.plan][:, bass.ds(U * i + k, 4), :]).then_inc(
                        self.fields_staged, 1)
                    pool.wait_ge(self.fields_staged, 2 * i + k // 4 + 1)
                    pool.wait_ge(self.places, 2 * i + k // 4 + 1)
                    take_waits(pool)
                pool.indirect_dma_start(self.plan.tables[k], bass.IndirectOffsetOnAxis(ap=self.row_at[:, k:k + 1], axis=0),
                                        self.staged[:, k, :], None).then_inc(self.scattered[k], 16)

            def end(self, pool):
                for scattered in self.scattered:
                    pool.wait_ge(scattered, 16 * (C // U))

        rank8 = tmp("rank8", [P, U])
        junk_t = tmp("junk_t", [P, T])
        row_at = tmp("row_at", [P, U], I32)
        staged = tmp("staged", [P, U, 4])
        xin = tmp("xin", [P, 4, 2, ROW])
        junk_d = tmp("junk_d", [P, D])
        score8 = tmp("score8", [P, 2, 4])
        x_pairs = x[0:(N // (2 * P)) * 2 * P, :].rearrange("(g k p) d -> g p k d", k=2, p=P)
        t0_pairs = table0.rearrange("(g k p) d -> g p k d", k=2, p=P)
        WHOLE_PAIRS = N // (2 * P)

        def place_edges(plan, key_hi):
            with phase(nc, f"{plan.name}_onehot", "rank_ready", "rank_read", "places", "fields_staged", "ones_used",
                       "dots", "dots_kept", "pad_zero", "coef_set", *[f"x_in{k}" for k in range(4)],
                       *[f"t0_out{k}" for k in range(4)]) as (block, sems):
                dots, dots_kept, pad_zero, coef_set, *dmas = sems[6:]
                x_in, t0_out = dmas[0:4], dmas[4:8]
                placer = Placer(plan, key_hi, (oh_dst, junk_t, rank8, row_at, staged), sems[0:6], gathered_m)

                @block.tensor
                def _(pe):
                    sweep(pe, C, 0, lambda i, k: placer.count(pe, i, k), 0)

                @block.vector
                def _(dve):
                    def step(i, k):
                        placer.set_onehot(dve, *tile_at(i, k + 3))
                        if k < 0:
                            return
                        c, h, q = U * i + k, k // 4, k % 4
                        placer.read_rank(dve, i, k)
                        if isinstance(c, int) and c == T - U:
                            dve.wait_ge(t0_out[3], 16 * (T // U - 1))
                            dve.memset(xin[:, 3], 0.0).then_inc(pad_zero, 1)
                        dve.wait_ge(x_in[k // 2], 16 * (i + 1))
                        need(dve, dots, c)
                        dve.tensor_tensor_reduce(junk_d[:], xin[:, k // 2, k % 2, 0:D], p_row[:], 1.0, 0.0, ALU.mult,
                                                 ALU.add, score8[:, h, q:q + 1]).then_inc(dots, 1)
                        if q == 3:
                            dve.wait_ge(dots, U * i + k + 1)
                            dve.tensor_copy(score[:, bass.ds(U * i + 4 * h, 4)], score8[:, h]).then_inc(dots_kept, 1)
                    sweep(dve, C, 3, step, 0)

                @block.gpsimd
                def _(pool):
                    sweep(pool, C, 0, lambda i, k: placer.scatter(pool, i, k), 0)
                    placer.end(pool)

                @block.sync
                def _(sp):
                    def step(i, k):
                        if k % 2:
                            return
                        g, r = 4 * i + k // 2, k // 2
                        need(sp, t0_out[r], 16 * i)
                        if isinstance(g, int) and g >= WHOLE_PAIRS:
                            if g == WHOLE_PAIRS:
                                sp.wait_ge(pad_zero, 1)
                                sp.dma_start(xin[0:REST, r, 0, 0:D], x[N - REST:N, :]).then_inc(x_in[r], 16)
                            return
                        sp.dma_start(xin[:, r, :, 0:D], x_pairs[g]).then_inc(x_in[r], 16)
                    sweep(sp, T, 0, step, 0)

                @block.scalar
                def _(act):
                    def step(i, k):
                        if k % 2 == 0:
                            return
                        g, r, t = 4 * i + k // 2, k // 2, U * i + k - 1
                        need(act, t0_out[r], 16 * i)
                        act.copy(xin[:, r, :, D], dinv[:, bass.ds(t, 2)]).then_inc(coef_set, 1)
                        act.wait_ge(coef_set, g + 1)
                        act.wait_ge(dots, U * i + k + 1)
                        act.dma_start(t0_pairs[g], xin[:, r]).then_inc(t0_out[r], 16)
                    sweep(act, T, 0, step, 0)
                    for r in range(4):
                        act.wait_ge(t0_out[r], 16 * (T // U))

        place_tiles(by_dst, in_sb, seed, row_i, deg)
        place_edges(by_dst, dst_hi)
        early.close()
        before_now = [C // U] * U

        mid = ExitStack()

        def tmp(name, shape, dt=F32):
            return mid.enter_context(nc.sbuf_tensor(name, shape, dt))

        def list_chunks(plan, uses):
            held = ExitStack()

            def tmp(name, shape, dt=F32):
                return held.enter_context(nc.sbuf_tensor(name, shape, dt))

            main_at = tmp(f"{plan.name}_main_at", [P, TB], I32)
            extra_at = tmp(f"{plan.name}_extra_at", [P, TB], I32)
            first_col = tmp(f"{plan.name}_first_col", [P, TB])
            has_over = tmp(f"{plan.name}_has_over", [P, TB, P])
            starts = tmp(f"{plan.name}_starts", [P, TB, TW])
            x_num = tmp(f"{plan.name}_x_num", [P, TB])
            before_x = tmp(f"{plan.name}_before_x", [P, T])
            tile_of = tmp(f"{plan.name}_tile_of", [P, TB])
            table_rows = tmp(f"{plan.name}_table_rows", [P, 2, U, 4 * P])
            chunk_rows = tmp(f"{plan.name}_chunk_rows", [P, 2, 4 * P])

            edge_chunks = [e[0:SLOTS * P, :].rearrange("(v e) f -> v (e f)", e=P) for e in plan.tables]
            with phase(nc, "cols_made", "cols_read", "lists_made", "fields_made", "fields_read", "starts_made",
                       "carried", "rows_summed", "dve_done") as (
                    block, (cols_made, cols_read, lists_made, fields_made, fields_read, starts_made, carried,
                            rows_summed, dve_done)):
                jobs = [(b, half) for half in range(2) for b in range(TB)]

                @block.tensor
                def _(pe):
                    for b in range(TB):
                        at = slice(b * P, b * P + P)
                        need(pe, cols_read, b)
                        for j, row in enumerate((plan.base, plan.first, plan.overflow)):
                            last = pe.transpose(psM[:, 0, j * P:j * P + P], row[:, at], ident[:])
                        last.then_inc(cols_made, 1)
                    for b in range(TB):
                        pe.wait_ge(starts_made, b + 1)
                        last = pe.matmul(psT[:, 0, 0:TW], has_over[:, b], starts[:, b], start=b == 0, stop=b == TB - 1)
                    last.then_inc(carried, 1)
                    for n, (b, half) in enumerate(jobs):
                        pe.wait_ge(rows_summed, n + 1)
                        rows = chunk_rows[:, n % 2].rearrange("v (e f) -> v f e", f=4)
                        need(pe, fields_read, n - 1)
                        for f in range(3):
                            last = pe.transpose(psO[:, n % 2, f * P:f * P + P], rows[:, f], ident[:])
                        last.then_inc(fields_made, 1)

                @block.vector
                def _(dve):
                    steps = [0]

                    def link(ins):
                        steps[0] += 1
                        ins.then_inc(dve_done, 1)
                        dve.wait_ge(dve_done, steps[0])

                    for b in range(TB):
                        dve.wait_ge(cols_made, b + 1)
                        dve.tensor_copy(main_at[:, b:b + 1], psM[:, 0, 0:1])
                        dve.tensor_copy(first_col[:, b:b + 1], psM[:, 0, P:P + 1])
                        dve.tensor_scalar(has_over[:, b], psM[:, 0, 2 * P:3 * P], 0.0, None, ALU.is_gt).then_inc(cols_read, 1)
                    dve.wait_ge(cols_read, TB)
                    for b in range(TB):
                        link(dve.tensor_scalar(x_num[:, b:b + 1], pcol[:], float(b * P), None, ALU.add))
                        link(dve.tensor_scalar(before_x[:], plan.upto[:, 0:T], x_num[:, b:b + 1], None, ALU.is_le))
                        link(dve.tensor_reduce(tile_of[:, b:b + 1], before_x[:], AX.X, ALU.add))
                        link(dve.scalar_tensor_tensor(extra_at[:, b:b + 1], tile_of[:, b:b + 1], 1.0, x_num[:, b:b + 1],
                                                      ALU.add, ALU.add))
                    dve.tensor_scalar(x_num[:, 0:1], pcol[:], 0.0, None, ALU.add).then_inc(lists_made, 1)
                    for b in range(TB):
                        dve.tensor_scalar(starts[:, b], iota_f[:], first_col[:, b:b + 1], None, ALU.is_equal).then_inc(
                            starts_made, 1)
                    dve.wait_ge(carried, 1)
                    dve.tensor_scalar(plan.carry[:], psT[:, 0, 0:TW], -1.0, 1.0, ALU.mult, ALU.add)
                    def copy_fields(n):
                        b, half = jobs[n]
                        at = slice(b * P, b * P + P)
                        to_src, to_lo, to_w = (plan.main, plan.extra)[half]
                        dve.wait_ge(fields_made, n + 1)
                        dve.tensor_copy(to_src[:, at], psO[:, n % 2, 0:P])
                        dve.tensor_scalar(to_lo[:, at], psO[:, n % 2, P:2 * P], -1.0, None, ALU.add)
                        dve.tensor_copy(to_w[:, at], psO[:, n % 2, 2 * P:3 * P]).then_inc(fields_read, 1)

                    for n in range(len(jobs)):
                        if n >= 2:
                            copy_fields(n - 2)
                        dve.wait_ge(gathered_m[n % 2], 16 * (uses[n % 2] + U * (n // 2 + 1)))
                        dve.tensor_reduce(chunk_rows[:, n % 2], table_rows[:, n % 2].rearrange("v k x -> v x k"), AX.X,
                                          ALU.add).then_inc(rows_summed, 1)
                    for n in range(len(jobs) - 2, len(jobs)):
                        copy_fields(n)

                @block.gpsimd
                def _(pool):
                    pool.wait_ge(lists_made, 1)
                    for n, (b, half) in enumerate(jobs):
                        at = (main_at, extra_at)[half]
                        need(pool, rows_summed, n - 1)
                        for k in range(U):
                            pool.indirect_dma_start(table_rows[:, n % 2, k], None, edge_chunks[k],
                                                    bass.IndirectOffsetOnAxis(ap=at[:, b:b + 1], axis=0)).then_inc(
                                gathered_m[n % 2], 16)

            held.close()
            before_now[:] = [n + U * TB * (k < 2) for k, n in enumerate(before_now)]

        list_chunks(by_dst, list(before_now))

        bits = score[:].bitcast(I32)
        key_i = tmp("key_i", [P, T], I32)
        half_i = tmp("half_i", [P, T], I32)
        key_hi = tmp("key_hi", [P, T])
        key_lo = tmp("key_lo", [P, T])
        real = tmp("real", [P, T])
        hits = tmp("hits", [P, T])
        count = tmp("count", [P, 1])
        wanted = tmp("wanted", [P, 1])
        best_hi = tmp("best_hi", [P, 1])
        best_lo = tmp("best_lo", [P, 1])
        unit = tmp("unit", [P, 1])
        trial = tmp("trial", [P, 1])
        taken = tmp("taken", [P, 1])
        above = tmp("above", [P, T], BF16)
        equal = tmp("equal", [P, T], BF16)
        tmp_t = tmp("tmp_t", [P, T])
        col_sum = tmp("col_sum", [P, T])
        place = tmp("place", [P, T])
        place_eq = tmp("place_eq", [P, T])
        pair_of = tmp("pair_of", [P, T, 2], FP16)

        HALF = 16
        with phase(nc, "counts", "total", "dve_done", "loop_done") as (block, (counts, total, dve_done, loop_done)):
            @block.tensor
            def _(pe):
                for half in range(2):
                    with pe.Fori(0, HALF) as j:
                        n = (HALF + 1) * half + j
                        pe.wait_ge(counts, n + 1)
                        pe.matmul(psM[:, 0, 0:1], ones_f[:], count[:], start=True, stop=True).then_inc(total, 1)
                    n = (HALF + 1) * half + HALF
                    pe.wait_ge(counts, n + 1)
                    pe.matmul(psM[:, 0, 0:1], ones_f[:], count[:], start=True, stop=True).then_inc(total, 1)

            @block.vector
            def _(dve):
                steps = [0]

                def link(ins):
                    steps[0] += 1
                    ins.then_inc(dve_done, 1)
                    dve.wait_ge(dve_done, steps[0])

                def bisect(keys, best, half):
                    link(dve.memset(best[:], 0.0))
                    link(dve.memset(unit[:], float(1 << (HALF - 1))))
                    with dve.Fori(0, HALF) as j:
                        n, m = (HALF + 1) * half + j, 5 * (HALF * half + j)
                        dve.tensor_scalar(trial[:], best[:], unit[:, 0:1], None, ALU.add).then_inc(loop_done, 1)
                        dve.wait_ge(loop_done, m + 1)
                        dve.tensor_scalar(hits[:], keys[:], trial[:, 0:1], None, ALU.is_ge).then_inc(loop_done, 1)
                        dve.wait_ge(loop_done, m + 2)
                        dve.tensor_reduce(count[:], hits[:], AX.X, ALU.add).then_inc(counts, 1)
                        dve.wait_ge(total, n + 1)
                        dve.scalar_tensor_tensor(taken[:], psM[:, 0, 0:1], wanted[:, 0:1], unit[:], ALU.is_ge,
                                                 ALU.mult).then_inc(loop_done, 1)
                        dve.wait_ge(loop_done, m + 3)
                        dve.tensor_tensor(best[:], best[:], taken[:], ALU.add).then_inc(loop_done, 1)
                        dve.tensor_scalar(unit[:], unit[:], 0.5, None, ALU.mult).then_inc(loop_done, 1)
                        dve.wait_ge(loop_done, m + 5)
                    link(dve.tensor_scalar(hits[:], keys[:], best[:, 0:1], None, ALU.is_gt))
                    dve.tensor_reduce(count[:], hits[:], AX.X, ALU.add).then_inc(counts, 1)
                    dve.wait_ge(total, (HALF + 1) * half + HALF + 1)
                    link(dve.scalar_tensor_tensor(wanted[:], psM[:, 0, 0:1], -1.0, wanted[:], ALU.mult, ALU.add))

                link(dve.tensor_scalar(key_i[:], bits, 31, None, ALU.arith_shift_right))
                link(dve.tensor_scalar(key_i[:], key_i[:], -2147483648, None, ALU.bitwise_or))
                link(dve.tensor_tensor(key_i[:], key_i[:], bits, ALU.bitwise_xor))
                link(dve.tensor_scalar(half_i[:], key_i[:], HALF, 0xFFFF, ALU.logical_shift_right, ALU.bitwise_and))
                link(dve.tensor_copy(key_hi[:], half_i[:]))
                link(dve.tensor_scalar(half_i[:], key_i[:], 0xFFFF, None, ALU.bitwise_and))
                link(dve.tensor_copy(key_lo[:], half_i[:]))
                link(dve.tensor_scalar(tmp_t[:], iota_f[:, 0:T], float(P), pcol[:, 0:1], ALU.mult, ALU.add))
                link(dve.tensor_scalar(real[:], tmp_t[:], float(N), None, ALU.is_lt))
                link(dve.scalar_tensor_tensor(key_hi[:], key_hi[:], 1.0, real[:], ALU.add, ALU.mult))
                link(dve.tensor_scalar(key_hi[:], key_hi[:], -1.0, None, ALU.add))
                link(dve.memset(wanted[:], float(K)))
                bisect(key_hi, best_hi, 0)
                link(dve.tensor_scalar(above[:], key_hi[:], best_hi[:, 0:1], None, ALU.is_gt))
                link(dve.tensor_scalar(hits[:], key_hi[:], best_hi[:, 0:1], None, ALU.is_equal))
                link(dve.scalar_tensor_tensor(key_lo[:], key_lo[:], 1.0, hits[:], ALU.add, ALU.mult))
                link(dve.tensor_scalar(key_lo[:], key_lo[:], -1.0, None, ALU.add))
                bisect(key_lo, best_lo, 1)
                link(dve.tensor_scalar(hits[:], key_lo[:], best_lo[:, 0:1], None, ALU.is_gt))
                dve.tensor_tensor(above[:], above[:], hits[:], ALU.add)
                dve.tensor_scalar(equal[:], key_lo[:], best_lo[:, 0:1], None, ALU.is_equal)
                dve.tensor_copy(pair_of[:, :, 0], iota_f[:, 0:T])
                dve.tensor_copy(pair_of[:, :, 1], pcol[:, 0:1].to_broadcast([P, T]))

        with phase(nc, "prefixed", "dve_done") as (block, (prefixed, dve_done)):
            @block.tensor
            def _(pe):
                for j, mask in enumerate((above, equal)):
                    pe.matmul((psM, psO)[j][:, 0, 0:T], before[:], mask[:], start=True, stop=True)
                    last = pe.matmul((psM, psO)[j][:, 1, 0:T], ones_b[:], mask[:], start=True, stop=True)
                last.then_inc(prefixed, 1)

            @block.vector
            def _(dve):
                steps = [0]

                def link(ins):
                    steps[0] += 1
                    ins.then_inc(dve_done, 1)
                    dve.wait_ge(dve_done, steps[0])

                dve.wait_ge(prefixed, 1)
                for ps, to in ((psM, place), (psO, place_eq)):
                    link(dve.tensor_copy(tmp_t[:], ps[:, 1, 0:T]))
                    link(dve.tensor_tensor_scan(col_sum[:], ones_row[:, 0:T], tmp_t[:], 0.0, ALU.mult, ALU.add))
                    if ps is psM:
                        link(dve.tensor_copy(count[:], col_sum[:, T - 1:T]))
                    link(dve.tensor_tensor(col_sum[:], col_sum[:], tmp_t[:], ALU.subtract))
                    link(dve.tensor_tensor(to[:], ps[:, 0, 0:T], col_sum[:], ALU.add))
                link(dve.scalar_tensor_tensor(place[:], place[:], 1.0, above[:], ALU.add, ALU.mult))
                link(dve.tensor_scalar(hits[:], place_eq[:], wanted[:, 0:1], None, ALU.is_lt))
                link(dve.tensor_tensor(hits[:], hits[:], equal[:], ALU.mult))
                link(dve.tensor_scalar(count[:], count[:], 1.0, None, ALU.add))
                link(dve.scalar_tensor_tensor(place_eq[:], place_eq[:], count[:, 0:1], hits[:], ALU.add, ALU.mult))
                link(dve.tensor_tensor(place[:], place[:], place_eq[:], ALU.add))
                dve.tensor_scalar(place[:], place[:], -1.0, None, ALU.add)

        picks = tmp("picks", [P, RING, K], FP16)
        picked = [psM[:, 0, 0:2], psM[:, 1, 0:2]]
        with phase(nc, "picks_made", "picks_used") as (block, (picks_made, picks_used)):
            @block.vector
            def _(dve):
                def step(i, k):
                    c = U * i + k
                    need(dve, picks_used, c - RING + 1)
                    dve.tensor_scalar(picks[:, k % RING], iota_h[:, 0:K], place[:, bass.ds(c, 1)], None,
                                      ALU.is_equal).then_inc(picks_made, 1)
                sweep(dve, T, 0, step, 0)

            @block.tensor
            def _(pe):
                def step(i, k):
                    c = U * i + k
                    at_start = isinstance(c, int) and c == 0
                    at_end = isinstance(c, int) and c == T - 1
                    pe.wait_ge(picks_made, c + 1)
                    for b in range(K // P):
                        last = pe.matmul(picked[b], picks[:, k % RING, b * P:b * P + P],
                                         pair_of[:, bass.ds(c, 1), :].rearrange("p a b -> p (a b)"),
                                         start=at_start, stop=at_end)
                    last.then_inc(picks_used, 1)
                sweep(pe, T, 0, step, 0)

        KB = K // P
        node = tmp("node", [P, KB])
        node_i = tmp("node_i", [P, KB], I32)
        pick_rows = tmp("pick_rows", [P, KB, ROW])
        pick_dot = tmp("pick_dot", [P, KB])
        norm = tmp("norm", [P, 1])
        tanh_s = tmp("tanh_s", [P, KB])
        shared = tmp("shared", [P, 2, KB, P])
        rows_sn = tmp("rows_sn", [P, 2, K])
        greater = tmp("greater", [P, K])
        same = tmp("same", [P, K])
        rank = tmp("rank", [P, KB])
        order = tmp("order", [P, KB, K])
        w_ih = tmp("w_ih", [P, 6, D])
        w_hh = tmp("w_hh", [P, 6, D])
        w_ih_t = tmp("w_ih_t", [P, DB, 3 * D])
        w_hh_t = tmp("w_hh_t", [P, DB, 3 * D])
        w0 = tmp("w0", [P, DB, D])
        w0_t = tmp("w0_t", [P, DB, D])
        x_t = tmp("x_t", [P, DB, K])
        bih_row = tmp("bih_row", [P, 3 * D])
        bhh_row = tmp("bhh_row", [P, 3 * D])
        gate = tmp("gate", [P, KB, 2 * D])
        cand = tmp("cand", [P, KB, D])
        hid = tmp("hid", [P, KB, D])

        with phase(nc, "nodes_made", "w_in", "dots_made", "tanhs", "shared_made", "turned", "dve_done",
                   "w_turned", "w_copied", "ordered", "norm_made") as (
                block, (nodes_made, w_in, dots_made, tanhs, shared_made, turned, dve_done, w_turned, w_copied,
                        ordered, norm_made)):
            @block.sync
            def _(sp):
                sp.dma_start(w_ih[:], W_ih.rearrange("(b p) d -> p b d", p=P)).then_inc(w_in, 16)
                sp.dma_start(w_hh[:], W_hh.rearrange("(b p) d -> p b d", p=P)).then_inc(w_in, 16)
                sp.dma_start(w0[:], W0.rearrange("(b p) d -> p b d", p=P)).then_inc(w_in, 16)
                for to, what in ((bih_row, b_ih), (bhh_row, b_hh)):
                    sp.dma_start(to[:], what.rearrange("(a d) -> a d", a=1).to_broadcast([P, 3 * D])).then_inc(w_in, 16)
                sp.wait_ge(w_in, 16 * 5)

            @block.gpsimd
            def _(pool):
                pool.wait_ge(nodes_made, 1)
                for b in range(KB):
                    pool.indirect_dma_start(pick_rows[:, b], None, table0,
                                            bass.IndirectOffsetOnAxis(ap=node_i[:, b:b + 1], axis=0)).then_inc(
                        gathered_m[0], 16)

            turns = [(w_ih, w_ih_t, o) for o in range(6)] + [(w_hh, w_hh_t, o) for o in range(6)] + \
                    [(w0, w0_t, o) for o in range(DB)]

            @block.vector
            def _(dve):
                steps = [0]

                def link(ins):
                    steps[0] += 1
                    ins.then_inc(dve_done, 1)
                    dve.wait_ge(dve_done, steps[0])

                for b in range(KB):
                    link(dve.tensor_copy(tmp_t[:, 0:2], picked[b]))
                    link(dve.scalar_tensor_tensor(node[:, b:b + 1], tmp_t[:, 0:1], float(P), tmp_t[:, 1:2], ALU.mult,
                                                  ALU.add))
                dve.tensor_copy(node_i[:], node[:]).then_inc(nodes_made, 1)
                link(dve.tensor_tensor_reduce(greater[:], p_row[:], p_row[:], 1.0, 0.0, ALU.mult, ALU.add, norm[:]))
                dve.tensor_copy(norm[:], norm[:]).then_inc(norm_made, 1)
                dve.wait_ge(norm_made, 2)
                link(dve.reciprocal(norm[:], norm[:]))
                dve.wait_ge(gathered_m[0], 16 * (before_now[0] + KB))
                for b in range(KB):
                    link(dve.tensor_tensor_reduce(greater[:], pick_rows[:, b, 0:D], p_row[:], 1.0, 0.0, ALU.mult, ALU.add,
                                                  pick_dot[:, b:b + 1]))
                dve.tensor_copy(rank[:], pick_dot[:]).then_inc(dots_made, 1)
                for b in range(KB):
                    dve.tensor_scalar(shared[:, 0, b], ones_f[:], pick_dot[:, b:b + 1], None, ALU.mult)
                    last = dve.tensor_scalar(shared[:, 1, b], ones_f[:], node[:, b:b + 1], None, ALU.mult)
                last.then_inc(shared_made, 1)
                dve.wait_ge(turned, 1)
                link(dve.tensor_copy(rows_sn[:].rearrange("p a k -> p (a k)"), psA[:, 0, :]))
                for b in range(KB):
                    link(dve.tensor_scalar(greater[:], rows_sn[:, 0], pick_dot[:, b:b + 1], None, ALU.is_gt))
                    link(dve.tensor_scalar(same[:], rows_sn[:, 0], pick_dot[:, b:b + 1], None, ALU.is_equal))
                    link(dve.scalar_tensor_tensor(same[:], rows_sn[:, 1], node[:, b:b + 1], same[:], ALU.is_lt, ALU.mult))
                    link(dve.tensor_tensor(same[:], same[:], greater[:], ALU.add))
                    link(dve.tensor_reduce(rank[:, b:b + 1], same[:], AX.X, ALU.add))
                    link(dve.tensor_scalar(order[:, b], iota_f[:, 0:K], rank[:, b:b + 1], None, ALU.is_equal))
                dve.wait_ge(tanhs, 1)
                for b in range(KB):
                    link(dve.tensor_scalar(pick_rows[:, b, 0:D], pick_rows[:, b, 0:D], tanh_s[:, b:b + 1], None, ALU.mult))
                dve.tensor_copy(count[:], norm[:]).then_inc(ordered, 1)
                for n, (_, to, o) in enumerate(turns):
                    dve.wait_ge(w_turned, n + 1)
                    for b in range(DB):
                        last = dve.tensor_copy(to[:, b, o * P:o * P + P], psT[:, n % 2, b * P:b * P + P])
                    last.then_inc(w_copied, 1)
                dve.wait_ge(ordered, 2)
                for b in range(DB):
                    dve.tensor_copy(x_t[:, b], psO[:, b, 0:K])

            @block.scalar
            def _(act):
                act.wait_ge(norm_made, 1)
                act.activation(norm[:], norm[:], ACT.Sqrt).then_inc(norm_made, 1)
                act.wait_ge(dots_made, 1)
                act.activation(tanh_s[:], pick_dot[:], ACT.Tanh, scale=norm[:, 0:1]).then_inc(tanhs, 1)

            @block.tensor
            def _(pe):
                pe.wait_ge(shared_made, 1)
                for a in range(2):
                    for b in range(KB):
                        last = pe.transpose(psA[:, 0, (a * KB + b) * P:(a * KB + b + 1) * P], shared[:, a, b], ident[:])
                last.then_inc(turned, 1)
                pe.wait_ge(ordered, 1)
                for d in range(DB):
                    for b in range(KB):
                        last = pe.matmul(psO[:, d, 0:K], pick_rows[:, b, d * P:d * P + P], order[:, b], start=b == 0,
                                         stop=b == KB - 1)
                last.then_inc(ordered, 1)
                pe.wait_ge(w_in, 16 * 5)
                for n, (what, _, o) in enumerate(turns):
                    need(pe, w_copied, n - 1)
                    for b in range(DB):
                        last = pe.transpose(psT[:, n % 2, b * P:b * P + P], what[:, o, b * P:b * P + P], ident[:])
                    last.then_inc(w_turned, 1)

        with phase(nc, "products", "dve_done", "gates", "gated", "cands") as (
                block, (products, dve_done, gates, gated, cands)):
            @block.tensor
            def _(pe):
                for b in range(KB):
                    at = slice(b * P, b * P + P)
                    for n, (left, right) in enumerate([(x_t, w_ih_t), (w0_t, w_hh_t)]):
                        for d in range(DB):
                            pe.matmul(psA[:, b, 0:2 * D], left[:, d, at], right[:, d, 0:2 * D], start=n + d == 0,
                                      stop=n + d == DB)
                        for d in range(DB):
                            last = pe.matmul((psT, psO)[n][:, b, 0:D], left[:, d, at], right[:, d, 2 * D:3 * D],
                                             start=d == 0, stop=d == DB - 1)
                    last.then_inc(products, 1)

            @block.vector
            def _(dve):
                steps = [0]

                def link(ins):
                    steps[0] += 1
                    ins.then_inc(dve_done, 1)
                    dve.wait_ge(dve_done, steps[0])

                for b in range(KB):
                    dve.wait_ge(products, b + 1)
                    link(dve.tensor_tensor(gate[:, b], psA[:, b, 0:2 * D], bih_row[:, 0:2 * D], ALU.add))
                    dve.tensor_tensor(gate[:, b], gate[:, b], bhh_row[:, 0:2 * D], ALU.add).then_inc(gates, 1)
                    link(dve.tensor_tensor(cand[:, b], psT[:, b, 0:D], bih_row[:, 2 * D:], ALU.add))
                    link(dve.tensor_tensor(hid[:, b], psO[:, b, 0:D], bhh_row[:, 2 * D:], ALU.add))
                    dve.wait_ge(gated, b + 1)
                    link(dve.tensor_tensor(hid[:, b], hid[:, b], gate[:, b, 0:D], ALU.mult))
                    dve.tensor_tensor(cand[:, b], cand[:, b], hid[:, b], ALU.add).then_inc(gates, 1)
                    dve.wait_ge(cands, b + 1)
                    link(dve.tensor_tensor(hid[:, b], w0[:, b], cand[:, b], ALU.subtract))
                    link(dve.tensor_tensor(hid[:, b], hid[:, b], gate[:, b, D:2 * D], ALU.mult))
                    link(dve.tensor_tensor(w_gcn[:, b], hid[:, b], cand[:, b], ALU.add))

            @block.scalar
            def _(act):
                for b in range(KB):
                    act.wait_ge(gates, 2 * b + 1)
                    act.activation(gate[:, b], gate[:, b], ACT.Sigmoid).then_inc(gated, 1)
                    act.wait_ge(gates, 2 * b + 2)
                    act.activation(cand[:, b], cand[:, b], ACT.Tanh).then_inc(cands, 1)
        mid.close()
        before_now[0] += KB

        def layer_buffers(held, part):
            def tmp(name, shape, dt=F32):
                return held.enter_context(nc.sbuf_tensor(name, shape, dt))

            rows = tmp(f"rows_{part}", [P, U, ROW])
            gather_at = tmp(f"gather_at_{part}", [P, U], I32)
            select = tmp(f"select_{part}", [P, U, P])
            edge_coef = tmp(f"edge_coef_{part}", [P, U])
            running = tmp(f"running_{part}", [P, U, D])
            xb = tmp(f"xb_{part}", [P, 4, 2, ROW])
            diag = tmp(f"diag_{part}", [P, 4, P])
            rb = tmp(f"rb_{part}", [P, 4, 2, D])
            extra = running
            total_b = tmp(f"total_b_{part}", [P, 4, D])
            mixed = tmp(f"mixed_{part}", [P, 4, 2, D])
            turned_b = tmp(f"turned_b_{part}", [P, 4, 4, P])
            wb = tmp(f"wb_{part}", [P, 2 * DB, D])
            u_b = tmp(f"u_b_{part}", [P, U, D])
            act_b = tmp(f"act_b_{part}", [P, 2, D])
            v_b = tmp(f"v_b_{part}", [P, 4, D])
            squares = tmp(f"squares_{part}", [P, D])
            sq_sum = tmp(f"sq_sum_{part}", [P, 2])
            inv_norm = tmp(f"inv_norm_{part}", [P, 2])
            stats = tmp(f"stats_{part}", [P, U, 6])
            mean_var = tmp(f"mean_var_{part}", [P, U, 2])
            root = tmp(f"root_{part}", [P, U])
            length = tmp(f"length_{part}", [P, 2])
            rstd = tmp(f"rstd_{part}", [P, U])
            shift = tmp(f"shift_{part}", [P, U])
            ob = tmp(f"ob_{part}", [P, 4, 2, ROW])
            return (rows, gather_at, select, edge_coef, running, xb, diag, rb, extra, total_b, mixed, turned_b,
                    wb, u_b, act_b, v_b, squares, sq_sum, inv_norm, stats, mean_var, root, length, rstd, shift,
                    ob)

        layer_mem = ExitStack()
        (rows, gather_at, select, edge_coef, running, xb, diag, rb, extra, total_b, mixed, turned_b, wb, u_b,
         act_b, v_b, squares, sq_sum, inv_norm, stats, mean_var, root, length, rstd, shift, ob) = layer_buffers(layer_mem, "a")

        GCN, SAGE, SAGE_LAST, PAIR, CONV = range(5)

        def edge_sums(kind, width, table, srcs, los, ws, gathered):
            def gather(pool, i, k, base, staged, summed):
                c = U * i + k
                if k % 4 == 0:
                    for j in range(k, k + 4):
                        slot_freed(pool, gathered[j], i, base[j])
                    if isinstance(i, int) and i and not isinstance(base[k], int):
                        take_waits(pool, 3 + k // 4)
                    pool.tensor_copy(gather_at[:, k:k + 4], srcs[:, bass.ds(c, 4)]).then_inc(staged, 1)
                    pool.wait_ge(staged, 2 * i + k // 4 + 1)
                    need(pool, summed, c - U + 4)
                    take_waits(pool)
                pool.indirect_dma_start(rows[:, k, 0:width], None, table,
                                        bass.IndirectOffsetOnAxis(ap=gather_at[:, k:k + 1], axis=0)).then_inc(
                    gathered[k], 16)

            def coefficient(act, i, k, base, coef_made, selected):
                c = U * i + k
                act.wait_ge(gathered[k], 16 * (i + 1 + base[k]))
                need(act, selected, c - U + 1)
                act.activation(edge_coef[:, k:k + 1], ws[:, bass.ds(c, 1)], ACT.Copy,
                               scale=rows[:, k, D:D + 1]).then_inc(coef_made, 1)

            def choose(dve, i, k, base, coef_made, selected, summed):
                c, r = U * i + k, k
                need(dve, summed, c - U + 1)
                if kind == GCN:
                    dve.wait_ge(coef_made, c + 1)
                    coef = edge_coef[:, k:k + 1]
                elif kind == PAIR:
                    dve.wait_ge(gathered[k], 16 * (i + 1 + base[k]))
                    coef = rows[:, k, D:D + 1]
                elif kind == CONV:
                    coef = ws[:, bass.ds(c, 1)]
                else:
                    coef = None
                lo = los[:, bass.ds(c, 1)]
                if coef is None:
                    dve.tensor_scalar(select[:, r], iota_f[:, 0:P], lo, None, ALU.is_equal).then_inc(selected, 1)
                else:
                    dve.tensor_scalar(select[:, r], iota_f[:, 0:P], lo, coef, ALU.is_equal, ALU.mult).then_inc(
                        selected, 1)

            def multiply(pe, i, k, base, selected, sum_read, summed, add_own=None):
                c = U * i + k
                pe.wait_ge(selected, c + 1)
                pe.wait_ge(gathered[k], 16 * (i + 1 + base[k]))
                need(pe, sum_read, c - 1)
                if kind == PAIR:
                    last = pe.matmul(sum_ps[k % 2], select[:, k], rows[:, k, 0:D], start=True, stop=True)
                else:
                    for b in range(DB):
                        at = slice(b * P, b * P + P)
                        last = pe.matmul(sum_ps[k % 2][:, at], rows[:, k, at], select[:, k], start=True,
                                         stop=add_own is None)
                        if add_own is not None:
                            last = add_own(sum_ps[k % 2][:, at], at)
                last.then_inc(summed, 1)
            return gather, coefficient, choose, multiply

        def overflow_sweep(name, kind, width, table, weights, plan):
            gather, coefficient, choose, multiply = edge_sums(kind, width, table, *plan.extra, plan.gathered)

            def counted(eng, step):
                final = eng.value_load(plan.x_last[0:1, 0:1], min_val=2, max_val=XB // U - 1)
                base = [(final + 1) * plan.sweeps if plan.sweeps else 0] * U
                for i in range(2):
                    for k in range(U):
                        step(i, k, base)
                with eng.Fori(2, final + 1) as i:
                    for k in range(U):
                        step(i, k, base)
                return final

            with phase(nc, *[f"{name}_{n}" for n in ("staged", "coef_made", "selected", "summed", "sum_done", "w_in",
                                                     "carry_set")],
                       *[f"{name}_sums_out{k}" for k in range(U)]) as (
                    block, (staged, coef_made, selected, summed, sum_done, w_in, carry_set, *sums_out)):

                @block.gpsimd
                def _(pool):
                    counted(pool, lambda i, k, base: gather(pool, i, k, base, staged, summed))

                @block.scalar
                def _(act):
                    if kind == GCN:
                        counted(act, lambda i, k, base: coefficient(act, i, k, base, coef_made, selected))

                @block.tensor
                def _(pe):
                    final = counted(pe, lambda i, k, base: multiply(pe, i, k, base, selected, sum_done, summed))
                    for k in range(U):
                        pe.wait_ge(sums_out[k], 16 * final + 16)

                @block.vector
                def _(dve):
                    dve.memset(running[:, U - 1], 0.0).then_inc(carry_set, 1)
                    dve.wait_ge(carry_set, 1)

                    def add(i, k):
                        if isinstance(i, int) and i < 0:
                            return
                        c = U * i + k
                        dve.wait_ge(summed, c + 1)
                        need(dve, sum_done, c)
                        need(dve, sums_out[k], 16 * i)
                        dve.scalar_tensor_tensor(running[:, k], running[:, (k - 1) % U], plan.carry[:, bass.ds(c, 1)],
                                                 sum_ps[k % 2], ALU.mult, ALU.add).then_inc(sum_done, 1)

                    def step(i, k, base):
                        choose(dve, i, k, base, coef_made, selected, summed)
                        add(*tile_at(i, k - 1))
                    final = counted(dve, step)
                    add(final, U - 1)

                @block.sync
                def _(sp):
                    for j, w in enumerate(weights):
                        sp.dma_start(wb[:, DB * j:DB * j + DB], w.rearrange("(b p) d -> p b d", p=P)).then_inc(w_in, 16)

                    def step(i, k, base):
                        c = U * i + k
                        sp.wait_ge(sum_done, c + 1)
                        sp.dma_start(overflow_sums[bass.ds(c, 1)].rearrange("a p d -> p (a d)"), running[:, k]).then_inc(
                            sums_out[k], 16)
                    counted(sp, step)
                    need(sp, w_in, 16 * len(weights))
                    sp.wait_ge(sum_done, 1)

        def tile_sweep(name, kind, width, table, weights, bias, residual, target, plan, placing=None):
            gather, coefficient, choose, multiply = edge_sums(kind, width, table, *plan.main, gathered_m)
            base = list(before_now)
            banks, FREE = (product_ps, 3) if placing is None else (product_ps[2:] * 2, 1)
            PLACING = [f"{name}_place_{n}" for n in ("onehot", "rank_ready", "rank_read", "places", "fields_staged",
                                                     "ones_used")] if placing else []
            pairs = table.rearrange("(g k p) d -> g p k d", k=2, p=P)
            final = target is None
            out_width = D if final else target.shape[1]
            out_pairs = (out[0:WHOLE_PAIRS * 2 * P] if final else target).rearrange("(g k p) d -> g p k d", k=2, p=P)
            TURN = {GCN: None, SAGE: 1, SAGE_LAST: 1, PAIR: 2, CONV: None}[kind]
            COPY = TURN and TURN + 1
            PRODUCT = TURN + 2 if TURN else 2
            CHOOSE = 2 if kind in (GCN, PAIR) else 3
            FINISH = PRODUCT + 1
            MEASURE = FINISH + (2 if kind == PAIR else 1)
            ROOT, SCALE = MEASURE + 1, MEASURE + 2
            LAG = FINISH + 1 if kind == SAGE else SCALE + 1
            CHAIN = {GCN: 2, SAGE_LAST: 3, PAIR: 4, CONV: 3, SAGE: 0}[kind]
            BLOCKS = 2 * DB if kind == PAIR else DB
            normed = kind != SAGE

            def real(i, k):
                return not isinstance(i, int) or 0 <= U * i + k < T

            with phase(nc, *[f"{name}_{n}" for n in ("staged", "coef_made", "selected", "summed", "part_done",
                                                     "total_done", "scaled", "turned", "copied", "product", "product_read",
                                                     "chained", "measured", "rooted", "inverted", "ready", "activated", "leaked",
                                                     "rows_done", "x_scaled")],
                       *[f"{name}_x_in{k}" for k in range(4)],
                       *[f"{name}_extra_in{k}" for k in range(U)], *[f"{name}_rows_out{k}" for k in range(4)],
                       *PLACING) as (
                    block, (staged, coef_made, selected, summed, part_done, total_done, scaled, turned, copied, product,
                            product_read, chained, measured, rooted, inverted, ready, activated, leaked,
                            rows_done, x_scaled, *dmas)):
                x_in, extra_in, rows_out, sems = dmas[0:4], dmas[4:U + 4], dmas[U + 4:U + 8], dmas[U + 8:]
                placer = Placer(*placing[:3], sems, placing[3]) if placing else None
                sum_read = part_done if kind == PAIR else total_done
                X_LOADS = 2 if residual is not None else 1

                @block.gpsimd
                def _(pool):
                    if not placer:
                        sweep(pool, T, 0, lambda i, k: gather(pool, i, k, base, staged, summed), 0)
                        return

                    def step(i, k):
                        if real(i, k):
                            gather(pool, i, k, base, staged, summed)
                        a = tile_at(i, k - U)
                        if real(*a):
                            placer.scatter(pool, *a)
                    sweep(pool, T, 0, step, U, peeled=2)
                    placer.end(pool)

                @block.sync
                def _(sp):
                    def step(i, k):
                        t, g, r = U * i + k, 4 * i + k // 2, k // 2
                        if k % 2 == 0:
                            if kind == SAGE:
                                need(sp, turned, t - 6)
                            else:
                                need(sp, chained, CHAIN * (t - 7) + {GCN: 1, SAGE_LAST: 2, PAIR: 3, CONV: 2}[kind])
                            sp.dma_start(xb[:, r, :, 0:width], pairs[g]).then_inc(x_in[r], 16)
                            if residual is not None:
                                sp.dma_start(rb[:, r], residual.rearrange("(g k p) d -> g p k d", k=2, p=P)[g]).then_inc(
                                    x_in[r], 16)
                        at = sp.value_load(plan.sums_at[0:1, bass.ds(t, 1)], min_val=0, max_val=XB)
                        need(sp, total_done, t - U + 1)
                        sp.dma_start(extra[:, k], overflow_sums[bass.ds(at, 1)].rearrange("a p d -> p (a d)")).then_inc(
                            extra_in[k], 16)
                    sweep(sp, T, 0, step, 0)

                @block.tensor
                def _(pe):
                    def turn(i, k):
                        if not real(i, k):
                            return
                        t, r = U * i + k, k % 4
                        if kind == PAIR:
                            pe.wait_ge(total_done, t + 1)
                            left = [mixed[:, r, 0], mixed[:, r, 1]]
                        else:
                            pe.wait_ge(x_in[k // 2], 16 * X_LOADS * (i + 1))
                            left = [xb[:, k // 2, k % 2]]
                        need(pe, copied, t - 1)
                        for j, a in enumerate(left):
                            for b in range(DB):
                                n = DB * j + b
                                last = pe.transpose(turned_ps[k % 2][:, n * P:n * P + P], a[:, b * P:b * P + P], ident[:])
                        last.then_inc(turned, 1)

                    def multiply_w(i, k):
                        if not real(i, k):
                            return
                        t, r = U * i + k, k % 4
                        if TURN:
                            pe.wait_ge(copied, t + 1)
                        pe.wait_ge(total_done, t + 1)
                        if kind == PAIR:
                            need(pe, product_read, t - 3)
                        elif kind == SAGE:
                            need(pe, ready, t - FREE)
                        else:
                            need(pe, chained, CHAIN * (t - 4) + 1)
                        sums = [mixed[:, r, 0, b * P:b * P + P] for b in range(DB)]
                        if kind == GCN:
                            parts = [list(zip(sums, [w_gcn[:, b] for b in range(DB)]))]
                        elif kind == CONV:
                            parts = [list(zip(sums, [wb[:, b] for b in range(DB)]))]
                        elif kind == PAIR:
                            parts = [[(turned_b[:, r, n], wb[:, n]) for n in range(2 * DB)]]
                        else:
                            parts = [[(turned_b[:, r, b], wb[:, b]) for b in range(DB)],
                                     [(sums[b], wb[:, DB + b]) for b in range(DB)]]
                        for j, part in enumerate(parts):
                            for n, (left, w) in enumerate(part):
                                last = pe.matmul(banks[r][:, j * D:j * D + D], left, w, start=n == 0,
                                                 stop=n == len(part) - 1)
                        last.then_inc(product, 1)

                    def step(i, k):
                        if real(i, k):
                            own = None
                            if kind == GCN:
                                pe.wait_ge(x_in[k // 2], 16 * X_LOADS * (i + 1))
                                pe.wait_ge(scaled, U * i + k + 1)

                                def own(to, at):
                                    return pe.matmul(to, xb[:, k // 2, k % 2, at], diag[:, k % 4], start=False, stop=True)
                            multiply(pe, i, k, base, selected, sum_read, summed, own)
                        if TURN:
                            turn(*tile_at(i, k - TURN))
                        multiply_w(*tile_at(i, k - PRODUCT))
                        if placer and real(i, k):
                            placer.count(pe, i, k)
                    sweep(pe, T, 0, lambda i, k: step(*tile_at(i, k)), PRODUCT, peeled=2)

                @block.vector
                def _(dve):
                    def add(i, k):
                        if not real(i, k):
                            return
                        t, r = U * i + k, k % 4
                        dve.wait_ge(summed, t + 1)
                        dve.wait_ge(extra_in[k], 16 * (i + 1))
                        if kind == PAIR:
                            need(dve, turned, t - 3)
                            dve.tensor_tensor(total_b[:, r], sum_ps[k % 2], extra[:, k], ALU.add).then_inc(part_done, 1)
                        else:
                            need(dve, product, t - 3)
                            dve.tensor_tensor(mixed[:, r, 0], sum_ps[k % 2], extra[:, k], ALU.add).then_inc(total_done, 1)

                    def make_factors(i, k):
                        if not real(i, k) or kind != PAIR:
                            return
                        t, r = U * i + k, k % 4
                        dve.wait_ge(part_done, t + 1)
                        dve.wait_ge(x_in[k // 2], 16 * X_LOADS * (i + 1))
                        dve.tensor_tensor(mixed[:, r, 1], total_b[:, r], xb[:, k // 2, k % 2, 0:D], ALU.mult)
                        dve.wait_ge(x_scaled, t + 1)
                        dve.tensor_tensor(mixed[:, r, 0], total_b[:, r], rb[:, k // 2, k % 2],
                                          ALU.add).then_inc(total_done, 1)

                    def take_product(i, k):
                        if not real(i, k):
                            return
                        t, r = U * i + k, k % 4
                        dve.wait_ge(product, t + 1)
                        if kind == GCN:
                            need(dve, rows_done, t - U + 1)
                            dve.scalar_tensor_tensor(u_b[:, k], banks[r][:, 0:D], dinv[:, bass.ds(t, 1)],
                                                     xb[:, k // 2, k % 2, 0:D], ALU.mult, ALU.add).then_inc(chained, 1)
                        elif kind in (SAGE, SAGE_LAST):
                            if kind == SAGE:
                                need(dve, ready, t - 3)
                            dve.scalar_tensor_tensor(v_b[:, r], banks[r][:, D:2 * D], inv_deg[:, bass.ds(t, 1)], bias,
                                                     ALU.mult, ALU.add).then_inc(part_done, 1)
                        elif kind == PAIR:
                            dve.scalar_tensor_tensor(v_b[:, r], banks[r][:, 0:D], has_in[:, bass.ds(t, 1)], bias, ALU.mult,
                                                     ALU.add).then_inc(product_read, 1)
                        else:
                            dve.tensor_tensor(v_b[:, r], banks[r][:, 0:D], bias, ALU.add).then_inc(chained, 1)

                    def add_rows_product(i, k):
                        if not real(i, k) or kind not in (SAGE, SAGE_LAST):
                            return
                        t = U * i + k
                        dve.wait_ge(part_done, t + 1)
                        if kind == SAGE:
                            need(dve, rows_done, t - U + 1)
                            dve.tensor_tensor(u_b[:, k], banks[k % 4][:, 0:D], v_b[:, k % 4], ALU.add).then_inc(ready, 1)
                        else:
                            dve.tensor_tensor(act_b[:, k % 2], banks[k % 4][:, 0:D], v_b[:, k % 4], ALU.add).then_inc(chained, 1)

                    def add_residual(i, k):
                        if not real(i, k) or kind not in (SAGE_LAST, CONV):
                            return
                        t = U * i + k
                        row = act_b[:, k % 2] if kind == SAGE_LAST else v_b[:, k % 4]
                        other = rb[:, k // 2, k % 2] if residual is not None else xb[:, k // 2, k % 2, 0:D]
                        dve.wait_ge(chained, CHAIN * t + 1)
                        need(dve, rows_done, t - U + 1)
                        dve.tensor_tensor(u_b[:, k], row, other, ALU.add).then_inc(chained, 1)

                    def leak(i, k):
                        if not real(i, k) or kind != PAIR:
                            return
                        t, q, r = U * i + k, k % 2, k % 4
                        dve.wait_ge(product_read, t + 1)
                        need(dve, activated, t - 1)
                        dve.scalar_tensor_tensor(act_b[:, q], v_b[:, r], 0.01, v_b[:, r], ALU.mult,
                                                 ALU.max).then_inc(leaked, 1)

                    def bound_norm(i, k):
                        if not real(i, k) or kind != PAIR:
                            return
                        q = k % 2
                        dve.wait_ge(activated, U * i + k + 1)
                        dve.tensor_scalar(inv_norm[:, q:q + 1], length[:, q:q + 1], 1e-12, None,
                                          ALU.max).then_inc(chained, 1)

                    def invert_norm(i, k):
                        if not real(i, k) or kind != PAIR:
                            return
                        q = k % 2
                        dve.wait_ge(chained, CHAIN * (U * i + k) + 1)
                        dve.reciprocal(inv_norm[:, q:q + 1], inv_norm[:, q:q + 1]).then_inc(chained, 1)

                    def unit_rows(i, k):
                        if not real(i, k) or kind != PAIR:
                            return
                        t, q = U * i + k, k % 2
                        dve.wait_ge(chained, CHAIN * t + 2)
                        need(dve, rows_done, t - U + 1)
                        dve.scalar_tensor_tensor(u_b[:, k], act_b[:, q], inv_norm[:, q:q + 1],
                                                 xb[:, k // 2, k % 2, 0:D], ALU.mult, ALU.add).then_inc(chained, 1)

                    def measure(i, k):
                        if not real(i, k) or not normed:
                            return
                        dve.wait_ge(chained, CHAIN * (U * i + k + 1) - 1)
                        dve.bn_stats(stats[:, k], u_b[:, k]).then_inc(chained, 1)

                    def invert_root(i, k):
                        if not real(i, k) or not normed:
                            return
                        dve.wait_ge(rooted, U * i + k + 1)
                        dve.reciprocal(rstd[:, k:k + 1], root[:, k:k + 1]).then_inc(inverted, 1)

                    def make_shift(i, k):
                        if not real(i, k) or not normed:
                            return
                        dve.wait_ge(inverted, U * i + k + 1)
                        dve.scalar_tensor_tensor(shift[:, k:k + 1], mean_var[:, k, 0:1], -1.0, rstd[:, k:k + 1], ALU.mult,
                                                 ALU.mult).then_inc(ready, 1)

                    def step(i, k):
                        take_product(*tile_at(i, k - FINISH))
                        bound_norm(*tile_at(i, k - FINISH - 1))
                        add(*tile_at(i, k - 1))
                        invert_root(*tile_at(i, k - SCALE))
                        invert_norm(*tile_at(i, k - FINISH - 1))
                        leak(*tile_at(i, k - FINISH))
                        add_rows_product(*tile_at(i, k - FINISH))
                        if kind == CONV:
                            add_residual(*tile_at(i, k - FINISH))
                        make_shift(*tile_at(i, k - SCALE))
                        unit_rows(*tile_at(i, k - FINISH - 1))
                        make_factors(*tile_at(i, k - 1))
                        m, mk = tile_at(i, k - MEASURE)
                        measures = normed and real(m, mk)
                        if measures:
                            dve.wait_ge(chained, CHAIN * (U * m + mk + 1))
                        b = tile_at(i, k + CHOOSE)
                        if real(*b):
                            choose(dve, *b, base, coef_made, selected, summed)
                        if measures:
                            dve.bn_aggr(mean_var[:, mk], stats[:, mk]).then_inc(measured, 1)
                        if kind == SAGE_LAST:
                            add_residual(*tile_at(i, k - FINISH))
                        measure(*tile_at(i, k - MEASURE + 1))
                        if placer:
                            placer.set_onehot(dve, *tile_at(i, k + 1))
                            if real(i, k):
                                placer.read_rank(dve, i, k)
                    sweep(dve, T, 3, step, LAG, peeled=2)

                @block.scalar
                def _(act):
                    def store(i, k):
                        g, r = 4 * i + k // 2, k // 2
                        act.wait_ge(rows_done, U * i + k + 1)
                        if final and isinstance(g, int) and g == WHOLE_PAIRS:
                            act.dma_start(out[N - REST:N, :], ob[0:REST, r, 0, 0:D]).then_inc(rows_out[r], 16)
                        else:
                            act.dma_start(out_pairs[g], ob[:, r, :, 0:out_width]).then_inc(rows_out[r], 16)

                    def finish(i, k):
                        if not real(i, k):
                            return
                        t, q, r, s = U * i + k, k % 2, k // 2, k
                        need(act, rows_out[r], 16 * i)
                        act.wait_ge(ready, t + 1)
                        if out_width == ROW:
                            act.copy(ob[:, r, q, D:ROW], root_out[:, bass.ds(t, 1)])
                        if normed:
                            act.activation(ob[:, r, q, 0:D], u_b[:, s], ACT.Identity,
                                           bias=shift[:, s:s + 1], scale=rstd[:, s:s + 1]).then_inc(rows_done, 1)
                        else:
                            act.activation(ob[:, r, q, 0:D], u_b[:, s], ACT.Relu).then_inc(rows_done, 1)
                        if k % 2:
                            store(i, k)

                    def step(i, k):
                        finish(*tile_at(i, k - LAG))
                        a = tile_at(i, k - ROOT)
                        if normed and real(*a):
                            t, s = U * a[0] + a[1], a[1]
                            act.wait_ge(measured, t + 1)
                            act.activation(root[:, s:s + 1], mean_var[:, s, 1:2], ACT.Sqrt,
                                           bias=eps_col[:, 0:1]).then_inc(rooted, 1)
                        a = tile_at(i, k - (COPY or 0))
                        if TURN and real(*a):
                            t, r = U * a[0] + a[1], a[1] % 4
                            act.wait_ge(turned, t + 1)
                            need(act, product, t - 3)
                            act.copy(turned_b[:, r, 0:BLOCKS].rearrange("p b n -> p (b n)"),
                                     turned_ps[a[1] % 2][:, 0:BLOCKS * P]).then_inc(copied, 1)
                        if kind == PAIR and real(i, k):
                            t = U * i + k
                            act.wait_ge(x_in[k // 2], 16 * X_LOADS * (i + 1))
                            need(act, total_done, t - U + 1)
                            act.activation(rb[:, k // 2, k % 2], xb[:, k // 2, k % 2, 0:D], ACT.Copy,
                                           scale=root_deg[:, bass.ds(t, 1)]).then_inc(x_scaled, 1)
                        a = tile_at(i, k + 1)
                        if kind == GCN and real(*a):
                            t, r = U * a[0] + a[1], a[1] % 4
                            need(act, summed, t - 3)
                            act.activation(diag[:, r], ident[:], ACT.Copy,
                                           scale=dinv[:, bass.ds(t, 1)]).then_inc(scaled, 1)
                        b = tile_at(i, k + 3)
                        if kind == GCN and real(*b):
                            coefficient(act, *b, base, coef_made, selected)
                        a = tile_at(i, k - FINISH)
                        if kind == PAIR and real(*a):
                            t, q = U * a[0] + a[1], a[1] % 2
                            act.wait_ge(leaked, t + 1)
                            act.activation(squares[:], act_b[:, q], ACT.Square,
                                           accum_out=sq_sum[:, q:q + 1]).then_inc(scaled, 1)
                            act.wait_ge(scaled, t + 1)
                            act.activation(length[:, q:q + 1], sq_sum[:, q:q + 1], ACT.Sqrt,
                                           bias=tiny_col[:, 0:1]).then_inc(activated, 1)
                    sweep(act, T, 4, step, LAG, peeled=3)
                    for r in range(4):
                        act.wait_ge(rows_out[r], 16 * (T // U))

        def layer(name, kind, table, weights, bias, residual, target, plan=by_dst, placing=None):
            width = table.shape[1]
            overflow_sweep("x_" + name, kind, width, table, weights, plan)
            if placing:
                place_tiles(by_src, out_sb, by_dst.upto[:, 0:T], by_dst.first[:, 0:T].bitcast(I32), by_dst.base[:, 0:T])
            tile_sweep(name, kind, width, table, weights, bias, residual, target, plan, placing)
            before_now[:] = [n + T // U for n in before_now]
            plan.sweeps += 1

        place_bufs = [layer_mem.enter_context(nc.sbuf_tensor(f"late_{name}", shape, dt)) for name, shape, dt in (
            ("onehots", [P, 4, T], BF16), ("junk", [P, T], F32), ("rank8", [P, U], F32), ("row_at", [P, U], I32),
            ("staged", [P, U, 4], F32))]
        layer("gcn", GCN, table0, [], None, None, table1)
        layer("sage0", SAGE, table1, [W_self[0], W_neigh[0]], bsage_row[:, 0], None, table1a,
              placing=(by_src, src_hi, place_bufs, scattered))
        layer("sage1", SAGE, table1a, [W_self[1], W_neigh[1]], bsage_row[:, 1], None, table1b)
        layer("sage2", SAGE_LAST, table1b, [W_self[2], W_neigh[2]], bsage_row[:, 2], table1, table2)
        layer("pair", PAIR, table2, [W_one, W_two], bpair_row[:], None, table3)
        layer_mem.close()
        late.close()
        list_chunks(by_src, list(before_now))
        layer_mem = ExitStack()
        (rows, gather_at, select, edge_coef, running, xb, diag, rb, extra, total_b, mixed, turned_b, wb, u_b,
         act_b, v_b, squares, sq_sum, inv_norm, stats, mean_var, root, length, rstd, shift, ob) = layer_buffers(layer_mem, "b")
        layer("conv", CONV, table3, [W_conv], bconv_row[:], None, None, by_src)
        layer_mem.close()


_INS = ["x", "src", "dst", "edge_weight", "L0_gnn_p", "L0_gnn_W_ih", "L0_gnn_W_hh", "L0_gnn_b_ih", "L0_gnn_b_hh",
        "L0_gnn_W0", "L1_gnn_W_self", "L1_gnn_W_neigh", "L1_gnn_bias", "L2_gnn_W1", "L2_gnn_W2", "L2_gnn_b",
        "L3_gnn_weight", "L3_gnn_bias"]


def kernel(**inputs):
    import numpy as _np
    import concourse.bacc as _bacc
    from concourse import mybir as _mybir
    from concourse.bass_utils import run_bass_kernel_spmd as _run

    nc = _bacc.Bacc("TRN2", target_bir_lowering=False, num_devices=1)
    arrays, args = {}, []
    for name in _INS:
        a = _np.ascontiguousarray(inputs[name])
        arrays[f"in_{name}_dram"] = a
        args.append(nc.dram_tensor(f"in_{name}_dram", a.shape, _mybir.dt.from_np(a.dtype), kind="ExternalInput").ap())
    shape = tuple(inputs["x"].shape)
    result = nc.dram_tensor("out_0_dram", shape, _mybir.dt.float32, kind="ExternalOutput").ap()
    graph_stack(nc, *args, result)
    r = _run(nc, [arrays], core_ids=[0])
    return r.results[0]["out_0_dram"]
```
